# Optimizing a Trainium2 kernel written in Bass

```python
import numpy as np
import jax
import jax.numpy as jnp

def _softmax(x, axis=-1):
    return jax.nn.softmax(x, axis=axis)

def _gelu(x):
    return jax.nn.gelu(x, approximate=True)

def _silu(x):
    return jax.nn.silu(x)

def _sigmoid(x):
    return jax.nn.sigmoid(x)

def _layernorm(x, axis=-1, eps=1e-05):
    m = jnp.mean(x, axis=axis, keepdims=True)
    v = jnp.var(x, axis=axis, keepdims=True)
    return (x - m) / jnp.sqrt(v + eps)

def _scatter_add(tgt, idx, src, axis=0):
    return tgt.at[idx].add(src)

def _segment_sum(src, seg, n):
    return jax.ops.segment_sum(src, seg, n)
kernel_name = 'mk_gnn_resnorm_d4_gnn_r32_41969f'

def setup_inputs(seed: int=0):
    np.random.seed(seed)
    _w = jnp.asarray

    def _rec_inputs():
        import jax
        import jax.numpy as jnp
        _gk = jax.random.key(seed)
        x = -1.686e-05 + 1 * jax.random.normal(jax.random.fold_in(_gk, 1), (3125, 160), jnp.float32)
        src = jax.random.randint(jax.random.fold_in(_gk, 2), (100000,), 0, 3125, jnp.int32)
        dst = jax.random.randint(jax.random.fold_in(_gk, 3), (100000,), 0, 3125, jnp.int32)
        _o = jnp.argsort(dst, stable=True)
        src = src[_o]
        dst = dst[_o]
        edge_attr_16 = -0.000191324 + 0.999809 * jax.random.normal(jax.random.fold_in(_gk, 12), (100000, 16), jnp.float32)
        edge_attr_4 = 0.0007022 + 0.999661 * jax.random.normal(jax.random.fold_in(_gk, 13), (100000, 4), jnp.float32)
        node_vec1 = -0.00915711 + 0.999674 * jax.random.normal(jax.random.fold_in(_gk, 15), (3125, 1), jnp.float32)
        return (x, src, dst, edge_attr_16, edge_attr_4, node_vec1)
    x, src, dst, edge_attr_16, edge_attr_4, node_vec1 = _rec_inputs()

    def _L0_gnn_setup():
        import jax, jax.numpy as jnp
        import numpy as np
        MUL0, MUL1 = (64, 32)
        INV_SQRT3 = 1.0 / np.sqrt(3.0)

        def _split(x):
            return (x[:, :MUL0], x[:, MUL0:].reshape(x.shape[0], MUL1, 3))

        def _merge(o0, o1):
            return jnp.concatenate([o0, o1.reshape(o1.shape[0], -1)], axis=-1)

        def _tp(x0, x1, y0, y1, w000, w011, w101, w110):
            fan0 = x0.shape[1] * y0.shape[1] + x1.shape[1] * y1.shape[1]
            fan1 = x0.shape[1] * y1.shape[1] + x1.shape[1] * y0.shape[1]
            out0 = (jnp.einsum('eu,ev,uvw->ew', x0, y0, w000) + INV_SQRT3 * jnp.einsum('euk,evk,uvw->ew', x1, y1, w110)) / np.sqrt(fan0)
            out1 = (jnp.einsum('eu,evk,uvw->ewk', x0, y1, w011) + jnp.einsum('euk,ev,uvw->ewk', x1, y0, w101)) / np.sqrt(fan1)
            return (out0, out1)

        def _lin(x0, x1, w0, w1):
            return (x0 @ w0 / np.sqrt(x0.shape[1]), jnp.einsum('euk,uv->evk', x1, w1) / np.sqrt(x1.shape[1]))
        key = jax.random.key(seed)
        ks = jax.random.split(key, 20)
        N, E = (50000, 15625)
        inp = {'node_features': jax.random.normal(ks[0], (N, MUL0 + 3 * MUL1), dtype=jnp.float32), 'edge_index': jax.random.randint(ks[1], (2, E), 0, N, dtype=jnp.int64), 'edge_attr_tensor': jax.random.normal(ks[2], (E, 4), dtype=jnp.float32), 'node_attr_scalar_raw': jax.random.normal(ks[3], (N, 1), dtype=jnp.float32), 'wm000': jax.random.normal(ks[4], (MUL0, 1, MUL0), dtype=jnp.float32), 'wm011': jax.random.normal(ks[5], (MUL0, 1, MUL1), dtype=jnp.float32), 'wm101': jax.random.normal(ks[6], (MUL1, 1, MUL1), dtype=jnp.float32), 'wm110': jax.random.normal(ks[7], (MUL1, 1, MUL0), dtype=jnp.float32), 'lm0': jax.random.normal(ks[8], (MUL0, MUL0), dtype=jnp.float32), 'lm1': jax.random.normal(ks[9], (MUL1, MUL1), dtype=jnp.float32), 'wu000': jax.random.normal(ks[10], (MUL0, MUL0, MUL0), dtype=jnp.float32), 'wu011': jax.random.normal(ks[11], (MUL0, MUL1, MUL1), dtype=jnp.float32), 'wu101': jax.random.normal(ks[12], (MUL1, MUL0, MUL1), dtype=jnp.float32), 'wu110': jax.random.normal(ks[13], (MUL1, MUL1, MUL0), dtype=jnp.float32), 'lu0': jax.random.normal(ks[14], (MUL0, MUL0), dtype=jnp.float32), 'lu1': jax.random.normal(ks[15], (MUL1, MUL1), dtype=jnp.float32)}
        return inp
    _L0_gnn_all = _L0_gnn_setup()
    _L0_gnn_in = {k: v for k, v in _L0_gnn_all.items() if k in ('wm000', 'wm011', 'wm101', 'wm110', 'lm0', 'lm1', 'wu000', 'wu011', 'wu101', 'wu110', 'lu0', 'lu1')}
    del _L0_gnn_all

    def _L1_gnn_setup():
        import jax, jax.numpy as jnp
        import numpy as np
        N = 625
        E = 10000
        MUL0 = 64
        MUL1 = 32
        FC_IN = 16
        FC_H = 64
        WNUM = 192
        key = jax.random.key(seed)
        ks = jax.random.split(key, 16)
        return {'x': jax.random.normal(ks[0], (N, MUL0 + 3 * MUL1), jnp.float32), 'node_attr': jnp.ones((N, 1), jnp.float32), 'edge_scalars': jax.random.normal(ks[1], (E, FC_IN), jnp.float32), 'edge_attr_sh': jax.random.normal(ks[2], (E, 4), jnp.float32), 'edge_src': jax.random.randint(ks[3], (E,), 0, N), 'edge_dst': jax.random.randint(ks[4], (E,), 0, N), 'Wfc1': jax.random.normal(ks[5], (FC_IN, FC_H), jnp.float32), 'Wfc2': jax.random.normal(ks[6], (FC_H, WNUM), jnp.float32), 'Wsc0': jax.random.normal(ks[7], (MUL0, MUL0), jnp.float32), 'Wsc1': jax.random.normal(ks[8], (MUL1, MUL1), jnp.float32), 'Wl1_0': jax.random.normal(ks[9], (MUL0, MUL0), jnp.float32), 'Wl1_1': jax.random.normal(ks[10], (MUL1, MUL1), jnp.float32), 'Wl2_s': jax.random.normal(ks[11], (MUL0 + MUL1, MUL0), jnp.float32), 'Wl2_v': jax.random.normal(ks[12], (MUL0 + MUL1, MUL1), jnp.float32), 'Wa': 0.1 * jax.random.normal(ks[13], (MUL0 + MUL1, 1), jnp.float32)}
    _L1_gnn_all = _L1_gnn_setup()
    _L1_gnn_in = {k: v for k, v in _L1_gnn_all.items() if k in ('Wfc1', 'Wfc2', 'Wsc0', 'Wsc1', 'Wl1_0', 'Wl1_1', 'Wl2_s', 'Wl2_v', 'Wa')}
    del _L1_gnn_all

    def _L2_gnn_setup():
        import jax, jax.numpy as jnp
        import numpy as np
        N = 625
        E = 20000
        INV_SQRT3 = 0.5773502691896258
        INV8 = 0.125
        INV_SQRT32 = 0.17677669529663687
        INV64 = 0.015625
        INV32 = 0.03125
        INV_SQRT2048 = 0.022097086912079608
        key = jax.random.key(seed)
        ks = jax.random.split(key, 16)
        f32 = jnp.float32
        return {'node_features': jax.random.normal(ks[0], (N, 160), f32), 'edge_index': jax.random.randint(ks[1], (2, E), 0, N), 'edge_attr_tensor': jax.random.normal(ks[2], (E, 4), f32), 'node_attr_scalar_raw': jax.random.normal(ks[3], (N, 1), f32), 'Wm_ss': jax.random.normal(ks[4], (64, 64), f32), 'Wm_vv': jax.random.normal(ks[5], (32, 64), f32), 'Wm_sv': jax.random.normal(ks[6], (64, 32), f32), 'Wm_vs': jax.random.normal(ks[7], (32, 32), f32), 'Lm_s': jax.random.normal(ks[8], (64, 64), f32), 'Lm_v': jax.random.normal(ks[9], (32, 32), f32), 'Wu_ss': jax.random.normal(ks[10], (64, 64, 64), f32), 'Wu_vv': jax.random.normal(ks[11], (32, 32, 64), f32), 'Wu_sv': jax.random.normal(ks[12], (64, 32, 32), f32), 'Wu_vs': jax.random.normal(ks[13], (32, 64, 32), f32), 'Lu_s': jax.random.normal(ks[14], (64, 64), f32), 'Lu_v': jax.random.normal(ks[15], (32, 32), f32)}
    _L2_gnn_all = _L2_gnn_setup()
    _L2_gnn_in = {k: v for k, v in _L2_gnn_all.items() if k in ('Wm_ss', 'Wm_vv', 'Wm_sv', 'Wm_vs', 'Lm_s', 'Lm_v', 'Wu_ss', 'Wu_vv', 'Wu_sv', 'Wu_vs', 'Lu_s', 'Lu_v')}
    del _L2_gnn_all

    def _L3_gnn_setup():
        import jax, jax.numpy as jnp
        import numpy as np
        N, E = (50000, 25000)
        MUL0, MUL1 = (64, 32)
        D = MUL0 + 3 * MUL1
        INV3 = float(1.0 / np.sqrt(3.0))
        INV6 = float(1.0 / np.sqrt(6.0))
        C0 = float(1.0 / np.sqrt(MUL0 + MUL1))
        C1 = float(np.sqrt(3.0 / (MUL0 + 2 * MUL1)))
        LIN_S = float(1.0 / np.sqrt(MUL0))
        LIN_V = float(1.0 / np.sqrt(MUL1))
        key = jax.random.key(seed)
        ks = jax.random.split(key, 10)
        x = jax.random.normal(ks[0], (N, D), dtype=jnp.float32)
        sh = jax.random.normal(ks[1], (E, 4), dtype=jnp.float32)
        edge_index = jax.random.randint(ks[2], (2, E), 0, N, dtype=jnp.int64)
        W1 = jax.random.normal(ks[3], (MUL0, MUL0), dtype=jnp.float32)
        W2 = jax.random.normal(ks[4], (MUL1, MUL0), dtype=jnp.float32)
        W3 = jax.random.normal(ks[5], (MUL0, MUL1), dtype=jnp.float32)
        W4 = jax.random.normal(ks[6], (MUL1, MUL1), dtype=jnp.float32)
        W5 = jax.random.normal(ks[7], (MUL1, MUL1), dtype=jnp.float32)
        Ws = jax.random.normal(ks[8], (MUL0, MUL0), dtype=jnp.float32)
        Wv = jax.random.normal(ks[9], (MUL1, MUL1), dtype=jnp.float32)
        return {'x': x, 'sh': sh, 'W1': W1, 'W2': W2, 'W3': W3, 'W4': W4, 'W5': W5, 'Ws': Ws, 'Wv': Wv, 'edge_index': edge_index}
    _L3_gnn_all = _L3_gnn_setup()
    _L3_gnn_in = {k: v for k, v in _L3_gnn_all.items() if k in ('W1', 'W2', 'W3', 'W4', 'W5', 'Ws', 'Wv')}
    del _L3_gnn_all
    return {'x': x, 'src': src, 'dst': dst, 'edge_attr_16': edge_attr_16, 'edge_attr_4': edge_attr_4, 'node_vec1': node_vec1, 'L0_gnn_wm000': _L0_gnn_in['wm000'], 'L0_gnn_wm011': _L0_gnn_in['wm011'], 'L0_gnn_wm101': _L0_gnn_in['wm101'], 'L0_gnn_wm110': _L0_gnn_in['wm110'], 'L0_gnn_lm0': _L0_gnn_in['lm0'], 'L0_gnn_lm1': _L0_gnn_in['lm1'], 'L0_gnn_wu000': _L0_gnn_in['wu000'], 'L0_gnn_wu011': _L0_gnn_in['wu011'], 'L0_gnn_wu101': _L0_gnn_in['wu101'], 'L0_gnn_wu110': _L0_gnn_in['wu110'], 'L0_gnn_lu0': _L0_gnn_in['lu0'], 'L0_gnn_lu1': _L0_gnn_in['lu1'], 'L1_gnn_Wfc1': _L1_gnn_in['Wfc1'], 'L1_gnn_Wfc2': _L1_gnn_in['Wfc2'], 'L1_gnn_Wsc0': _L1_gnn_in['Wsc0'], 'L1_gnn_Wsc1': _L1_gnn_in['Wsc1'], 'L1_gnn_Wl1_0': _L1_gnn_in['Wl1_0'], 'L1_gnn_Wl1_1': _L1_gnn_in['Wl1_1'], 'L1_gnn_Wl2_s': _L1_gnn_in['Wl2_s'], 'L1_gnn_Wl2_v': _L1_gnn_in['Wl2_v'], 'L1_gnn_Wa': _L1_gnn_in['Wa'], 'L2_gnn_Wm_ss': _L2_gnn_in['Wm_ss'], 'L2_gnn_Wm_vv': _L2_gnn_in['Wm_vv'], 'L2_gnn_Wm_sv': _L2_gnn_in['Wm_sv'], 'L2_gnn_Wm_vs': _L2_gnn_in['Wm_vs'], 'L2_gnn_Lm_s': _L2_gnn_in['Lm_s'], 'L2_gnn_Lm_v': _L2_gnn_in['Lm_v'], 'L2_gnn_Wu_ss': _L2_gnn_in['Wu_ss'], 'L2_gnn_Wu_vv': _L2_gnn_in['Wu_vv'], 'L2_gnn_Wu_sv': _L2_gnn_in['Wu_sv'], 'L2_gnn_Wu_vs': _L2_gnn_in['Wu_vs'], 'L2_gnn_Lu_s': _L2_gnn_in['Lu_s'], 'L2_gnn_Lu_v': _L2_gnn_in['Lu_v'], 'L3_gnn_W1': _L3_gnn_in['W1'], 'L3_gnn_W2': _L3_gnn_in['W2'], 'L3_gnn_W3': _L3_gnn_in['W3'], 'L3_gnn_W4': _L3_gnn_in['W4'], 'L3_gnn_W5': _L3_gnn_in['W5'], 'L3_gnn_Ws': _L3_gnn_in['Ws'], 'L3_gnn_Wv': _L3_gnn_in['Wv']}

def reference(x, src, dst, edge_attr_16, edge_attr_4, node_vec1, L0_gnn_wm000, L0_gnn_wm011, L0_gnn_wm101, L0_gnn_wm110, L0_gnn_lm0, L0_gnn_lm1, L0_gnn_wu000, L0_gnn_wu011, L0_gnn_wu101, L0_gnn_wu110, L0_gnn_lu0, L0_gnn_lu1, L1_gnn_Wfc1, L1_gnn_Wfc2, L1_gnn_Wsc0, L1_gnn_Wsc1, L1_gnn_Wl1_0, L1_gnn_Wl1_1, L1_gnn_Wl2_s, L1_gnn_Wl2_v, L1_gnn_Wa, L2_gnn_Wm_ss, L2_gnn_Wm_vv, L2_gnn_Wm_sv, L2_gnn_Wm_vs, L2_gnn_Lm_s, L2_gnn_Lm_v, L2_gnn_Wu_ss, L2_gnn_Wu_vv, L2_gnn_Wu_sv, L2_gnn_Wu_vs, L2_gnn_Lu_s, L2_gnn_Lu_v, L3_gnn_W1, L3_gnn_W2, L3_gnn_W3, L3_gnn_W4, L3_gnn_W5, L3_gnn_Ws, L3_gnn_Wv):
    import jax
    import jax.numpy as jnp

    def _L0_gnn_ref(node_features, edge_index, edge_attr_tensor, node_attr_scalar_raw, wm000, wm011, wm101, wm110, lm0, lm1, wu000, wu011, wu101, wu110, lu0, lu1):
        import jax, jax.numpy as jnp
        import numpy as np
        MUL0, MUL1 = (64, 32)
        INV_SQRT3 = 1.0 / np.sqrt(3.0)

        def _split(x):
            return (x[:, :MUL0], x[:, MUL0:].reshape(x.shape[0], MUL1, 3))

        def _merge(o0, o1):
            return jnp.concatenate([o0, o1.reshape(o1.shape[0], -1)], axis=-1)

        def _tp(x0, x1, y0, y1, w000, w011, w101, w110):
            fan0 = x0.shape[1] * y0.shape[1] + x1.shape[1] * y1.shape[1]
            fan1 = x0.shape[1] * y1.shape[1] + x1.shape[1] * y0.shape[1]
            out0 = (jnp.einsum('eu,ev,uvw->ew', x0, y0, w000) + INV_SQRT3 * jnp.einsum('euk,evk,uvw->ew', x1, y1, w110)) / np.sqrt(fan0)
            out1 = (jnp.einsum('eu,evk,uvw->ewk', x0, y1, w011) + jnp.einsum('euk,ev,uvw->ewk', x1, y0, w101)) / np.sqrt(fan1)
            return (out0, out1)

        def _lin(x0, x1, w0, w1):
            return (x0 @ w0 / np.sqrt(x0.shape[1]), jnp.einsum('euk,uv->evk', x1, w1) / np.sqrt(x1.shape[1]))
        N = node_features.shape[0]
        row, col = (edge_index[0], edge_index[1])
        r_vec = edge_attr_tensor[:, :3]
        dist = edge_attr_tensor[:, 3:4]
        e0 = dist
        e1 = r_vec[:, None, :]
        xj0, xj1 = _split(node_features[col])
        m0, m1 = _tp(xj0, xj1, e0, e1, wm000, wm011, wm101, wm110)
        d0, d1 = _lin(xj0, xj1, lm0, lm1)
        msgs = _merge(m0 + d0, m1 + d1)
        agg = jax.ops.segment_sum(msgs, row, num_segments=N)
        a0, a1 = _split(agg)
        x0, x1 = _split(node_features)
        u0, u1 = _tp(x0, x1, a0, a1, wu000, wu011, wu101, wu110)
        ud0, ud1 = _lin(x0, x1, lu0, lu1)
        return node_features + _merge(u0 + ud0, u1 + ud1)

    def _L1_gnn_ref(x, node_attr, edge_scalars, edge_attr_sh, edge_src, edge_dst, Wfc1, Wfc2, Wsc0, Wsc1, Wl1_0, Wl1_1, Wl2_s, Wl2_v, Wa):
        import jax, jax.numpy as jnp
        import numpy as np
        N = 625
        E = 10000
        MUL0 = 64
        MUL1 = 32
        FC_IN = 16
        FC_H = 64
        WNUM = 192
        n = x.shape[0]
        x0 = x[:, :MUL0]
        x1 = x[:, MUL0:].reshape(n, MUL1, 3)
        a = node_attr
        h = jax.nn.silu(edge_scalars @ (Wfc1 / jnp.sqrt(jnp.float32(FC_IN))))
        w = h @ (Wfc2 / jnp.sqrt(jnp.float32(FC_H)))
        w0 = w[:, :64]
        w1 = w[:, 64:128]
        w2 = w[:, 128:160]
        w3 = w[:, 160:192]
        inv8 = 1.0 / jnp.sqrt(jnp.float32(MUL0))
        inv32 = 1.0 / jnp.sqrt(jnp.float32(MUL1))
        sc = jnp.concatenate([x0 @ Wsc0 * a * inv8, (jnp.einsum('num,uv->nvm', x1, Wsc1) * a[..., None] * inv32).reshape(n, 3 * MUL1)], axis=1)
        f0 = x0 @ Wl1_0 * a * inv8
        f1 = jnp.einsum('num,uv->nvm', x1, Wl1_1) * a[..., None] * inv32
        e0 = f0[edge_src]
        e1 = f1[edge_src]
        sh0 = edge_attr_sh[:, :1]
        sh1 = edge_attr_sh[:, 1:4]
        mid0 = w0 * e0 * sh0
        mid1 = w3 * jnp.einsum('eum,em->eu', e1, sh1) / jnp.sqrt(3.0)
        mid2 = w1[:, :, None] * e0[:, :, None] * sh1[:, None, :]
        mid3 = w2[:, :, None] * e1 * sh0[:, :, None]
        cnt = jnp.clip(jax.ops.segment_sum(jnp.ones(edge_dst.shape, x.dtype), edge_dst, num_segments=n), 1.0)

        def smean(v):
            s = jax.ops.segment_sum(v, edge_dst, num_segments=n)
            return s / cnt.reshape((n,) + (1,) * (v.ndim - 1))
        n0, n1 = (smean(mid0), smean(mid1))
        n2, n3 = (smean(mid2), smean(mid3))
        scal = jnp.concatenate([n0, n1], axis=1)
        vec = jnp.concatenate([n2, n3], axis=1)
        inv96 = 1.0 / jnp.sqrt(jnp.float32(MUL0 + MUL1))
        alpha = scal @ Wa * a * inv96
        out_s = scal @ Wl2_s * a * inv96
        out_v = jnp.einsum('num,uv->nvm', vec, Wl2_v) * a[..., None] * inv96
        conv = jnp.concatenate([out_s, out_v.reshape(n, 3 * MUL1)], axis=1)
        return sc + alpha * conv

    def _L2_gnn_ref(node_features, edge_index, edge_attr_tensor, node_attr_scalar_raw, Wm_ss, Wm_vv, Wm_sv, Wm_vs, Lm_s, Lm_v, Wu_ss, Wu_vv, Wu_sv, Wu_vs, Lu_s, Lu_v):
        import jax, jax.numpy as jnp
        import numpy as np
        N = 625
        E = 20000
        INV_SQRT3 = 0.5773502691896258
        INV8 = 0.125
        INV_SQRT32 = 0.17677669529663687
        INV64 = 0.015625
        INV32 = 0.03125
        INV_SQRT2048 = 0.022097086912079608
        n = node_features.shape[0]
        e = edge_attr_tensor.shape[0]
        row, col = (edge_index[0], edge_index[1])
        r_vec = edge_attr_tensor[:, :3]
        dist = edge_attr_tensor[:, 3:4]
        xj = node_features[col]
        s = xj[:, :64]
        v = xj[:, 64:].reshape(e, 32, 3)
        m0 = s @ Wm_ss * dist * INV8 + jnp.einsum('eui,ei->eu', v, r_vec) @ Wm_vv * (INV_SQRT3 * INV_SQRT32)
        m1 = (s @ Wm_sv)[:, :, None] * r_vec[:, None, :] * INV8 + jnp.einsum('eui,uw->ewi', v, Wm_vs) * dist[:, :, None] * INV_SQRT32
        m0 = m0 + s @ Lm_s * INV8
        m1 = m1 + jnp.einsum('eui,uw->ewi', v, Lm_v) * INV_SQRT32
        msg = jnp.concatenate([m0, m1.reshape(e, 96)], axis=-1)
        agg = jax.ops.segment_sum(msg, row, num_segments=n)
        a0 = agg[:, :64]
        a1 = agg[:, 64:].reshape(n, 32, 3)
        xs = node_features[:, :64]
        xv = node_features[:, 64:].reshape(n, 32, 3)
        u0 = jnp.einsum('nu,nv,uvw->nw', xs, a0, Wu_ss) * INV64 + jnp.einsum('nui,nvi,uvw->nw', xv, a1, Wu_vv) * (INV_SQRT3 * INV32)
        u1 = jnp.einsum('nu,nvi,uvw->nwi', xs, a1, Wu_sv) * INV_SQRT2048 + jnp.einsum('nui,nv,uvw->nwi', xv, a0, Wu_vs) * INV_SQRT2048
        u0 = u0 + xs @ Lu_s * INV8
        u1 = u1 + jnp.einsum('nui,uw->nwi', xv, Lu_v) * INV_SQRT32
        upd = jnp.concatenate([u0, u1.reshape(n, 96)], axis=-1)
        return node_features + upd

    def _L3_gnn_ref(x, sh, W1, W2, W3, W4, W5, Ws, Wv, edge_index):
        import jax, jax.numpy as jnp
        import numpy as np
        N, E = (50000, 25000)
        MUL0, MUL1 = (64, 32)
        D = MUL0 + 3 * MUL1
        INV3 = float(1.0 / np.sqrt(3.0))
        INV6 = float(1.0 / np.sqrt(6.0))
        C0 = float(1.0 / np.sqrt(MUL0 + MUL1))
        C1 = float(np.sqrt(3.0 / (MUL0 + 2 * MUL1)))
        LIN_S = float(1.0 / np.sqrt(MUL0))
        LIN_V = float(1.0 / np.sqrt(MUL1))
        n = x.shape[0]
        src, dst = (edge_index[0], edge_index[1])
        s = x[:, :MUL0]
        v = x[:, MUL0:].reshape(n, MUL1, 3)
        ss, vv = (s[src], v[src])
        e0 = sh[:, 0:1]
        e1 = sh[:, 1:4]
        dot = jnp.einsum('eui,ei->eu', vv, e1)
        out0 = C0 * (ss * e0 @ W1 + dot * INV3 @ W2)
        p3 = (ss @ W3)[:, :, None] * e1[:, None, :] * INV3
        p4 = jnp.einsum('eui,uw->ewi', vv * e0[:, :, None], W4) * INV3
        p5 = jnp.einsum('eui,uw->ewi', jnp.cross(vv, e1[:, None, :]), W5) * INV6
        out1 = C1 * (p3 + p4 + p5)
        m = jnp.concatenate([out0, out1.reshape(-1, 3 * MUL1)], axis=1)
        m_agg = jax.ops.segment_sum(m, dst, num_segments=n)
        hs = m_agg[:, :MUL0] @ Ws * LIN_S
        hv = jnp.einsum('nui,uw->nwi', m_agg[:, MUL0:].reshape(n, MUL1, 3), Wv) * LIN_V
        h = jnp.concatenate([hs, hv.reshape(n, 3 * MUL1)], axis=1)
        return x + jax.nn.relu(h)
    edge_index = jnp.stack([src, dst])
    x = _layernorm(x + _L0_gnn_ref(x, edge_index, edge_attr_4, node_vec1, L0_gnn_wm000, L0_gnn_wm011, L0_gnn_wm101, L0_gnn_wm110, L0_gnn_lm0, L0_gnn_lm1, L0_gnn_wu000, L0_gnn_wu011, L0_gnn_wu101, L0_gnn_wu110, L0_gnn_lu0, L0_gnn_lu1), axis=-1)
    x = _layernorm(x + _L1_gnn_ref(x, node_vec1, edge_attr_16, edge_attr_4, src, dst, L1_gnn_Wfc1, L1_gnn_Wfc2, L1_gnn_Wsc0, L1_gnn_Wsc1, L1_gnn_Wl1_0, L1_gnn_Wl1_1, L1_gnn_Wl2_s, L1_gnn_Wl2_v, L1_gnn_Wa), axis=-1)
    x = _layernorm(x + _L2_gnn_ref(x, edge_index, edge_attr_4, node_vec1, L2_gnn_Wm_ss, L2_gnn_Wm_vv, L2_gnn_Wm_sv, L2_gnn_Wm_vs, L2_gnn_Lm_s, L2_gnn_Lm_v, L2_gnn_Wu_ss, L2_gnn_Wu_vv, L2_gnn_Wu_sv, L2_gnn_Wu_vs, L2_gnn_Lu_s, L2_gnn_Lu_v), axis=-1)
    x = _layernorm(x + _L3_gnn_ref(x, edge_attr_4, L3_gnn_W1, L3_gnn_W2, L3_gnn_W3, L3_gnn_W4, L3_gnn_W5, L3_gnn_Ws, L3_gnn_Wv, edge_index), axis=-1)
    return x

_drawn_inputs = setup_inputs


def setup_inputs(seed=0):
    import zlib

    import numpy as np

    out = dict(_drawn_inputs(seed))
    spreads = {}
    factors = {'edge_attr_16': 8.0,
     'L1_gnn_Wfc1': 8.0,
     'L1_gnn_Wfc2': 8.0,
     'L1_gnn_Wl1_0': 8.0,
     'L1_gnn_Wl1_1': 8.0,
     'L1_gnn_Wl2_s': 8.0,
     'L1_gnn_Wl2_v': 8.0,
     'L1_gnn_Wa': 8.0}
    for name, (base, spread) in spreads.items():
        noise = np.random.default_rng([zlib.crc32(name.encode()), seed]).standard_normal(out[name].shape)
        drawn = base * np.exp(spread * noise) if base else spread * noise
        out[name] = jnp.asarray(drawn.astype(out[name].dtype))
    for name, factor in factors.items():
        out[name] = (out[name] * factor).astype(out[name].dtype)
    return out
```

```python
import math
from contextlib import ExitStack, contextmanager

import concourse.bass as bass
from concourse import mybir

F32 = mybir.dt.float32
I32 = mybir.dt.int32
ALU = mybir.AluOpType
ACT = mybir.ActivationFunctionType
AXX = mybir.AxisListType.X

P = 128
N, D = 3125, 160
S0, V0, VD = 64, 32, 96
E = 100000
NT = (N + P - 1) // P
NPAD = NT * P
TAIL = N - (NT - 1) * P
EP, EC = 125, 800
JB = 4
GE = JB * P
NI = (E + NT * (GE - 1)) // GE
SL = 4
NJ = NI // SL
assert NI % SL == 0 and EP * EC == E
NIP = 2 * P
TW = 192
UP, VP = 8, 16
EPS = 1e-5
GC = 8
K3 = 1.0 / math.sqrt(3.0)


class Count:

    def __init__(self, eng, name, start):
        self.eng, self.reg = eng, eng.alloc_register(name)
        eng.reg_mov(self.reg, start)

    def up(self, by):
        self.eng.reg_add(self.reg, self.reg, by)


class Net:

    def __init__(self, nc, ctx):
        self.nc, self.ctx = nc, ctx

    def sb(self, name, shape, dt=F32, ctx=None):
        return (ctx or self.ctx).enter_context(self.nc.sbuf_tensor(name, shape, dt))

    def ps(self, name, shape, ctx):
        return ctx.enter_context(self.nc.psum_tensor(name, shape, F32))

    def sem(self, name, ctx):
        self.stage_sems.append(self.nc.alloc_semaphore(name=name))
        return self.stage_sems[-1]

    @contextmanager
    def stage(self):
        self.stage_sems = []
        with ExitStack() as c:
            yield c
        self.nc.clear_and_free_semaphores(self.stage_sems)
        self.nc.all_engine_barrier()

    def dram(self, name, shape, dt=F32):
        return self.nc.dram_tensor(name, shape, dt, kind="Internal").ap()


def constants(net, ins, layers):
    nc = net.nc
    net.ident = net.sb("ident", [P, P])
    net.ramp = net.sb("ramp", [P, P])
    net.part = net.sb("part", [P, 1])
    net.ones = net.sb("ones", [P, P])
    net.below = net.sb("below", [P, P])
    net.step_no = net.sb("step_no", [P, 2])
    net.eps = net.sb("eps", [P, 1])
    net.sel_u = net.sb("sel_u", [P, P // UP, P])
    net.sel_v = net.sb("sel_v", [P, P // VP, P])
    with net.stage() as c:
        ramp_i = net.sb("ramp_i", [P, P], I32, c)
        part_i = net.sb("part_i", [P, 1], I32, c)
        step_i = net.sb("step_i", [P, 2], I32, c)
        uv_i = net.sb("uv_i", [P, 2, P], I32, c)
        uv_f = net.sb("uv_f", [P, 2, P], F32, c)
        uv_split = net.sem("uv_split", c)
        pad = net.sb("pad", [P, GE // P * 22], F32, c)
        ramps_made = net.sem("ramps_made", c)
        floats_made = net.sem("floats_made", c)
        pad_zero = net.sem("pad_zero", c)
        pad_keys = net.sem("pad_keys", c)
        weights_loaded = net.sem("weights_loaded", c)
        pads_stored = net.sem("pads_stored", c)
        block = c.enter_context(nc.Block())
        n_loads = []

        @block.gpsimd
        def _(pool):
            pool.iota(ramp_i[:, :], pattern=[[1, P]], base=0, channel_multiplier=0)
            pool.iota(part_i[:, :], pattern=[[0, 1]], base=0, channel_multiplier=1)
            pool.iota(step_i[:, :], pattern=[[P, 2]], base=0, channel_multiplier=1).then_inc(ramps_made, 1)

        @block.vector
        def _(dve):
            dve.memset(net.ones[:, :], 1.0)
            dve.memset(net.eps[:, :], EPS)
            dve.memset(pad[:, :], 0.0).then_inc(pad_zero, 1)
            dve.wait_ge(pad_zero, 1)
            dve.memset(pad[:, 0:GE // P * 22].rearrange("p (j w) -> p j w", w=22)[:, :, 0:1], -1.0).then_inc(pad_keys, 1)
            dve.wait_ge(ramps_made, 1)
            dve.tensor_copy(net.ramp[:, :], ramp_i[:, :])
            dve.tensor_copy(net.part[:, :], part_i[:, :])
            dve.tensor_copy(net.step_no[:, :], step_i[:, :])
            dve.tensor_scalar(uv_i[:, 0, :], ramp_i[:, :], int(math.log2(VP)), None, ALU.logical_shift_right)
            dve.tensor_scalar(uv_i[:, 1, :], ramp_i[:, :], VP - 1, None, ALU.bitwise_and).then_inc(uv_split, 1)
            dve.wait_ge(uv_split, 1)
            dve.tensor_copy(uv_f[:, :, :], uv_i[:, :, :]).then_inc(floats_made, 1)
            dve.wait_ge(floats_made, 1)
            dve.tensor_scalar(net.ident[:, :], net.ramp[:, :], net.part[:, 0:1], None, ALU.is_equal)
            dve.tensor_scalar(net.below[:, :], net.ramp[:, :], net.part[:, 0:1], None, ALU.is_gt)
            for b in range(P // UP):
                dve.tensor_scalar(net.sel_u[:, b, :], uv_f[:, 0, :], float(UP * b), net.part[:, 0:1],
                                  ALU.add, ALU.is_equal)
            for b in range(P // VP):
                dve.tensor_scalar(net.sel_v[:, b, :], uv_f[:, 1, :], float(VP * b), net.part[:, 0:1],
                                  ALU.add, ALU.is_equal)

        @block.sync
        def _(sp):
            n = 0
            for lay in layers:
                for name, (tile, w) in lay["chunks"].items():
                    u, v, wd = w.shape
                    for ui in range(UP):
                        src = w.rearrange("(a b) (c d) w -> b d a c w", b=UP, d=VP)[ui]
                        for a in range(u // UP):
                            sp.dma_start(tile[ui * VP:(ui + 1) * VP, a, :, :], src[:, a]).then_inc(weights_loaded, 16)
                            n += 1
                for dst, src in lay["plain"]:
                    sp.dma_start(dst, src).then_inc(weights_loaded, 16)
                    n += 1
            sp.wait_ge(pad_keys, 1)
            pv = pad[:, :].rearrange("p (j w) -> p j w", w=22)
            for rec, w in net.pads:
                sp.dma_start(rec[E:E + GE, :].rearrange("(p j) w -> p j w", j=GE // P),
                             pv[:, :, 0:w]).then_inc(pads_stored, 16)
            sp.wait_ge(weights_loaded, 16 * n)
            sp.wait_ge(pads_stored, 16 * len(net.pads))

    with ExitStack() as c:
        block = c.enter_context(nc.Block())

        @block.scalar
        def _(act):
            for lay in layers:
                for ap, factor in lay["scales"]:
                    act.mul(ap, ap, factor)


def sort_edges(net, tag, key, other, attrs, rec, sched):
    nc = net.nc
    W = rec.shape[1]
    erow, trow, tbase = sched
    with net.stage() as c:
        key_i = net.sb(f"{tag}_key_i", [EP, EC], I32, c)
        oth_i = net.sb(f"{tag}_oth_i", [EP, EC], I32, c)
        bin_i = net.sb(f"{tag}_bin_i", [EP, EC], I32, c)
        bin_f = net.sb(f"{tag}_bin_f", [EP, EC], F32, c)
        mask = net.sb(f"{tag}_mask", [EP, 2, EC], I32, c)
        rank = net.sb(f"{tag}_rank", [EP, 2, EC], F32, c)
        pos = net.sb(f"{tag}_pos", [EP, EC], F32, c)
        recs = net.sb(f"{tag}_recs", [EP, EC, W], F32, c)
        PC = 100
        piece = net.sb(f"{tag}_piece", [EP, 2, PC * 16], F32, c)
        count = net.sb(f"{tag}_count", [EP, NT], F32, c)
        first = net.sb(f"{tag}_first", [EP, NT], F32, c)
        total = net.sb(f"{tag}_total", [P, NT], F32, c)
        t_end = net.sb(f"{tag}_t_end", [P, NT], F32, c)
        steps_f = net.sb(f"{tag}_steps_f", [P, NT], F32, c)
        steps_i = net.sb(f"{tag}_steps_i", [P, 2, NT], I32, c)
        s_first = net.sb(f"{tag}_s_first", [P, NT + 1], F32, c)
        e_first = net.sb(f"{tag}_e_first", [P, NT + 1], F32, c)
        shift = net.sb(f"{tag}_shift", [P, NT + 1], F32, c)
        dshift = net.sb(f"{tag}_dshift", [P, NT + 1], F32, c)
        junk = net.sb(f"{tag}_junk", [P, 2, 2, NT + 1], F32, c)
        sums = net.sb(f"{tag}_sums", [P, 2, 2], F32, c)
        step_e = net.sb(f"{tag}_step_e", [P, 2], F32, c)
        step_ei = net.sb(f"{tag}_step_ei", [P, 2], I32, c)
        step_t = net.sb(f"{tag}_step_t", [P, 2], F32, c)
        step_ti = net.sb(f"{tag}_step_ti", [P, 2], I32, c)
        step_b = net.sb(f"{tag}_step_b", [P, 2], F32, c)
        stage_rec = net.sb(f"{tag}_stage_rec", [EP, 2, GC, W], F32, c)
        stage_pos = net.sb(f"{tag}_stage_pos", [EP, 2, GC], I32, c)
        counts_ps = net.ps(f"{tag}_counts_ps", [P, 2, 512], c)
        dram_e = net.dram(f"{tag}_dram_e", [NIP], I32)
        dram_t = net.dram(f"{tag}_dram_t", [NIP], I32)
        dram_b = net.dram(f"{tag}_dram_b", [NIP], F32)

        keys_loaded = net.sem(f"{tag}_keys_loaded", c)
        others_loaded = net.sem(f"{tag}_others_loaded", c)
        piece_loaded = [net.sem(f"{tag}_piece_loaded{s}", c) for s in range(2)]
        piece_used = net.sem(f"{tag}_piece_used", c)
        dve_step = net.sem(f"{tag}_dve_step", c)
        summed = net.sem(f"{tag}_summed", c)
        sched_made = net.sem(f"{tag}_sched_made", c)
        sched_stored = net.sem(f"{tag}_sched_stored", c)
        sched_loaded = net.sem(f"{tag}_sched_loaded", c)
        placed = net.sem(f"{tag}_placed", c)
        recs_made = net.sem(f"{tag}_recs_made", c)
        staged = net.sem(f"{tag}_staged", c)
        scattered = [net.sem(f"{tag}_scattered{s}", c) for s in range(2)]
        block = c.enter_context(nc.Block())

        pieces = []
        w0 = 2
        for a in attrs:
            k = a.shape[1]
            av = a.rearrange("(p c) k -> p (c k)", p=EP)
            for q in range(EC // PC):
                pieces.append((av[:, q * PC * k:(q + 1) * PC * k], k, w0, q))
            w0 += k

        @block.sync
        def _(sp):
            sp.dma_start(key_i[:, :], key.rearrange("(p c) -> p c", p=EP)).then_inc(keys_loaded, 16)
            sp.dma_start(oth_i[:, :], other.rearrange("(p c) -> p c", p=EP)).then_inc(others_loaded, 16)
            for n, (src, k, _, _) in enumerate(pieces):
                if n >= 2:
                    sp.wait_ge(piece_used, n - 1)
                sp.dma_start(piece[:, n % 2, 0:PC * k], src).then_inc(piece_loaded[n % 2], 16)
            sp.wait_ge(sched_made, 1)
            for d, t in ((dram_e, step_ei), (dram_t, step_ti), (dram_b, step_b)):
                sp.dma_start(d.rearrange("(h p o) -> p h o", p=P, o=1),
                             t[:, :].rearrange("p (h o) -> p h o", o=1)).then_inc(sched_stored, 16)
            sp.wait_ge(sched_stored, 48)
            sp.dma_start(erow[:, :], dram_e.rearrange("(o n) -> o n", o=1)).then_inc(sched_loaded, 16)
            sp.dma_start(trow[:, :], dram_t.rearrange("(o n) -> o n", o=1)).then_inc(sched_loaded, 16)
            sp.dma_start(tbase[:, :], dram_b.rearrange("(o n) -> o n", o=1).broadcast_to([P, NIP])).then_inc(sched_loaded, 16)
            sp.wait_ge(sched_loaded, 48)

        @block.scalar
        def _(act):
            act.wait_ge(keys_loaded, 16)
            act.activation(recs[:, :, 0], key_i[:, :], ACT.Copy)
            act.wait_ge(others_loaded, 16)
            act.activation(recs[:, :, 1], oth_i[:, :], ACT.Copy)
            for n, (_, k, w, q) in enumerate(pieces):
                act.wait_ge(piece_loaded[n % 2], 16 * (n // 2 + 1))
                last = act.activation(recs[:, q * PC:(q + 1) * PC, w:w + k],
                                      piece[:, n % 2, 0:PC * k].rearrange("p (c k) -> p c k", k=k), ACT.Copy)
                last.then_inc(piece_used, 1)
            act.wait_ge(piece_used, len(pieces))
            act.wait_ge(placed, 1)

            def stage(j, s, free):
                if free is not None:
                    act.wait_ge(scattered[s], free)
                col = (2 * j + s) * GC
                act.activation(stage_pos[:, s, :], pos[:, bass.ds(col, GC)], ACT.Copy)
                act.activation(stage_rec[:, s, :, :], recs[:, bass.ds(col, GC), :], ACT.Copy).then_inc(staged, 1)

            for s in range(2):
                stage(0, s, None)
            with act.Fori(1, EC // GC // 2) as j:
                for s in range(2):
                    stage(j, s, 16 * GC * j)

        @block.tensor
        def _(pe):
            pe.wait_ge(dve_step, 2 + NT)
            pe.matmul(counts_ps[0:EP, 0, 0:NT], net.below[0:EP, 0:EP], count[:, :], start=True, stop=True)
            pe.matmul(counts_ps[:, 1, 0:NT], net.ones[0:EP, :], count[:, :], start=True, stop=True).then_inc(summed, 1)

        @block.gpsimd
        def _(pool):
            turn = Count(pool, f"{tag}_turn", 0)

            def scatter(j, s):
                turn.up(1)
                pool.wait_ge(staged, 1)
                pool.wait_ge(staged, turn.reg)
                for q in range(GC):
                    pool.indirect_dma_start(rec, bass.IndirectOffsetOnAxis(ap=stage_pos[:, s, q:q + 1], axis=0),
                                            stage_rec[:, s, q, :], None).then_inc(scattered[s], 16)

            with pool.Fori(0, EC // GC // 2) as j:
                for s in range(2):
                    scatter(j, s)
            for s in range(2):
                pool.wait_ge(scattered[s], 16 * EC // 2)

        @block.vector
        def _(dve):
            done = [0]

            def step(ins):
                done[0] += 1
                ins.then_inc(dve_step, 1)
                dve.wait_ge(dve_step, done[0])

            dve.wait_ge(keys_loaded, 16)
            step(dve.tensor_scalar(bin_i[:, :], key_i[:, :], int(math.log2(P)), None, ALU.logical_shift_right))
            step(dve.tensor_copy(bin_f[:, :], bin_i[:, :]))
            for k in range(NT):
                step(dve.tensor_scalar(rank[:, k % 2, :], bin_f[:, :], float(k), 0.0, ALU.is_equal, ALU.add,
                                       accum_out=count[:, k:k + 1]))
            dve.wait_ge(summed, 1)
            step(dve.tensor_copy(total[:, :], counts_ps[:, 1, 0:NT]))
            step(dve.tensor_tensor_scan(t_end[:, :], total[:, :], total[:, :], 0.0, ALU.add, ALU.max))
            dve.memset(e_first[:, 0:1], 0.0)
            step(dve.tensor_copy(e_first[:, 1:NT + 1], t_end[:, :]))
            step(dve.tensor_tensor(first[:, :], counts_ps[0:EP, 0, 0:NT], e_first[0:EP, 0:NT], ALU.add))
            step(dve.tensor_scalar(steps_i[:, 0, :], total[:, :], float(GE - 1), None, ALU.add))
            step(dve.tensor_scalar(steps_i[:, 1, :], steps_i[:, 0, :], int(math.log2(GE)), None, ALU.logical_shift_right))
            step(dve.tensor_copy(steps_f[:, :], steps_i[:, 1, :]))
            dve.memset(s_first[:, 0:1], 0.0)
            step(dve.tensor_tensor_scan(s_first[:, 1:NT + 1], steps_f[:, :], steps_f[:, :], 0.0, ALU.add, ALU.max))
            step(dve.scalar_tensor_tensor(shift[:, :], s_first[:, :], -float(GE), e_first[:, :], ALU.mult, ALU.add))
            dve.memset(dshift[:, 0:1], 0.0)
            step(dve.tensor_tensor(dshift[:, 1:NT + 1], shift[:, 1:NT + 1], shift[:, 0:NT], ALU.subtract))
            for h in range(2):
                dve.tensor_scalar(junk[:, h, 0, :], s_first[:, :], net.step_no[:, h:h + 1], -1.0, ALU.is_le, ALU.add,
                                  accum_out=step_t[:, h:h + 1])
                step(dve.scalar_tensor_tensor(junk[:, h, 1, :], s_first[:, :], net.step_no[:, h:h + 1], dshift[:, :],
                                              ALU.is_le, ALU.mult, accum_out=sums[:, 0, h:h + 1]))
            step(dve.scalar_tensor_tensor(step_e[:, :], net.step_no[:, :], float(GE), sums[:, 0, :], ALU.mult, ALU.add))
            dve.tensor_scalar(step_ei[:, :], step_e[:, :], float(E), None, ALU.min)
            dve.tensor_copy(step_ti[:, :], step_t[:, :])
            dve.tensor_scalar(step_b[:, :], step_t[:, :], float(P), None, ALU.mult).then_inc(sched_made, 1)
            for k in range(NT):
                s = k % 2
                step(dve.tensor_scalar(mask[:, s, :], bin_f[:, :], float(k), None, ALU.is_equal))
                step(dve.tensor_tensor_scan(rank[:, s, :], mask[:, s, :], mask[:, s, :], first[:, k:k + 1],
                                            ALU.add, ALU.max))
                step(dve.copy_predicated(pos[:, :], mask[:, s, :], rank[:, s, :]))
            dve.tensor_scalar(pos[:, :], pos[:, :], -1.0, None, ALU.add).then_inc(placed, 1)



def edge_loop(net, tag, kind, rec, sched, table, acc, C):
    nc = net.nc
    W = rec.shape[1]
    erow, trow, tbase = sched
    MC = {"plain": C - D, "conv": C, "cross": C}[kind]
    dist, vec = {"plain": (5, 2), "conv": (2, 3), "cross": (2, 3)}[kind]
    with net.stage() as c:
        recs = net.sb(f"{tag}_recs", [P, SL, JB, W], F32, c)
        far = net.sb(f"{tag}_far", [P, SL, JB], I32, c)
        rows = net.sb(f"{tag}_rows", [P, SL, JB, TW], F32, c)
        rel = net.sb(f"{tag}_rel", [P, 2, JB], F32, c)
        hot = net.sb(f"{tag}_hot", [P, 2, JB, P], F32, c)
        msg = net.sb(f"{tag}_msg", [P, 2, JB, MC], F32, c)
        prod = net.sb(f"{tag}_prod", [P, 3, JB, VD], F32, c)
        agg_ps = [net.ps(f"{tag}_agg_ps{s}", [P, 512], c) for s in range(2)]
        if kind == "conv":
            scaled = net.sb(f"{tag}_scaled", [P, 2, JB, D], F32, c)
            w0f = net.sb(f"{tag}_w0f", [P, JB, S0], F32, c)
            dot = net.sb(f"{tag}_dot", [P, JB, V0], F32, c)
            attT = net.sb(f"{tag}_attT", [16, 2, GE], F32, c)
            hidT = net.sb(f"{tag}_hidT", [S0, 2, GE], F32, c)
            attT_ps = net.ps(f"{tag}_attT_ps", [16, GE], c)
            hid_ps = net.ps(f"{tag}_hid_ps", [S0, GE], c)
            w_ps = [net.ps(f"{tag}_w_ps{s}", [P, 2, 2, 256], c) for s in range(2)]

        acc_zero = net.sem(f"{tag}_acc_zero", c)
        rec_loaded = [net.sem(f"{tag}_rec_loaded{s}", c) for s in range(SL)]
        far_ready = net.sem(f"{tag}_far_ready", c)
        gathered = [net.sem(f"{tag}_gathered{s}", c) for s in range(SL)]
        rel_ready = net.sem(f"{tag}_rel_ready", c)
        hot_ready = net.sem(f"{tag}_hot_ready", c)
        prod_ready = net.sem(f"{tag}_prod_ready", c)
        act_msgs = net.sem(f"{tag}_act_msgs", c)
        dve_msgs = net.sem(f"{tag}_dve_msgs", c)
        agg_done = net.sem(f"{tag}_agg_done", c)
        acc_added = net.sem(f"{tag}_acc_added", c)
        if kind == "conv":
            attT_done = net.sem(f"{tag}_attT_done", c)
            attT_ready = net.sem(f"{tag}_attT_ready", c)
            hid_done = net.sem(f"{tag}_hid_done", c)
            hid_ready = net.sem(f"{tag}_hid_ready", c)
            w_done = net.sem(f"{tag}_w_done", c)
            w_used = net.sem(f"{tag}_w_used", c)
        block = c.enter_context(nc.Block())

        def steps(eng, body):
            for u in range(SL):
                body(0, u)
            with eng.Fori(1, NJ - 1) as j:
                for u in range(SL):
                    body(j, u)
            for u in range(SL):
                body(NJ - 1, u)

        def has(j, u, d):
            return not isinstance(j, int) or 0 <= SL * j + u + d < NI

        @block.sync
        def _(sp):
            def load(j, u):
                i = SL * j + u
                if has(j, u, -SL):
                    sp.wait_ge(agg_done, i - SL + 1)
                e = sp.value_load(erow[0:1, bass.ds(i, 1)], min_val=0, max_val=E)
                sp.dma_start(recs[:, u, :, :], rec[bass.ds(e, GE), :].rearrange("(p j) w -> p j w", j=JB))\
                    .then_inc(rec_loaded[u], 16)
            steps(sp, load)

        @block.gpsimd
        def _(pool):
            this, past = Count(pool, f"{tag}_this", 0), Count(pool, f"{tag}_past", 0)

            def gather(j, u):
                i = SL * j + u
                this.up(1)
                if has(j, u, -SL):
                    past.up(1)
                pool.wait_ge(far_ready, 1)
                pool.wait_ge(far_ready, this.reg)
                if has(j, u, -SL):
                    pool.wait_ge(agg_done, past.reg)
                for q in range(JB):
                    pool.indirect_dma_start(rows[:, u, q, :], None, table,
                                            bass.IndirectOffsetOnAxis(ap=far[:, u, q:q + 1], axis=0))\
                        .then_inc(gathered[u], 16)
            steps(pool, gather)

        @block.scalar
        def _(act):
            AHEAD = 2

            def convert(j, u):
                act.wait_ge(rec_loaded[u], 16 * j + 16)
                act.activation(far[:, u, :], recs[:, u, :, 1], ACT.Copy).then_inc(far_ready, 1)

            def net_in(j, u):
                i = SL * j + u
                act.wait_ge(attT_done, i + 1)
                act.activation(attT[:, u % 2, :], attT_ps[:, :], ACT.Copy).then_inc(attT_ready, 1)
                act.wait_ge(hid_done, i + 1)
                act.activation(hidT[:, u % 2, :], hid_ps[:, :], ACT.Silu).then_inc(hid_ready, 1)

            for u in range(AHEAD):
                convert(0, u)
            if kind == "conv":
                net_in(0, 0)

            def body(j, u):
                i = SL * j + u
                if has(j, u, AHEAD):
                    convert(j + (u + AHEAD) // SL, (u + AHEAD) % SL)
                if kind == "conv" and has(j, u, 1):
                    net_in(j + (u + 1) // SL, (u + 1) % SL)
                act.wait_ge(gathered[u], 64 * j + 64)
                if has(j, u, -2):
                    act.wait_ge(dve_msgs if kind == "conv" else agg_done, i - 1)
                for q in range(JB):
                    by = recs[:, u, q, dist:dist + 1]
                    if kind == "plain":
                        last = act.activation(msg[:, u % 2, q, 0:D], rows[:, u, q, 0:D], ACT.Copy, scale=by)
                    elif kind == "conv":
                        last = act.activation(scaled[:, u % 2, q, :], rows[:, u, q, 0:D], ACT.Copy, scale=by)
                    else:
                        act.activation(msg[:, u % 2, q, 0:S0], rows[:, u, q, 0:S0], ACT.Copy, scale=by)
                        last = act.activation(
                            msg[:, u % 2, q, VD:4 * VD].rearrange("p (k f) -> p k f", k=3)[:, :, 0:V0],
                            rows[:, u, q, S0:D].rearrange("p (f k) -> p k f", k=3), ACT.Copy, scale=by)
                last.then_inc(act_msgs, 1)
            steps(act, body)

        @block.vector
        def _(dve):
            dve.memset(acc[:, :, :], 0.0).then_inc(acc_zero, 1)
            if kind == "conv":
                dve.memset(msg[:, :, :, 4 * VD:C], 1.0)
            dve.wait_ge(acc_zero, 1)

            def add_up(j, u):
                i = SL * j + u
                t = dve.value_load(trow[0:1, bass.ds(i, 1)], min_val=0, max_val=NT)
                dve.wait_ge(agg_done, i + 1)
                if has(j, u, -1):
                    dve.wait_ge(acc_added, i)
                to = acc[:, bass.ds(t, 1), :].rearrange("p a b -> p (a b)")[:, 0:C]
                dve.tensor_tensor(to, to, agg_ps[u % 2][:, 0:C], ALU.add).then_inc(acc_added, 1)

            def body(j, u):
                i, m = SL * j + u, u % 2
                dve.wait_ge(rec_loaded[u], 16 * j + 16)
                dve.tensor_scalar(rel[:, m, :], recs[:, u, :, 0], tbase[:, bass.ds(i, 1)], None, ALU.subtract)\
                    .then_inc(rel_ready, 1)
                if has(j, u, -2):
                    dve.wait_ge(agg_done, i - 1)
                dve.wait_ge(rel_ready, i + 1)
                dve.tensor_tensor(hot[:, m, :, :], net.ramp[:, :].unsqueeze(1).broadcast_to([P, JB, P]),
                                  rel[:, m, :].unsqueeze(2).broadcast_to([P, JB, P]), ALU.is_equal)\
                    .then_inc(hot_ready, 1)
                dve.wait_ge(gathered[u], 64 * j + 64)
                r = rows[:, u, :, :]
                out = msg[:, m, :, :]
                e3 = recs[:, u, :, vec:vec + 3]
                v = r[:, :, S0:D].rearrange("p j (f k) -> p j f k", k=3)
                if kind == "plain":
                    pv = prod[:, 0, :, :].rearrange("p j (f k) -> p j f k", k=3)
                    dve.tensor_tensor(pv, v, e3.unsqueeze(2).broadcast_to([P, JB, V0, 3]), ALU.mult)\
                        .then_inc(prod_ready, 1)
                    dve.tensor_tensor(out[:, :, D + V0:D + V0 + VD].rearrange("p j (f k) -> p j f k", k=3),
                                      r[:, :, D:TW].unsqueeze(3).broadcast_to([P, JB, V0, 3]),
                                      e3.unsqueeze(2).broadcast_to([P, JB, V0, 3]), ALU.mult)
                    dve.wait_ge(prod_ready, i + 1)
                    dve.tensor_reduce(out[:, :, D:D + V0], pv, AXX, ALU.add).then_inc(dve_msgs, 1)
                elif kind == "cross":
                    vk = r[:, :, S0:D].rearrange("p j (f k) -> p j k f", k=3)
                    for b in range(3):
                        last = dve.tensor_tensor(prod[:, b, :, :].rearrange("p j (k f) -> p j k f", k=3), vk,
                                                 e3[:, :, b:b + 1].unsqueeze(3).broadcast_to([P, JB, 3, V0]), ALU.mult)
                    last.then_inc(prod_ready, 1)
                    o3 = out[:, :, VD:4 * VD].rearrange("p j (k f) -> p j k f", k=3)
                    dve.tensor_tensor(o3[:, :, :, V0:2 * V0], r[:, :, D:TW].unsqueeze(2).broadcast_to([P, JB, 3, V0]),
                                      e3.unsqueeze(3).broadcast_to([P, JB, 3, V0]), ALU.mult)

                    def p(a, b):
                        return prod[:, b, :, a * V0:(a + 1) * V0]
                    dve.wait_ge(prod_ready, 2 * i + 1)
                    dve.tensor_tensor(out[:, :, S0:VD], p(0, 0), p(1, 1), ALU.add).then_inc(prod_ready, 1)
                    for k in range(3):
                        a, b = (k + 1) % 3, (k + 2) % 3
                        dve.tensor_tensor(o3[:, :, k, 2 * V0:3 * V0], p(a, b), p(b, a), ALU.subtract)
                    dve.wait_ge(prod_ready, 2 * i + 2)
                    dve.tensor_tensor(out[:, :, S0:VD], out[:, :, S0:VD], p(2, 2), ALU.add).then_inc(dve_msgs, 1)
                else:
                    wv = w_ps[m][:, :, :, :].rearrange("p a b w -> p (a b) w")
                    pv = prod[:, 0, :, :].rearrange("p j (f k) -> p j f k", k=3)
                    dve.tensor_tensor(pv, v, e3.unsqueeze(2).broadcast_to([P, JB, V0, 3]), ALU.mult)\
                        .then_inc(prod_ready, 1)
                    dve.wait_ge(w_done, i + 1)
                    dve.tensor_tensor(w0f[:, :, :], wv[:, :, S0:2 * S0], r[:, :, 0:S0], ALU.mult)
                    dve.wait_ge(prod_ready, 3 * i + 1)
                    dve.tensor_reduce(dot[:, :, :], pv, AXX, ALU.add).then_inc(prod_ready, 1)
                    dve.wait_ge(act_msgs, i + 1)
                    sc = scaled[:, m, :, :]
                    dve.tensor_tensor(out[:, :, 0:S0], wv[:, :, 0:S0], sc[:, :, 0:S0], ALU.mult)
                    o3 = out[:, :, VD:4 * VD].rearrange("p j (k f) -> p j k f", k=3)
                    dve.tensor_tensor(o3[:, :, :, S0:VD], wv[:, :, 2 * S0:2 * S0 + V0].unsqueeze(2).broadcast_to([P, JB, 3, V0]),
                                      sc[:, :, S0:D].rearrange("p j (f k) -> p j k f", k=3), ALU.mult)
                    dve.wait_ge(prod_ready, 3 * i + 2)
                    dve.tensor_tensor(out[:, :, S0:VD], wv[:, :, 2 * S0 + V0:TW], dot[:, :, :], ALU.mult)\
                        .then_inc(prod_ready, 1)
                    dve.tensor_tensor(o3[:, :, :, 0:S0], w0f[:, :, :].unsqueeze(2).broadcast_to([P, JB, 3, S0]),
                                      e3.unsqueeze(3).broadcast_to([P, JB, 3, S0]), ALU.mult).then_inc(dve_msgs, 1)
                if has(j, u, -1):
                    add_up(j + (u - 1) // SL, (u - 1) % SL)
            steps(dve, body)
            add_up(NJ - 1, SL - 1)

        @block.tensor
        def _(pe):
            def attributes(j, u):
                i = SL * j + u
                pe.wait_ge(rec_loaded[u], 16 * j + 16)
                if has(j, u, -1):
                    pe.wait_ge(attT_ready, i)
                for q in range(JB):
                    last = pe.matmul(attT_ps[:, q * P:(q + 1) * P], recs[:, u, q, 6:22], net.ident[:, :],
                                     start=True, stop=True)
                last.then_inc(attT_done, 1)

            def hidden(j, u):
                i = SL * j + u
                pe.wait_ge(attT_ready, i + 1)
                if has(j, u, -1):
                    pe.wait_ge(hid_ready, i)
                pe.matmul(hid_ps[:, :], net.wfc1[:, :], attT[:, u % 2, :], start=True, stop=True).then_inc(hid_done, 1)

            def weights(j, u):
                i = SL * j + u
                pe.wait_ge(hid_ready, i + 1)
                if has(j, u, -2):
                    pe.wait_ge(dve_msgs, i - 1)
                for q in range(JB):
                    last = pe.matmul(w_ps[u % 2][:, q // 2, q % 2, 0:TW], hidT[:, u % 2, q * P:(q + 1) * P],
                                     net.wfc2[:, :], start=True, stop=True)
                last.then_inc(w_done, 1)

            if kind == "conv":
                attributes(0, 0)
                hidden(0, 0)
                weights(0, 0)

            def body(j, u):
                i, m = SL * j + u, u % 2
                if kind == "conv" and has(j, u, 1):
                    nxt = (j + (u + 1) // SL, (u + 1) % SL)
                    attributes(*nxt)
                    hidden(*nxt)
                    weights(*nxt)
                pe.wait_ge(hot_ready, i + 1)
                if has(j, u, -2):
                    pe.wait_ge(acc_added, i - 1)
                if kind == "plain":
                    pe.wait_ge(gathered[u], 64 * j + 64)
                    for q in range(JB):
                        pe.matmul(agg_ps[m][:, 0:D], hot[:, m, q, :], rows[:, u, q, 0:D], start=(q == 0),
                                  stop=False, skip_group_check=True)
                        if q == 0:
                            pe.wait_ge(act_msgs, i + 1)
                            pe.wait_ge(dve_msgs, i + 1)
                        last = pe.matmul(agg_ps[m][:, D:C], hot[:, m, q, :], msg[:, m, q, :], start=False,
                                         stop=(q == JB - 1), skip_group_check=True)
                else:
                    pe.wait_ge(act_msgs, i + 1)
                    pe.wait_ge(dve_msgs, i + 1)
                    for q in range(JB):
                        last = pe.matmul(agg_ps[m][:, 0:C], hot[:, m, q, :], msg[:, m, q, 0:C], start=(q == 0),
                                         stop=(q == JB - 1))
                last.then_inc(agg_done, 1)
            steps(pe, body)



XS, XV, AS, AV = 0, 8, 20, 24
NREP = 30
SOURCES = ([(0, n) for n in range(16)] + [(2, n) for n in range(4)]
           + [(1, n) for n in range(8)] + [(2, 2), (2, 3)])


def outer_products(lay):
    w = lay["chunks"]
    out = [(XS, 8, AS + v, 1, w["ss"][0], v, 0, S0) for v in range(4)]
    out += [(XV + 4 * k, 4, AV + 2 * k, 2, w["vv"][0], 0, 0, S0) for k in range(3)]
    for k in range(3):
        out += [(XS, 8, AV + 2 * k + v, 1, w["sv"][0], v, S0 + V0 * k, V0) for v in range(2)]
        out += [(XV + 4 * k, 4, AS + v, 2, w["vs"][0], v, S0 + V0 * k, V0) for v in (0, 2)]
    return out


def node_stage(net, tag, kind, nxt, lay, prep, acc, C, table, out):
    nc = net.nc
    outer = outer_products(lay) if kind == "plain" else []
    NO = len(outer)
    with net.stage() as c:
        agg = net.sb(f"{tag}_agg", [P, 2, C], F32, c)
        xin = net.sb(f"{tag}_xin", [P, 2, D], F32, c)
        xnew = net.sb(f"{tag}_xnew", [P, 2, D], F32, c)
        aggT = net.sb(f"{tag}_aggT", [P, 2 * P], F32, c)
        vecT = net.sb(f"{tag}_vecT", [VD, 3 * P], F32, c)
        xT = net.sb(f"{tag}_xT", [S0, 4 * P], F32, c)
        a_nat = net.sb(f"{tag}_a_nat", [P, D], F32, c)
        xa = net.sb(f"{tag}_xa", [P, 3, P], F32, c)
        reps = net.sb(f"{tag}_reps", [P, NREP, P], F32, c)
        prods = net.sb(f"{tag}_prods", [P, 3, 8, P], F32, c)
        y = net.sb(f"{tag}_y", [P, 2, D], F32, c)
        stats = net.sb(f"{tag}_stats", [P, 6], F32, c)
        mv = net.sb(f"{tag}_mv", [P, 2], F32, c)
        sd = net.sb(f"{tag}_sd", [P, 1], F32, c)
        rstd = net.sb(f"{tag}_rstd", [P, 1], F32, c)
        small = net.sb(f"{tag}_small", [P, 8], F32, c)
        av = net.sb(f"{tag}_av", [P, 2, 1], F32, c)
        nT = net.sb(f"{tag}_nT", [S0, 4 * P], F32, c)
        trow = net.sb(f"{tag}_trow", [P, 2, TW], F32, c)
        aggT_ps = net.ps(f"{tag}_aggT_ps", [P, 512], c)
        vecT_ps = net.ps(f"{tag}_vecT_ps", [P, 512], c)
        xT_ps = net.ps(f"{tag}_xT_ps", [P, 512], c)
        lin_ps = net.ps(f"{tag}_lin_ps", [P, 512], c)
        rep_ps = [net.ps(f"{tag}_rep_ps{s}", [P, 512], c) for s in range(2)]
        u_ps = net.ps(f"{tag}_u_ps", [P, 512], c)
        nT_ps = net.ps(f"{tag}_nT_ps", [P, 512], c)
        next_ps = lin_ps if kind == "plain" else rep_ps[0]
        loaded = [net.sem(f"{tag}_loaded{s}", c) for s in range(2)]
        agg_transposed = net.sem(f"{tag}_agg_transposed", c)
        aggT_ready = net.sem(f"{tag}_aggT_ready", c)
        x_transposed = net.sem(f"{tag}_x_transposed", c)
        xT_ready = net.sem(f"{tag}_xT_ready", c)
        lin_done = net.sem(f"{tag}_lin_done", c)
        a_ready = net.sem(f"{tag}_a_ready", c)
        xa_zero = net.sem(f"{tag}_xa_zero", c)
        rstd_ready = net.sem(f"{tag}_rstd_ready", c)
        rep_done = net.sem(f"{tag}_rep_done", c)
        rep_ready = net.sem(f"{tag}_rep_ready", c)
        prod_ready = net.sem(f"{tag}_prod_ready", c)
        prod_used = net.sem(f"{tag}_prod_used", c)
        relu_ready = net.sem(f"{tag}_relu_ready", c)
        dve_step = net.sem(f"{tag}_dve_step", c)
        var_ready = net.sem(f"{tag}_var_ready", c)
        sd_ready = net.sem(f"{tag}_sd_ready", c)
        x_new = net.sem(f"{tag}_x_new", c)
        new_transposed = net.sem(f"{tag}_new_transposed", c)
        nT_ready = net.sem(f"{tag}_nT_ready", c)
        next_done = net.sem(f"{tag}_next_done", c)
        base_ready = net.sem(f"{tag}_base_ready", c)
        row_ready = net.sem(f"{tag}_row_ready", c)
        stored = [net.sem(f"{tag}_stored{s}", c) for s in range(2)]
        block = c.enter_context(nc.Block())

        NJT = NT // 2
        assert NT % 2 == 1

        def tiles(eng, body):
            body(0, 0)
            body(0, 1)
            with eng.Fori(1, NJT) as j:
                body(j, 0)
                body(j, 1)
            body(NJT, 0)

        def has(j, u, d):
            return not isinstance(j, int) or 0 <= 2 * j + u + d

        def prev(j, u):
            return j + (u - 1) // 2, (u - 1) % 2

        NLOAD = 1 if kind == "first" else 2

        @block.sync
        def _(sp):
            def body(j, u):
                t = 2 * j + u
                if has(j, u, -2):
                    sp.wait_ge(row_ready if kind == "first" else x_new, t - 1)
                sp.dma_start((xnew if kind == "first" else xin)[:, u, :],
                             net.xres[:, bass.ds(t, 1), :].rearrange("p a f -> p (a f)")).then_inc(loaded[u], 16)
                if kind != "first":
                    sp.dma_start(agg[:, u, :], acc[:, bass.ds(t, 1), 0:C].rearrange("p a f -> p (a f)"))\
                        .then_inc(loaded[u], 16)
                if has(j, u, -1):
                    store(*prev(j, u))

            def store(j, u):
                t = 2 * j + u
                if nxt is not None:
                    sp.wait_ge(row_ready, t + 1)
                    sp.dma_start(table[bass.ds(t * P, P), :], trow[:, u, :]).then_inc(stored[u], 16)
                else:
                    sp.wait_ge(x_new, t + 1)
                    rows = TAIL if isinstance(j, int) and t == NT - 1 else P
                    sp.dma_start(out[bass.ds(t * P, rows), :], xnew[0:rows, u, :]).then_inc(stored[u], 16)
            tiles(sp, body)
            store(NJT, 0)
            sp.wait_ge(stored[0], 16 * (NJT + 1))
            sp.wait_ge(stored[1], 16 * NJT)

        def v_of(ap):
            return ap.rearrange("p (f k) -> p k f", k=3)

        def k_of(ap):
            return ap.rearrange("p (k f) -> p k f", k=3)

        @block.tensor
        def _(pe):
            mm = pe.matmul

            def transpose(to, frm):
                return mm(to, frm, net.ident[:, :], start=True, stop=True)

            def prepare(j, u):
                t = 2 * j + u
                if kind == "first":
                    pe.wait_ge(loaded[u], 16 * j + 16)
                else:
                    pe.wait_ge(x_new, t + 1)
                if has(j, u, -1):
                    pe.wait_ge(nT_ready, t)
                transpose(nT_ps[0:S0, 0:P], xnew[:, u, 0:S0])
                xv = v_of(xnew[:, u, S0:D])
                for k in range(3):
                    last = transpose(nT_ps[0:V0, (k + 1) * P:(k + 2) * P], xv[:, k, :])
                last.then_inc(new_transposed, 1)
                pe.wait_ge(nT_ready, t + 1)
                if has(j, u, -1):
                    pe.wait_ge(row_ready, t)
                    if nxt == "conv":
                        pe.wait_ge(base_ready, t)
                if nxt == "conv":
                    mm(next_ps[:, 192:320], nT[:, 0:P], prep["ws"], start=True, stop=True)
                    for k in range(3):
                        last = mm(next_ps[:, 320 + 64 * k:384 + 64 * k], nT[0:V0, (k + 1) * P:(k + 2) * P],
                                  prep["wv"], start=True, stop=True)
                else:
                    last = mm(next_ps[:, 192:224], nT[:, 0:P], prep["ws"], start=True, stop=True)
                last.then_inc(next_done, 1)

            def body(j, u):
                t = 2 * j + u
                if kind == "first":
                    prepare(j, u)
                    return
                pe.wait_ge(loaded[u], 32 * j + 32)
                if has(j, u, -1):
                    pe.wait_ge(aggT_ready, t)
                ag = agg[:, u, :]
                if kind == "plain":
                    for n in range(2):
                        transpose(aggT_ps[S0 * n:S0 * (n + 1), 0:P], ag[:, D * n:D * n + S0])
                    transpose(aggT_ps[0:V0, P:2 * P], ag[:, 2 * D:2 * D + V0])
                    vecs = [ag[:, S0:D], ag[:, D + S0:2 * D], ag[:, 2 * D + V0:2 * D + V0 + VD]]
                    for n, ap in enumerate(vecs):
                        for k in range(3):
                            last = transpose(vecT_ps[V0 * n:V0 * (n + 1), k * P:(k + 1) * P], v_of(ap)[:, k, :])
                    last.then_inc(agg_transposed, 1)
                    if has(j, u, -1):
                        pe.wait_ge(xT_ready, t)
                    xu = xin[:, u, :]
                    xv = v_of(xu[:, S0:D])
                    transpose(xT_ps[0:S0, 0:P], xu[:, 0:S0])
                    transpose(xT_ps[S0:S0 + V0, 0:P], xv[:, 0, :])
                    transpose(xT_ps[S0 + V0:P, 0:P], xv[:, 1, :])
                    transpose(xT_ps[0:V0, P:2 * P], xv[:, 2, :]).then_inc(x_transposed, 1)

                    def replicate(g):
                        if g >= 2 or has(j, u, -1):
                            pe.wait_ge(rep_ready, 8 * t + g - 1)
                        for n, (part, sel) in enumerate(SOURCES[4 * g:4 * g + 4]):
                            sels = net.sel_v if 4 * g + n >= AS else net.sel_u
                            last = mm(rep_ps[g % 2][:, n * P:(n + 1) * P], sels[:, sel, :], xa[:, part, :],
                                      start=True, stop=True)
                        last.then_inc(rep_done, 1)

                    pe.wait_ge(xT_ready, t + 1)
                    for g in range(4):
                        replicate(g)
                    pe.wait_ge(aggT_ready, t + 1)
                    mm(lin_ps[0:S0, 0:P], lay["m0"], aggT[:, 0:P], start=True, stop=False)
                    mm(lin_ps[0:S0, 0:P], lay["mdot"], aggT[0:V0, P:2 * P], start=False, stop=True)
                    mm(lin_ps[S0:S0 + V0, 0:P], lay["m1"], vecT[:, 0:P], start=True, stop=True)
                    mm(lin_ps[S0 + V0:P, 0:P], lay["m1"], vecT[:, P:2 * P], start=True, stop=True)
                    mm(vecT_ps[V0:2 * V0, 3 * P:4 * P], lay["m1"], vecT[:, 2 * P:3 * P], start=True, stop=True)\
                        .then_inc(lin_done, 1)
                    pe.wait_ge(a_ready, t + 1)
                    for g in range(4, 8):
                        replicate(g)
                    if has(j, u, -1):
                        prepare(*prev(j, u))
                    col = None
                    for n, (_, nu, _, nv, w, v0, to, wd) in enumerate(outer):
                        if to != col:
                            col = to
                            k = (to - S0) // V0
                            part, r = (0, 0) if to == 0 else ((0, S0), (0, S0 + V0), (2, 0))[k]
                            mm(u_ps[:, to:to + wd], xa[r:r + wd, part, :], lay["l0"] if to == 0 else lay["l1"][r:r + V0, :],
                               start=True, stop=False)
                        pe.wait_ge(prod_ready, NO * t + n + 1)
                        ends = n + 1 == NO or outer[n + 1][6] != to
                        for v in range(nv):
                            for uu in range(nu):
                                last = mm(u_ps[:, to:to + wd], prods[:, n % 3, v * nu + uu, :], w[:, uu, v0 + v, :],
                                          start=False, stop=ends and v == nv - 1 and uu == nu - 1)
                        last.then_inc(prod_used, 1)
                else:
                    transpose(aggT_ps[0:VD, 0:P], ag[:, 0:VD])
                    for k in range(3):
                        last = transpose(vecT_ps[0:VD, k * P:(k + 1) * P], ag[:, VD * (k + 1):VD * (k + 2)])
                    last.then_inc(agg_transposed, 1)
                    pe.wait_ge(aggT_ready, t + 1)
                    if kind == "conv":
                        if has(j, u, -1):
                            pe.wait_ge(a_ready, t)
                        mm(lin_ps[:, 0:S0 + 1], aggT[0:VD, 0:P], lay["scal"], start=True, stop=True)
                        for k in range(3):
                            last = mm(lin_ps[:, 65 + V0 * k:65 + V0 * (k + 1)], vecT[:, k * P:(k + 1) * P],
                                      lay["vec"], start=True, stop=True)
                        last.then_inc(lin_done, 1)
                    else:
                        if has(j, u, -1):
                            pe.wait_ge(xT_ready, t)
                        mm(xT_ps[0:S0, 0:P], lay["scal"], aggT[0:VD, 0:P], start=True, stop=True)
                        mm(xT_ps[0:V0, P:4 * P], lay["vec"], vecT[:, :], start=True, stop=True).then_inc(x_transposed, 1)
                        pe.wait_ge(xT_ready, t + 1)
                        if has(j, u, -1):
                            pe.wait_ge(relu_ready, t)
                        mm(lin_ps[:, 0:S0], xT[:, 0:P], lay["hs"], start=True, stop=True)
                        for k in range(3):
                            last = mm(lin_ps[:, S0 + V0 * k:S0 + V0 * (k + 1)], xT[0:V0, (k + 1) * P:(k + 2) * P],
                                      lay["hv"], start=True, stop=True)
                        last.then_inc(lin_done, 1)
                    if nxt is not None and has(j, u, -1):
                        prepare(*prev(j, u))
            tiles(pe, body)
            if kind != "first" and nxt is not None:
                prepare(NJT, 0)

        @block.scalar
        def _(act):
            def copy(to, frm, **kw):
                return act.activation(to, frm, ACT.Copy, **kw)

            def prepare(j, u):
                t = 2 * j + u
                act.wait_ge(new_transposed, t + 1)
                if has(j, u, -1):
                    act.wait_ge(next_done, t)
                copy(nT[:, 0:P], nT_ps[0:S0, 0:P])
                copy(nT[0:V0, P:4 * P], nT_ps[0:V0, P:4 * P]).then_inc(nT_ready, 1)
                if has(j, u, -2):
                    act.wait_ge(stored[u], 16 * j)
                act.wait_ge(next_done, t + 1)
                if nxt == "conv":
                    by = av[:, u, :]
                    act.wait_ge(x_new, t + 1)
                    copy(trow[:, u, 0:S0], next_ps[:, 192:256], scale=by)
                    copy(v_of(trow[:, u, S0:D]),
                         next_ps[:, 320:512].rearrange("p (k h f) -> p k h f", k=3, h=2)[:, :, 0, :], scale=by)
                    copy(trow[:, u, D:TW], next_ps[:, 192:224]).then_inc(row_ready, 1)
                else:
                    copy(trow[:, u, 0:D], xnew[:, u, :])
                    copy(trow[:, u, D:TW], next_ps[:, 192:224]).then_inc(row_ready, 1)

            def body(j, u):
                t = 2 * j + u
                if kind == "first":
                    act.wait_ge(loaded[u], 16 * j + 16)
                    prepare(j, u)
                    return
                act.wait_ge(agg_transposed, t + 1)
                if has(j, u, -1):
                    act.wait_ge(lin_done, t)
                if kind == "plain":
                    copy(aggT[:, 0:P], aggT_ps[:, 0:P])
                    copy(aggT[0:V0, P:2 * P], aggT_ps[0:V0, P:2 * P])
                    copy(vecT[:, :], vecT_ps[0:VD, 0:3 * P]).then_inc(aggT_ready, 1)
                    act.wait_ge(x_transposed, t + 1)
                    if has(j, u, -1):
                        act.wait_ge(prod_used, NO * t)
                    copy(xa[:, 0, :], xT_ps[:, 0:P])
                    copy(xa[0:V0, 2, :], xT_ps[0:V0, P:2 * P]).then_inc(xT_ready, 1)
                    if has(j, u, -1):
                        act.wait_ge(prod_ready, NO * t)
                    for g in range(8):
                        if g == 4:
                            act.wait_ge(lin_done, t + 1)
                            if not has(j, u, -1):
                                act.wait_ge(xa_zero, 1)
                            copy(xa[:, 1, :], lin_ps[:, 0:P])
                            copy(xa[V0:2 * V0, 2, :], vecT_ps[V0:2 * V0, 3 * P:4 * P]).then_inc(a_ready, 1)
                        act.wait_ge(rep_done, 8 * t + g + 1)
                        n = min(4, NREP - 4 * g)
                        copy(reps[:, 4 * g:4 * g + n, :].rearrange("p a n -> p (a n)"), rep_ps[g % 2][:, 0:n * P])\
                            .then_inc(rep_ready, 1)
                else:
                    copy(aggT[0:VD, 0:P], aggT_ps[0:VD, 0:P])
                    copy(vecT[:, :], vecT_ps[0:VD, 0:3 * P]).then_inc(aggT_ready, 1)
                    if kind == "cross":
                        act.wait_ge(x_transposed, t + 1)
                        copy(xT[:, 0:P], xT_ps[0:S0, 0:P])
                        copy(xT[0:V0, P:4 * P], xT_ps[0:V0, P:4 * P]).then_inc(xT_ready, 1)
                        act.wait_ge(lin_done, t + 1)
                        if has(j, u, -1):
                            act.wait_ge(var_ready, t)
                        act.activation(a_nat[:, 0:S0], lin_ps[:, 0:S0], ACT.Relu)
                        act.activation(v_of(a_nat[:, S0:D]), k_of(lin_ps[:, S0:D]), ACT.Relu).then_inc(relu_ready, 1)
                if nxt is not None and has(j, u, -1):
                    prepare(*prev(j, u))
                act.wait_ge(var_ready, t + 1)
                act.activation(sd[:, :], mv[:, 1:2], ACT.Sqrt, bias=net.eps[:, 0:1]).then_inc(sd_ready, 1)
            tiles(act, body)
            if kind != "first" and nxt is not None:
                prepare(NJT, 0)

        @block.vector
        def _(dve):
            stats_count = Count(dve, f"{tag}_stats_count", 0)
            CHAIN = {"first": 0, "plain": 2, "conv": 6, "cross": 2}[kind]

            def base(j, u):
                t = 2 * j + u
                dve.wait_ge(row_ready, t + 1)
                b = net.base[:, bass.ds(t, 1), :].rearrange("p a f -> p (a f)")
                dve.scalar_tensor_tensor(b[:, 0:S0], next_ps[:, 256:320], av[:, u, :], xnew[:, u, 0:S0],
                                         ALU.mult, ALU.add)
                for k in range(3):
                    last = dve.scalar_tensor_tensor(
                        v_of(b[:, S0:D])[:, k, :], next_ps[:, 352 + 64 * k:384 + 64 * k], av[:, u, :],
                        v_of(xnew[:, u, S0:D])[:, k, :], ALU.mult, ALU.add)
                last.then_inc(base_ready, 1)

            def body(j, u):
                t = 2 * j + u
                if kind == "first":
                    return
                n_own = [0]

                def step(ins):
                    n_own[0] += 1
                    ins.then_inc(dve_step, 1)
                    dve.wait_ge(dve_step, CHAIN * t + n_own[0])

                x, ys = xin[:, u, :], y[:, u, :]
                if kind == "plain":
                    dve.wait_ge(loaded[u], 32 * j + 32)
                    if nxt == "conv" and has(j, u, -1):
                        base(*prev(j, u))
                    for n, (u0, nu, v0, nv, _, _, _, _) in enumerate(outer):
                        need = max(u0 + nu, v0 + nv)
                        dve.wait_ge(rep_ready, 8 * t + (need + 3) // 4)
                        if n >= 3:
                            dve.wait_ge(prod_used, NO * t + n - 2)
                        elif has(j, u, -1):
                            dve.wait_ge(prod_used, NO * t + n - 2)
                        dve.tensor_tensor(
                            prods[:, n % 3, :, :].rearrange("p (v u) n -> p v u n", v=nv),
                            reps[:, u0:u0 + nu, :].unsqueeze(1).broadcast_to([P, nv, nu, P]),
                            reps[:, v0:v0 + nv, :].unsqueeze(2).broadcast_to([P, nv, nu, P]),
                            ALU.mult).then_inc(prod_ready, 1)
                    dve.wait_ge(prod_used, NO * t + NO)
                    dve.scalar_tensor_tensor(ys[:, 0:S0], x[:, 0:S0], 2.0, u_ps[:, 0:S0], ALU.mult, ALU.add)
                    step(dve.scalar_tensor_tensor(v_of(ys[:, S0:D]), v_of(x[:, S0:D]), 2.0, k_of(u_ps[:, S0:D]),
                                                  ALU.mult, ALU.add))
                elif kind == "conv":
                    b = net.base[:, bass.ds(t, 1), :].rearrange("p a f -> p (a f)")
                    dve.wait_ge(loaded[u], 32 * j + 32)
                    step(dve.tensor_scalar(small[:, 0:1], agg[:, u, 4 * VD:C], 1.0, None, ALU.max))
                    step(dve.reciprocal(small[:, 1:2], small[:, 0:1]))
                    step(dve.scalar_tensor_tensor(small[:, 2:3], small[:, 1:2], 1.0 / math.sqrt(VD),
                                                  net.nodea[:, bass.ds(t, 1)], ALU.mult, ALU.mult))
                    dve.wait_ge(lin_done, t + 1)
                    step(dve.tensor_tensor(small[:, 3:4], lin_ps[:, S0:S0 + 1], small[:, 2:3], ALU.mult))
                    step(dve.tensor_tensor(small[:, 4:5], small[:, 3:4], small[:, 2:3], ALU.mult))
                    dve.scalar_tensor_tensor(ys[:, 0:S0], lin_ps[:, 0:S0], small[:, 4:5], b[:, 0:S0],
                                             ALU.mult, ALU.add)
                    step(dve.scalar_tensor_tensor(v_of(ys[:, S0:D]), k_of(lin_ps[:, S0 + 1:D + 1]), small[:, 4:5],
                                                  v_of(b[:, S0:D]), ALU.mult, ALU.add))
                else:
                    dve.wait_ge(loaded[u], 32 * j + 32)
                    dve.wait_ge(relu_ready, t + 1)
                    step(dve.scalar_tensor_tensor(ys, x, 2.0, a_nat[:, :], ALU.mult, ALU.add))
                dve.bn_stats(stats[:, :], ys).then_inc(a_ready if kind == "conv" else dve_step, 1)
                stats_count.up(1 if kind == "conv" else CHAIN)
                dve.wait_ge(loaded[0], 16)
                dve.wait_ge(a_ready if kind == "conv" else dve_step, stats_count.reg)
                dve.bn_aggr(mv[:, :], stats[:, :]).then_inc(var_ready, 1)
                if nxt == "conv":
                    if has(j, u, -2):
                        dve.wait_ge(row_ready, t - 1)
                    dve.tensor_copy(av[:, u, :], net.nodea[:, bass.ds(t, 1)])
                dve.wait_ge(sd_ready, t + 1)
                dve.reciprocal(rstd[:, :], sd[:, :]).then_inc(rstd_ready, 1)
                dve.wait_ge(rstd_ready, t + 1)
                if has(j, u, -2):
                    if nxt is not None:
                        dve.wait_ge(row_ready, t - 1)
                    else:
                        dve.wait_ge(stored[u], 16 * j)
                if nxt is not None:
                    dve.tensor_scalar(net.xres[:, bass.ds(t, 1), :].rearrange("p a f -> p (a f)"), ys,
                                      mv[:, 0:1], rstd[:, 0:1], ALU.subtract, ALU.mult)
                dve.tensor_scalar(xnew[:, u, :], ys, mv[:, 0:1], rstd[:, 0:1], ALU.subtract, ALU.mult)\
                    .then_inc(x_new, 1)
            if kind == "plain":
                dve.memset(xa[2 * V0:P, 2, :], 0.0).then_inc(xa_zero, 1)
            tiles(dve, body)
            if nxt == "conv":
                base(NJT, 0)


def gnn_kernel(nc, ins, out):
    with ExitStack() as ctx:
        net = Net(nc, ctx)
        ctx.enter_context(nc.allow_non_contiguous_dma(reason="small tables, one value a node"))
        g = lambda n: ins[n]
        rec_src = net.dram("rec_src", [E + GE, 6])
        rec_dst = net.dram("rec_dst", [E + GE, 22])
        net.pads = [(rec_src, 6), (rec_dst, 22)]
        table = net.dram("table", [NPAD, TW])
        net.xres = net.sb("xres", [P, NT, D])
        net.base = net.sb("base", [P, NT, D])
        net.nodea = net.sb("nodea", [P, NT])
        net.wfc1 = net.sb("wfc1", [16, S0])
        net.wfc2 = net.sb("wfc2", [S0, TW])

        def full_layer(n, ss, vv, sv, vs, l0, l1, m0d, m1d, m0, m1, mdot, f, msv, fsv):
            t = {k: net.sb(f"w{n}_{k}", shape) for k, shape in (
                ("ss", [P, 8, 4, S0]), ("vv", [P, 4, 2, S0]), ("sv", [P, 8, 2, V0]), ("vs", [P, 4, 4, V0]),
                ("l0", [S0, S0]), ("l1", [P, V0]), ("m0", [2 * S0, S0]), ("m1", [VD, V0]), ("mdot", [V0, S0]),
                ("msv", [S0, V0]))}
            lay = {"chunks": {"ss": (t["ss"], ss), "vv": (t["vv"], vv), "sv": (t["sv"], sv), "vs": (t["vs"], vs)},
                   "plain": [(t["l0"][:, :], l0), (t["l1"][0:V0, :], l1), (t["l1"][S0:S0 + V0, :], l1),
                             (t["l1"][S0 + V0:P, :], l1), (t["m0"][0:S0, :], m0), (t["m0"][S0:2 * S0, :], m0d),
                             (t["m1"][0:V0, :], m1), (t["m1"][V0:2 * V0, :], m1d), (t["mdot"][:, :], mdot),
                             (t["msv"][:, :], msv)],
                   "scales": [(t["ss"][:, :, :, :], f["ss"]), (t["vv"][:, :, :, :], f["vv"]),
                              (t["sv"][:, :, :, :], f["uv"]), (t["vs"][:, :, :, :], f["uv"]),
                              (t["l0"][:, :], f["l0"]), (t["l1"][0:V0, :], f["l1"]), (t["l1"][S0:P, :], f["l1"]), (t["m0"][0:S0, :], f["m0"]),
                              (t["m0"][S0:2 * S0, :], f["m0d"]), (t["m1"][0:V0, :], f["m1"]),
                              (t["m1"][V0:2 * V0, :], f["m1d"]), (t["mdot"][:, :], f["mdot"]), (t["msv"][:, :], fsv)]}
            for k in ("l0", "l1", "m0", "m1", "mdot"):
                lay[k] = t[k][:, :]
            lay["prep"] = {"ws": t["msv"][:, :]}
            return lay

        i64, i32, i96 = 1.0 / 8, 1.0 / math.sqrt(V0), 1.0 / math.sqrt(VD)
        fan0, fan1 = S0 * S0 + V0 * V0, 2 * S0 * V0
        lay0 = full_layer(0, g("L0_gnn_wu000"), g("L0_gnn_wu110"), g("L0_gnn_wu011"), g("L0_gnn_wu101"),
                          g("L0_gnn_lu0"), g("L0_gnn_lu1"),
                          g("L0_gnn_wm000").rearrange("u o w -> u (o w)"), g("L0_gnn_wm101").rearrange("u o w -> u (o w)"),
                          g("L0_gnn_lm0"), g("L0_gnn_lm1"), g("L0_gnn_wm110").rearrange("u o w -> u (o w)"),
                          dict(ss=1 / math.sqrt(fan0), vv=K3 / math.sqrt(fan0), uv=1 / math.sqrt(fan1), l0=i64, l1=i32,
                               m0=i64, m0d=i96, m1=i32, m1d=i96, mdot=K3 * i96),
                          g("L0_gnn_wm011").rearrange("u o w -> u (o w)"), i96)
        lay2 = full_layer(2, g("L2_gnn_Wu_ss"), g("L2_gnn_Wu_vv"), g("L2_gnn_Wu_sv"), g("L2_gnn_Wu_vs"),
                          g("L2_gnn_Lu_s"), g("L2_gnn_Lu_v"), g("L2_gnn_Wm_ss"), g("L2_gnn_Wm_vs"),
                          g("L2_gnn_Lm_s"), g("L2_gnn_Lm_v"), g("L2_gnn_Wm_vv"),
                          dict(ss=0.015625, vv=K3 * 0.03125, uv=1 / math.sqrt(2048), l0=i64, l1=i32,
                               m0=i64, m0d=i64, m1=i32, m1d=i32, mdot=K3 * i32),
                          g("L2_gnn_Wm_sv"), i64)
        w1 = {k: net.sb(f"w1_{k}", s) for k, s in (("ws", [S0, 2 * S0]), ("wv", [V0, 2 * V0]),
                                                  ("scal", [VD, S0 + 1]), ("vec", [VD, V0]))}
        lay1 = {"chunks": {}, "plain": [
                    (w1["ws"][:, 0:S0], g("L1_gnn_Wl1_0")), (w1["ws"][:, S0:2 * S0], g("L1_gnn_Wsc0")),
                    (w1["wv"][:, 0:V0], g("L1_gnn_Wl1_1")), (w1["wv"][:, V0:2 * V0], g("L1_gnn_Wsc1")),
                    (w1["scal"][:, 0:S0], g("L1_gnn_Wl2_s")), (w1["scal"][:, S0:S0 + 1], g("L1_gnn_Wa")),
                    (w1["vec"][:, :], g("L1_gnn_Wl2_v")),
                    (net.wfc1[:, :], g("L1_gnn_Wfc1")), (net.wfc2[:, :], g("L1_gnn_Wfc2")),
                    (net.xres[:, 0:NT - 1, :], g("x")[0:(NT - 1) * P, :].rearrange("(t p) f -> p t f", p=P)),
                    (net.xres[0:TAIL, NT - 1, :], g("x")[(NT - 1) * P:N, :]),
                    (net.nodea[:, 0:NT - 1].rearrange("p (t o) -> p t o", o=1),
                     g("node_vec1")[0:(NT - 1) * P, :].rearrange("(t p) o -> p t o", p=P)),
                    (net.nodea[0:TAIL, NT - 1:NT], g("node_vec1")[(NT - 1) * P:N, :])],
                "scales": [(w1["ws"][:, :], i64), (w1["wv"][:, :], i32), (net.wfc1[:, :], 0.25),
                           (net.wfc2[:, 0:TW - V0], i64), (net.wfc2[:, TW - V0:TW], i64 * K3)],
                "scal": w1["scal"][:, :], "vec": w1["vec"][:, :],
                "prep": {"ws": w1["ws"][:, :], "wv": w1["wv"][:, :]}}
        w3 = {k: net.sb(f"w3_{k}", s) for k, s in (("w3", [S0, V0]), ("scal", [VD, S0]), ("vec", [VD, V0]),
                                                  ("hs", [S0, S0]), ("hv", [V0, V0]))}
        C0, C1 = 1 / math.sqrt(S0 + V0), math.sqrt(3.0 / (S0 + 2 * V0))
        lay3 = {"chunks": {}, "plain": [
                    (w3["w3"][:, :], g("L3_gnn_W3")), (w3["scal"][0:S0, :], g("L3_gnn_W1")),
                    (w3["scal"][S0:VD, :], g("L3_gnn_W2")), (w3["vec"][0:V0, :], g("L3_gnn_W4")),
                    (w3["vec"][2 * V0:VD, :], g("L3_gnn_W5")), (w3["hs"][:, :], g("L3_gnn_Ws")),
                    (w3["hv"][:, :], g("L3_gnn_Wv"))],
                "scales": [(w3["w3"][:, :], C1 * K3), (w3["scal"][0:S0, :], C0), (w3["scal"][S0:VD, :], C0 * K3),
                           (w3["vec"][0:V0, :], C1 * K3), (w3["vec"][2 * V0:VD, :], C1 / math.sqrt(6.0)),
                           (w3["hs"][:, :], i64), (w3["hv"][:, :], i32)],
                "scal": w3["scal"][:, :], "vec": w3["vec"][:, :], "hs": w3["hs"][:, :], "hv": w3["hv"][:, :],
                "prep": {"ws": w3["w3"][:, :]}}

        with ExitStack() as c:
            block = c.enter_context(nc.Block())

            @block.vector
            def _(dve):
                dve.memset(net.xres[:, NT - 1, :], 0.0)
                dve.memset(net.nodea[:, NT - 1:NT], 0.0)

        constants(net, ins, [lay0, lay1, lay2, lay3])
        with ExitStack() as c:
            block = c.enter_context(nc.Block())

            @block.vector
            def _(dve):
                dve.tensor_copy(w3["vec"][V0:2 * V0, :], net.ident[V0:2 * V0, V0:2 * V0])
                for lay in (lay0, lay2):
                    dve.tensor_copy(lay["m1"][2 * V0:VD, :], net.ident[2 * V0:VD, 2 * V0:VD])

        def schedule(tag):
            return (net.sb(f"{tag}_erow", [1, NIP], I32), net.sb(f"{tag}_trow", [1, NIP], I32),
                    net.sb(f"{tag}_tbase", [P, NIP], F32))

        by_src, by_dst = schedule("src"), schedule("dst")
        sort_edges(net, "src", ins["src"], ins["dst"], [ins["edge_attr_4"]], rec_src, by_src)
        sort_edges(net, "dst", ins["dst"], ins["src"], [ins["edge_attr_4"], ins["edge_attr_16"]], rec_dst, by_dst)
        CM = 2 * D + V0 + VD
        acc = net.sb("acc", [P, NT + 1, CM])

        node_stage(net, "n", "first", "plain", None, lay0["prep"], acc, CM, table, out)
        edge_loop(net, "e0", "plain", rec_src, by_src, table, acc, CM)
        node_stage(net, "n0", "plain", "conv", lay0, lay1["prep"], acc, CM, table, out)
        edge_loop(net, "e1", "conv", rec_dst, by_dst, table, acc, 4 * VD + 1)
        node_stage(net, "n1", "conv", "plain", lay1, lay2["prep"], acc, 4 * VD + 1, table, out)
        edge_loop(net, "e2", "plain", rec_src, by_src, table, acc, CM)
        node_stage(net, "n2", "plain", "cross", lay2, lay3["prep"], acc, CM, table, out)
        edge_loop(net, "e3", "cross", rec_dst, by_dst, table, acc, 4 * VD)
        node_stage(net, "n3", "cross", None, lay3, None, acc, 4 * VD, table, out)


def kernel(**inputs):
    import numpy as _np
    import concourse.bacc as _bacc
    from concourse import mybir as _mybir
    from concourse.bass_utils import run_bass_kernel_spmd as _run

    nc = _bacc.Bacc("TRN2", target_bir_lowering=False, num_devices=1)
    arrays, args = {}, {}
    for name in inputs:
        a = _np.ascontiguousarray(inputs[name])
        arrays[f"in_{name}"] = a
        args[name] = nc.dram_tensor(f"in_{name}", a.shape, _mybir.dt.from_np(a.dtype), kind="ExternalInput").ap()
    out = nc.dram_tensor("out_x", (N, D), F32, kind="ExternalOutput").ap()
    gnn_kernel(nc, args, out)
    r = _run(nc, [arrays], core_ids=[0])
    return r.results[0]["out_x"]
```

```python
import math
from contextlib import ExitStack, contextmanager

import concourse.bass as bass
from concourse import mybir

F32 = mybir.dt.float32
I32 = mybir.dt.int32
ALU = mybir.AluOpType
ACT = mybir.ActivationFunctionType
AXX = mybir.AxisListType.X

P = 128
N, D = 3125, 160
S0, V0, VD = 64, 32, 96
E = 100000
NT = (N + P - 1) // P
TAIL = N - (NT - 1) * P
EP, EC = 125, 800
JB = 4
GE = JB * P
NI = (E + NT * (GE - 1)) // GE
SL = 4
NJ = NI // SL
assert NI % SL == 0 and EP * EC == E
NIP = 2 * P
GT = 2
GN = GT * P
NG = (NT + GT - 1) // GT
NXB = 10
NTP = GT * NG
TW = 192
UP, VP = 8, 16
EPS = 1e-5
GC = 8
K3 = 1.0 / math.sqrt(3.0)


class Count:

    def __init__(self, eng, name, start):
        self.eng, self.reg = eng, eng.alloc_register(name)
        eng.reg_mov(self.reg, start)

    def up(self, by):
        self.eng.reg_add(self.reg, self.reg, by)


class Net:

    def __init__(self, nc, ctx):
        self.nc, self.ctx = nc, ctx

    def sb(self, name, shape, dt=F32, ctx=None):
        return (ctx or self.ctx).enter_context(self.nc.sbuf_tensor(name, shape, dt))

    def ps(self, name, shape, ctx):
        return ctx.enter_context(self.nc.psum_tensor(name, shape, F32))

    def sem(self, name, ctx):
        self.stage_sems.append(self.nc.alloc_semaphore(name=name))
        return self.stage_sems[-1]

    @contextmanager
    def stage(self):
        self.stage_sems = []
        with ExitStack() as c:
            yield c
        self.nc.clear_and_free_semaphores(self.stage_sems)
        self.nc.all_engine_barrier()

    def dram(self, name, shape, dt=F32):
        return self.nc.dram_tensor(name, shape, dt, kind="Internal").ap()


def constants(net):
    nc = net.nc
    net.ident = net.sb("ident", [P, P])
    net.ramp = net.sb("ramp", [P, P])
    net.part = net.sb("part", [P, 1])
    net.eps = net.sb("eps", [P, 1])
    net.merge = net.sb("merge", [P, S0])
    net.sel_u = net.sb("sel_u", [P, P // UP, P])
    net.sel_v = net.sb("sel_v", [P, P // VP, P])
    with net.stage() as c:
        ramp_i = net.sb("ramp_i", [P, P], I32, c)
        part_i = net.sb("part_i", [P, 1], I32, c)
        uv_i = net.sb("uv_i", [P, 2, P], I32, c)
        uv_f = net.sb("uv_f", [P, 2, P], F32, c)
        pad = net.sb("pad", [P, GE // P * 22], F32, c)
        uv_split = net.sem("uv_split", c)
        ramps_made = net.sem("ramps_made", c)
        floats_made = net.sem("floats_made", c)
        ident_made = net.sem("ident_made", c)
        pad_zero = net.sem("pad_zero", c)
        pad_keys = net.sem("pad_keys", c)
        pads_stored = net.sem("pads_stored", c)
        block = c.enter_context(nc.Block())

        @block.gpsimd
        def _(pool):
            pool.iota(ramp_i[:, :], pattern=[[1, P]], base=0, channel_multiplier=0)
            pool.iota(part_i[:, :], pattern=[[0, 1]], base=0, channel_multiplier=1).then_inc(ramps_made, 1)

        @block.vector
        def _(dve):
            dve.memset(net.eps[:, :], EPS)
            dve.memset(pad[:, :], 0.0).then_inc(pad_zero, 1)
            dve.wait_ge(pad_zero, 1)
            dve.memset(pad[:, :].rearrange("p (j w) -> p j w", w=22)[:, :, 0:1], -1.0).then_inc(pad_keys, 1)
            dve.wait_ge(ramps_made, 1)
            dve.tensor_copy(net.ramp[:, :], ramp_i[:, :])
            dve.tensor_copy(net.part[:, :], part_i[:, :])
            dve.tensor_scalar(uv_i[:, 0, :], ramp_i[:, :], int(math.log2(VP)), None, ALU.logical_shift_right)
            dve.tensor_scalar(uv_i[:, 1, :], ramp_i[:, :], VP - 1, None, ALU.bitwise_and).then_inc(uv_split, 1)
            dve.wait_ge(uv_split, 1)
            dve.tensor_copy(uv_f[:, :, :], uv_i[:, :, :]).then_inc(floats_made, 1)
            dve.wait_ge(floats_made, 1)
            dve.tensor_scalar(net.ident[:, :], net.ramp[:, :], net.part[:, 0:1], None, ALU.is_equal)\
                .then_inc(ident_made, 1)
            for b in range(P // UP):
                dve.tensor_scalar(net.sel_u[:, b, :], uv_f[:, 0, :], float(UP * b), net.part[:, 0:1],
                                  ALU.add, ALU.is_equal)
            for b in range(P // VP):
                dve.tensor_scalar(net.sel_v[:, b, :], uv_f[:, 1, :], float(VP * b), net.part[:, 0:1],
                                  ALU.add, ALU.is_equal)
            dve.wait_ge(ident_made, 1)
            for h in range(2):
                half = slice(h * S0, (h + 1) * S0)
                dve.tensor_copy(net.merge[half, :], net.ident[half, half])

        @block.sync
        def _(sp):
            sp.wait_ge(pad_keys, 1)
            pv = pad[:, :].rearrange("p (j w) -> p j w", w=22)
            for rec, w in net.pads:
                sp.dma_start(rec[E:E + GE, :].rearrange("(p j) w -> p j w", j=GE // P),
                             pv[:, :, 0:w]).then_inc(pads_stored, 16)
            sp.wait_ge(pads_stored, 16 * len(net.pads))


def prepare_edges(net, ins, rec_src, rec_dst, by_src, by_dst, layers, fills):
    nc = net.nc
    W = {"src": 6, "dst": 22}
    PC = 50
    NQ = EC // PC
    rec_raw = net.dram("rec_raw", [E, W["dst"]])
    with ExitStack() as kept:
        pos = {t: net.sb(f"{t}_pos", [EP, EC], F32, kept) for t in W}
        moved_i = net.sb("moved_i", [1, 1], I32, kept)
        with net.stage() as c:
            below = net.sb("below", [P, P], F32, c)
            ones = net.sb("ones", [P, P], F32, c)
            step_i = net.sb("step_i", [P, 2], I32, c)
            step_no = net.sb("step_no", [P, 2], F32, c)
            key_i = {t: net.sb(f"{t}_key_i", [EP, EC], I32, c) for t in W}
            place_i = net.sb("place_i", [EP, EC], I32, c)
            bin_i = net.sb("bin_i", [EP, EC], I32, c)
            bin_f = net.sb("bin_f", [EP, EC], F32, c)
            mask = net.sb("mask", [EP, 2, EC], I32, c)
            rank = net.sb("rank", [EP, 2, EC], F32, c)
            a4 = net.sb("a4", [EP, EC, 4], F32, c)
            a16 = net.sb("a16", [EP, 2, PC, 16], F32, c)
            recs = net.sb("src_recs", [EP, EC, W["src"]], F32, c)
            piece = net.sb("dst_piece", [EP, 2, PC, W["dst"]], F32, c)
            stage_rec = net.sb("stage_rec", [EP, 2, GC, W["src"]], F32, c)
            stage_pos = net.sb("stage_pos", [EP, 2, GC], I32, c)
            moved = net.sb("moved", [EP, 1], F32, c)
            m = {}
            for t in W:
                m[t] = {n: net.sb(f"{t}_{n}", [P, w], dt, c) for n, w, dt in (
                    ("count", NT, F32), ("first", NT, F32), ("total", NT, F32), ("t_end", NT, F32),
                    ("steps_f", NT, F32), ("steps_i", 2 * NT, I32), ("s_first", NT + 1, F32),
                    ("e_first", NT + 1, F32), ("shift", NT + 1, F32), ("dshift", NT + 1, F32),
                    ("junk", 4 * (NT + 1), F32), ("sums", 2, F32), ("step_e", 2, F32), ("step_ei", 2, I32),
                    ("step_t", 2, F32), ("step_ti", 2, I32), ("step_b", 2, F32))}
                m[t]["dram"] = [net.dram(f"{t}_steps{n}", [NIP], dt) for n, dt in enumerate((I32, I32, F32))]
            counts_ps = {t: [net.ps(f"{t}_counts_ps{n}", [P, 512], c) for n in range(2)] for t in W}
            moved_ps = net.ps("moved_ps", [P, 512], c)

            keys_loaded = {t: net.sem(f"{t}_keys_loaded", c) for t in W}
            a4_loaded = net.sem("a4_loaded", c)
            a16_loaded = [net.sem(f"a16_loaded{s}", c) for s in range(2)]
            ramps_made = net.sem("prep_ramps_made", c)
            dve_step = net.sem("prep_dve_step", c)
            counted = net.sem("counted", c)
            summed = net.sem("summed", c)
            sched_made = net.sem("sched_made", c)
            sched_stored = net.sem("sched_stored", c)
            sched_loaded = net.sem("sched_loaded", c)
            placed = net.sem("placed", c)
            recs_made = net.sem("recs_made", c)
            staged = net.sem("staged", c)
            scattered = [net.sem(f"scattered{s}", c) for s in range(2)]
            piece_made = net.sem("piece_made", c)
            piece_stored = [net.sem(f"piece_stored{s}", c) for s in range(2)]
            moved_counted = net.sem("moved_counted", c)
            moved_summed = net.sem("moved_summed", c)
            weights_loaded = net.sem("weights_loaded", c)
            scaled = net.sem("weights_scaled", c)
            block = c.enter_context(nc.Block())

            @block.sync
            def _(sp):
                def load_piece(q):
                    if q >= 2:
                        sp.wait_ge(piece_made, q - 1)
                    sp.dma_start(a16[:, q % 2, :, :],
                                 ins["edge_attr_16"].rearrange("(p c) k -> p c k", p=EP)[:, q * PC:(q + 1) * PC, :])\
                        .then_inc(a16_loaded[q % 2], 16)

                def schedule(t, sched, n):
                    s = m[t]
                    sp.wait_ge(sched_made, n)
                    for d, name in zip(s["dram"], ("step_ei", "step_ti", "step_b")):
                        sp.dma_start(d.rearrange("(h p o) -> p h o", p=P, o=1),
                                     s[name][:, :].rearrange("p (h o) -> p h o", o=1)).then_inc(sched_stored, 16)
                    sp.wait_ge(sched_stored, 48 * n)
                    row = [d.rearrange("(o n) -> o n", o=1) for d in s["dram"]]
                    sp.dma_start(sched[0][:, :], row[0]).then_inc(sched_loaded, 16)
                    sp.dma_start(sched[1][:, :], row[1]).then_inc(sched_loaded, 16)
                    sp.dma_start(sched[2][:, :], row[2].broadcast_to([P, NIP])).then_inc(sched_loaded, 16)

                for t in W:
                    sp.dma_start(key_i[t][:, :], ins[t].rearrange("(p c) -> p c", p=EP)).then_inc(keys_loaded[t], 16)
                sp.dma_start(a4[:, :, :], ins["edge_attr_4"].rearrange("(p c) k -> p c k", p=EP)).then_inc(a4_loaded, 16)
                load_piece(0)
                load_piece(1)
                n = 0
                for lay in layers:
                    for tile, w in lay["chunks"].values():
                        u = w.shape[0]
                        for ui in range(UP):
                            src = w.rearrange("(a b) (c d) w -> b d a c w", b=UP, d=VP)[ui]
                            for a in range(u // UP):
                                sp.dma_start(tile[ui * VP:(ui + 1) * VP, a, :, :], src[:, a])\
                                    .then_inc(weights_loaded, 16)
                                n += 1
                    for dst, src in lay["plain"]:
                        sp.dma_start(dst, src).then_inc(weights_loaded, 16)
                        n += 1
                schedule("src", by_src, 1)
                raw, by_place = (r[0:E, :].rearrange("(p c) w -> p c w", p=EP) for r in (rec_raw, rec_dst))
                for q in range(NQ):
                    sp.wait_ge(piece_made, q + 1)
                    for to in (raw, by_place):
                        sp.dma_start(to[:, q * PC:(q + 1) * PC, :], piece[:, q % 2, :, :])\
                            .then_inc(piece_stored[q % 2], 16)
                    if q + 2 < NQ:
                        load_piece(q + 2)
                schedule("dst", by_dst, 2)
                sp.wait_ge(sched_loaded, 96)
                for s in range(2):
                    sp.wait_ge(piece_stored[s], 32 * NQ // 2)
                sp.wait_ge(weights_loaded, 16 * n)

            n_weights = sum(UP * (w.shape[0] // UP) for lay in layers for _, w in lay["chunks"].values()) \
                + sum(len(lay["plain"]) for lay in layers)

            @block.scalar
            def _(act):
                act.wait_ge(keys_loaded["src"], 16)
                act.activation(recs[:, :, 0], key_i["src"][:, :], ACT.Copy)
                act.wait_ge(keys_loaded["dst"], 16)
                act.activation(recs[:, :, 1], key_i["dst"][:, :], ACT.Copy)
                act.wait_ge(a4_loaded, 16)
                act.activation(recs[:, :, 2:6], a4[:, :, :], ACT.Copy).then_inc(recs_made, 1)
                act.wait_ge(recs_made, 1)
                act.wait_ge(placed, 1)

                def stage(j, s, free):
                    if free is not None:
                        act.wait_ge(scattered[s], free)
                    col = (2 * j + s) * GC
                    act.activation(stage_pos[:, s, :], pos["src"][:, bass.ds(col, GC)], ACT.Copy)
                    act.activation(stage_rec[:, s, :, :], recs[:, bass.ds(col, GC), :], ACT.Copy).then_inc(staged, 1)

                for s in range(2):
                    stage(0, s, None)
                with act.Fori(1, EC // GC // 2) as j:
                    for s in range(2):
                        stage(j, s, 16 * GC * j)

            @block.tensor
            def _(pe):
                for n, t in enumerate(W):
                    pe.wait_ge(counted, n + 1)
                    count = m[t]["count"][0:EP, :]
                    pe.matmul(counts_ps[t][0][0:EP, 0:NT], below[0:EP, 0:EP], count, start=True, stop=True)
                    pe.matmul(counts_ps[t][1][:, 0:NT], ones[0:EP, :], count, start=True, stop=True).then_inc(summed, 1)
                pe.wait_ge(moved_counted, 1)
                pe.matmul(moved_ps[:, 0:1], ones[0:EP, :], moved[:, :], start=True, stop=True).then_inc(moved_summed, 1)

            @block.gpsimd
            def _(pool):
                pool.iota(step_i[:, :], pattern=[[P, 2]], base=0, channel_multiplier=1)
                pool.iota(place_i[:, :], pattern=[[1, EC]], base=0, channel_multiplier=EC).then_inc(ramps_made, 1)
                scatter_columns(pool, "src", rec_src, stage_pos, stage_rec, staged, scattered)

            @block.vector
            def _(dve):
                done = [0]

                def step(ins):
                    done[0] += 1
                    ins.then_inc(dve_step, 1)
                    dve.wait_ge(dve_step, done[0])

                def places(t, n):
                    s = {k: v[:, :] for k, v in m[t].items() if k != "dram"}
                    steps_i = s["steps_i"].rearrange("p (a n) -> p a n", a=2)
                    junk = s["junk"].rearrange("p (h a n) -> p h a n", h=2, a=2)
                    dve.wait_ge(keys_loaded[t], 16)
                    step(dve.tensor_scalar(bin_i[:, :], key_i[t][:, :], int(math.log2(P)), None, ALU.logical_shift_right))
                    step(dve.tensor_copy(bin_f[:, :], bin_i[:, :]))
                    for k in range(NT):
                        step(dve.tensor_scalar(rank[:, k % 2, :], bin_f[:, :], float(k), 0.0, ALU.is_equal, ALU.add,
                                               accum_out=s["count"][0:EP, k:k + 1]))
                    dve.sem_inc(counted, 1)
                    dve.wait_ge(summed, n)
                    step(dve.tensor_copy(s["total"], counts_ps[t][1][:, 0:NT]))
                    step(dve.tensor_tensor_scan(s["t_end"], s["total"], s["total"], 0.0, ALU.add, ALU.max))
                    dve.memset(s["e_first"][:, 0:1], 0.0)
                    step(dve.tensor_copy(s["e_first"][:, 1:NT + 1], s["t_end"]))
                    step(dve.tensor_tensor(s["first"][0:EP, :], counts_ps[t][0][0:EP, 0:NT], s["e_first"][0:EP, 0:NT],
                                           ALU.add))
                    for k in range(NT):
                        h = k % 2
                        step(dve.tensor_scalar(mask[:, h, :], bin_f[:, :], float(k), None, ALU.is_equal))
                        step(dve.tensor_tensor_scan(rank[:, h, :], mask[:, h, :], mask[:, h, :],
                                                    s["first"][0:EP, k:k + 1], ALU.add, ALU.max))
                        step(dve.copy_predicated(pos[t][:, :], mask[:, h, :], rank[:, h, :]))
                    step(dve.tensor_scalar(pos[t][:, :], pos[t][:, :], -1.0, None, ALU.add))
                    dve.sem_inc(placed, 1)
                    step(dve.tensor_scalar(steps_i[:, 0, :], s["total"], float(GE - 1), None, ALU.add))
                    step(dve.tensor_scalar(steps_i[:, 1, :], steps_i[:, 0, :], int(math.log2(GE)), None,
                                           ALU.logical_shift_right))
                    step(dve.tensor_copy(s["steps_f"], steps_i[:, 1, :]))
                    dve.memset(s["s_first"][:, 0:1], 0.0)
                    step(dve.tensor_tensor_scan(s["s_first"][:, 1:NT + 1], s["steps_f"], s["steps_f"], 0.0,
                                                ALU.add, ALU.max))
                    step(dve.scalar_tensor_tensor(s["shift"], s["s_first"], -float(GE), s["e_first"], ALU.mult, ALU.add))
                    dve.memset(s["dshift"][:, 0:1], 0.0)
                    step(dve.tensor_tensor(s["dshift"][:, 1:NT + 1], s["shift"][:, 1:NT + 1], s["shift"][:, 0:NT],
                                           ALU.subtract))
                    for h in range(2):
                        dve.tensor_scalar(junk[:, h, 0, :], s["s_first"], step_no[:, h:h + 1], -1.0, ALU.is_le, ALU.add,
                                          accum_out=s["step_t"][:, h:h + 1])
                        step(dve.scalar_tensor_tensor(junk[:, h, 1, :], s["s_first"], step_no[:, h:h + 1], s["dshift"],
                                                      ALU.is_le, ALU.mult, accum_out=s["sums"][:, h:h + 1]))
                    step(dve.scalar_tensor_tensor(s["step_e"], step_no[:, :], float(GE), s["sums"], ALU.mult, ALU.add))
                    dve.tensor_scalar(s["step_ei"], s["step_e"], float(E), None, ALU.min)
                    dve.tensor_copy(s["step_ti"], s["step_t"])
                    dve.tensor_scalar(s["step_b"], s["step_t"], float(P), None, ALU.mult).then_inc(sched_made, 1)

                dve.memset(ones[:, :], 1.0)
                dve.wait_ge(ramps_made, 1)
                dve.tensor_copy(step_no[:, :], step_i[:, :])
                step(dve.tensor_scalar(below[:, :], net.ramp[:, :], net.part[:, 0:1], None, ALU.is_gt))
                places("src", 1)
                places("dst", 2)
                step(dve.tensor_copy(bin_f[:, :], place_i[:, :]))
                step(dve.tensor_tensor(rank[:, 0, :], bin_f[:, :], pos["dst"][:, :], ALU.not_equal))
                dve.tensor_reduce(moved[:, :], rank[:, 0, :], AXX, ALU.add).then_inc(moved_counted, 1)
                dve.wait_ge(a4_loaded, 16)
                for q in range(NQ):
                    cols = slice(q * PC, (q + 1) * PC)
                    to = piece[:, q % 2, :, :]
                    if q >= 2:
                        dve.wait_ge(piece_stored[q % 2], 32 * (q // 2))
                    dve.tensor_copy(to[:, :, 0], key_i["dst"][:, cols])
                    dve.tensor_copy(to[:, :, 1], key_i["src"][:, cols])
                    dve.tensor_copy(to[:, :, 2:6], a4[:, cols, :])
                    dve.wait_ge(a16_loaded[q % 2], 16 * (q // 2 + 1))
                    dve.tensor_copy(to[:, :, 6:22], a16[:, q % 2, :, :]).then_inc(piece_made, 1)
                dve.wait_ge(moved_summed, 1)
                dve.tensor_copy(moved_i[:, :], moved_ps[0:1, 0:1])
                dve.wait_ge(weights_loaded, 16 * n_weights)
                for lay in layers:
                    for ap, factor in lay["scales"]:
                        last = dve.tensor_scalar(ap, ap, factor, None, ALU.mult)
                last.then_inc(scaled, 1)
                dve.wait_ge(scaled, 1)
                for to, frm in fills:
                    dve.tensor_copy(to, frm)

        with net.stage() as c:
            raw_rec = net.sb("raw_rec", [EP, 2, GC, W["dst"]], F32, c)
            raw_pos = net.sb("raw_pos", [EP, 2, GC], I32, c)
            raw_loaded = [net.sem(f"raw_loaded{s}", c) for s in range(2)]
            pos_ready = net.sem("pos_ready", c)
            moves = [net.sem(f"moves{s}", c) for s in range(2)]
            block = c.enter_context(nc.Block())

            def if_moved(eng, then):
                with eng.If(eng.value_load(moved_i[0:1, 0:1], min_val=0, max_val=E) != 0):
                    then()

            @block.sync
            def _(sp):
                raw = rec_raw.rearrange("(p c) w -> p c w", p=EP)

                def load(j, s, free):
                    if free is not None:
                        sp.wait_ge(moves[s], free)
                    sp.dma_start(raw_rec[:, s, :, :], raw[:, bass.ds((2 * j + s) * GC, GC), :])\
                        .then_inc(raw_loaded[s], 16)

                def loads():
                    for s in range(2):
                        load(0, s, None)
                    with sp.Fori(1, EC // GC // 2) as j:
                        for s in range(2):
                            load(j, s, 16 * GC * j)
                if_moved(sp, loads)

            @block.scalar
            def _(act):
                def place(j, s, free):
                    if free is not None:
                        act.wait_ge(moves[s], free)
                    act.wait_ge(raw_loaded[s], 16 * j + 16)
                    act.activation(raw_pos[:, s, :], pos["dst"][:, bass.ds((2 * j + s) * GC, GC)], ACT.Copy)\
                        .then_inc(pos_ready, 1)

                def all_places():
                    for s in range(2):
                        place(0, s, None)
                    with act.Fori(1, EC // GC // 2) as j:
                        for s in range(2):
                            place(j, s, 16 * GC * j)
                if_moved(act, all_places)

            @block.gpsimd
            def _(pool):
                if_moved(pool, lambda: scatter_columns(pool, "dst", rec_dst, raw_pos, raw_rec, pos_ready, moves))


def scatter_columns(pool, tag, rec, places, recs, ready, scattered):
    turn = Count(pool, f"{tag}_turn", 0)
    with pool.Fori(0, EC // GC // 2):
        for s in range(2):
            turn.up(1)
            pool.wait_ge(ready, 1)
            pool.wait_ge(ready, turn.reg)
            for q in range(GC):
                pool.indirect_dma_start(rec, bass.IndirectOffsetOnAxis(ap=places[:, s, q:q + 1], axis=0),
                                        recs[:, s, q, :], None).then_inc(scattered[s], 16)
    for s in range(2):
        pool.wait_ge(scattered[s], 16 * EC // 2)



def edge_loop(net, tag, kind, rec, sched, table, acc, C):
    nc = net.nc
    W = rec.shape[1]
    erow, trow, tbase = sched
    MC = {"plain": C - D, "conv": C, "cross": C}[kind]
    dist, vec = {"plain": (5, 2), "conv": (2, 3), "cross": (2, 3)}[kind]
    with net.stage() as c:
        recs = net.sb(f"{tag}_recs", [P, SL, JB, W], F32, c)
        far = net.sb(f"{tag}_far", [P, SL, JB], I32, c)
        rows = net.sb(f"{tag}_rows", [P, SL, JB, TW], F32, c)
        rel = net.sb(f"{tag}_rel", [P, 2, JB], F32, c)
        hot = net.sb(f"{tag}_hot", [P, 2, JB, P], F32, c)
        msg = net.sb(f"{tag}_msg", [P, 2, JB, MC], F32, c)
        prod = net.sb(f"{tag}_prod", [P, 3, JB, VD], F32, c)
        agg_ps = [net.ps(f"{tag}_agg_ps{s}", [P, 512], c) for s in range(2)]
        if kind == "conv":
            scaled = net.sb(f"{tag}_scaled", [P, 2, JB, D], F32, c)
            w0f = net.sb(f"{tag}_w0f", [P, JB, S0], F32, c)
            dot = net.sb(f"{tag}_dot", [P, JB, V0], F32, c)
            recT = net.sb(f"{tag}_recT", [JB * W, 2, P], F32, c)
            hidT = net.sb(f"{tag}_hidT", [2 * S0, 2, JB // 2, P], F32, c)
            recT_ps = net.ps(f"{tag}_recT_ps", [JB * W, P], c)
            hid_ps = net.ps(f"{tag}_hid_ps", [2 * S0, JB // 2, P], c)
            w_ps = [net.ps(f"{tag}_w_ps{s}", [P, 2, 2, 256], c) for s in range(2)]

        acc_zero = net.sem(f"{tag}_acc_zero", c)
        rec_loaded = [net.sem(f"{tag}_rec_loaded{s}", c) for s in range(SL)]
        far_ready = net.sem(f"{tag}_far_ready", c)
        gathered = [net.sem(f"{tag}_gathered{s}", c) for s in range(SL)]
        rel_ready = net.sem(f"{tag}_rel_ready", c)
        hot_ready = net.sem(f"{tag}_hot_ready", c)
        prod_ready = net.sem(f"{tag}_prod_ready", c)
        act_msgs = net.sem(f"{tag}_act_msgs", c)
        dve_msgs = net.sem(f"{tag}_dve_msgs", c)
        agg_done = net.sem(f"{tag}_agg_done", c)
        acc_added = net.sem(f"{tag}_acc_added", c)
        if kind == "conv":
            recT_done = net.sem(f"{tag}_recT_done", c)
            recT_ready = net.sem(f"{tag}_recT_ready", c)
            hid_done = net.sem(f"{tag}_hid_done", c)
            hid_ready = net.sem(f"{tag}_hid_ready", c)
            w_done = net.sem(f"{tag}_w_done", c)
            w_used = net.sem(f"{tag}_w_used", c)
        block = c.enter_context(nc.Block())

        def steps(eng, body):
            for u in range(SL):
                body(0, u)
            with eng.Fori(1, NJ - 1) as j:
                for u in range(SL):
                    body(j, u)
            for u in range(SL):
                body(NJ - 1, u)

        def has(j, u, d):
            return not isinstance(j, int) or 0 <= SL * j + u + d < NI

        @block.sync
        def _(sp):
            def load(j, u):
                i = SL * j + u
                if has(j, u, -SL):
                    sp.wait_ge(agg_done, i - SL + 1)
                e = sp.value_load(erow[0:1, bass.ds(i, 1)], min_val=0, max_val=E)
                sp.dma_start(recs[:, u, :, :], rec[bass.ds(e, GE), :].rearrange("(p j) w -> p j w", j=JB))\
                    .then_inc(rec_loaded[u], 16)
            steps(sp, load)

        @block.gpsimd
        def _(pool):
            this, past = Count(pool, f"{tag}_this", 0), Count(pool, f"{tag}_past", 0)

            def gather(j, u):
                i = SL * j + u
                this.up(1)
                if has(j, u, -SL):
                    past.up(1)
                pool.wait_ge(far_ready, 1)
                pool.wait_ge(far_ready, this.reg)
                if has(j, u, -SL):
                    pool.wait_ge(agg_done, past.reg)
                for q in range(JB):
                    pool.indirect_dma_start(rows[:, u, q, :], None, table[0:NT * P, :],
                                            bass.IndirectOffsetOnAxis(ap=far[:, u, q:q + 1], axis=0))\
                        .then_inc(gathered[u], 16)
            steps(pool, gather)

        @block.scalar
        def _(act):
            AHEAD = 2

            def convert(j, u):
                act.wait_ge(rec_loaded[u], 16 * j + 16)
                act.activation(far[:, u, :], recs[:, u, :, 1], ACT.Copy).then_inc(far_ready, 1)

            def attributes(j, u):
                i = SL * j + u
                act.wait_ge(recT_done, i + 1)
                if has(j, u, -2):
                    act.wait_ge(hid_done, i - 1)
                act.activation(recT[:, u % 2, :], recT_ps[:, :], ACT.Copy).then_inc(recT_ready, 1)

            def hidden(j, u):
                i = SL * j + u
                act.wait_ge(hid_done, i + 1)
                if has(j, u, -2):
                    act.wait_ge(w_done, i - 1)
                act.activation(hidT[:, u % 2, :, :], hid_ps[:, :, :], ACT.Silu).then_inc(hid_ready, 1)

            def scale_rows(j, u):
                i = SL * j + u
                act.wait_ge(gathered[u], 64 * j + 64)
                if has(j, u, -2):
                    act.wait_ge(dve_msgs if kind == "conv" else agg_done, i - 1)
                for q in range(JB):
                    by = recs[:, u, q, dist:dist + 1]
                    if kind == "plain":
                        last = act.activation(msg[:, u % 2, q, 0:D], rows[:, u, q, 0:D], ACT.Copy, scale=by)
                    elif kind == "conv":
                        last = act.activation(scaled[:, u % 2, q, :], rows[:, u, q, 0:D], ACT.Copy, scale=by)
                    else:
                        act.activation(msg[:, u % 2, q, 0:S0], rows[:, u, q, 0:S0], ACT.Copy, scale=by)
                        last = act.activation(
                            msg[:, u % 2, q, VD:4 * VD].rearrange("p (k f) -> p k f", k=3)[:, :, 0:V0],
                            rows[:, u, q, S0:D].rearrange("p (f k) -> p k f", k=3), ACT.Copy, scale=by)
                last.then_inc(act_msgs, 1)

            for u in range(AHEAD):
                convert(0, u)
            if kind == "conv":
                for u in range(AHEAD):
                    attributes(0, u)
                    hidden(0, u)
                scale_rows(0, 0)

            def body(j, u):
                ahead = (j + (u + AHEAD) // SL, (u + AHEAD) % SL)
                coming = has(j, u, AHEAD)
                if coming:
                    convert(*ahead)
                if kind == "conv":
                    if has(j, u, 1):
                        scale_rows(j + (u + 1) // SL, (u + 1) % SL)
                    if coming:
                        attributes(*ahead)
                        hidden(*ahead)
                else:
                    scale_rows(j, u)
            steps(act, body)

        @block.vector
        def _(dve):
            dve.memset(acc[:, :, :], 0.0).then_inc(acc_zero, 1)
            if kind == "conv":
                dve.memset(msg[:, :, :, 4 * VD:C], 1.0)
            dve.wait_ge(acc_zero, 1)

            def add_up(j, u):
                i = SL * j + u
                t = dve.value_load(trow[0:1, bass.ds(i, 1)], min_val=0, max_val=NT)
                dve.wait_ge(agg_done, i + 1)
                if has(j, u, -1):
                    dve.wait_ge(acc_added, i)
                to = acc[:, bass.ds(t, 1), :].rearrange("p a b -> p (a b)")[:, 0:C]
                dve.tensor_tensor(to, to, agg_ps[u % 2][:, 0:C], ALU.add).then_inc(acc_added, 1)

            def body(j, u):
                i, m = SL * j + u, u % 2
                dve.wait_ge(rec_loaded[u], 16 * j + 16)
                dve.tensor_scalar(rel[:, m, :], recs[:, u, :, 0], tbase[:, bass.ds(i, 1)], None, ALU.subtract)\
                    .then_inc(rel_ready, 1)
                if has(j, u, -2):
                    dve.wait_ge(agg_done, i - 1)
                dve.wait_ge(rel_ready, i + 1)
                dve.tensor_tensor(hot[:, m, :, :], net.ramp[:, :].unsqueeze(1).broadcast_to([P, JB, P]),
                                  rel[:, m, :].unsqueeze(2).broadcast_to([P, JB, P]), ALU.is_equal)\
                    .then_inc(hot_ready, 1)
                dve.wait_ge(gathered[u], 64 * j + 64)
                r = rows[:, u, :, :]
                out = msg[:, m, :, :]
                e3 = recs[:, u, :, vec:vec + 3]
                v = r[:, :, S0:D].rearrange("p j (f k) -> p j f k", k=3)
                if kind == "plain":
                    pv = prod[:, 0, :, :].rearrange("p j (f k) -> p j f k", k=3)
                    dve.tensor_tensor(pv, v, e3.unsqueeze(2).broadcast_to([P, JB, V0, 3]), ALU.mult)\
                        .then_inc(prod_ready, 1)
                    dve.tensor_tensor(out[:, :, D + V0:D + V0 + VD].rearrange("p j (f k) -> p j f k", k=3),
                                      r[:, :, D:TW].unsqueeze(3).broadcast_to([P, JB, V0, 3]),
                                      e3.unsqueeze(2).broadcast_to([P, JB, V0, 3]), ALU.mult)
                    dve.wait_ge(prod_ready, i + 1)
                    dve.tensor_reduce(out[:, :, D:D + V0], pv, AXX, ALU.add).then_inc(dve_msgs, 1)
                elif kind == "cross":
                    vk = r[:, :, S0:D].rearrange("p j (f k) -> p j k f", k=3)
                    for b in range(3):
                        last = dve.tensor_tensor(prod[:, b, :, :].rearrange("p j (k f) -> p j k f", k=3), vk,
                                                 e3[:, :, b:b + 1].unsqueeze(3).broadcast_to([P, JB, 3, V0]), ALU.mult)
                    last.then_inc(prod_ready, 1)
                    o3 = out[:, :, VD:4 * VD].rearrange("p j (k f) -> p j k f", k=3)
                    dve.tensor_tensor(o3[:, :, :, V0:2 * V0], r[:, :, D:TW].unsqueeze(2).broadcast_to([P, JB, 3, V0]),
                                      e3.unsqueeze(3).broadcast_to([P, JB, 3, V0]), ALU.mult)

                    def p(a, b):
                        return prod[:, b, :, a * V0:(a + 1) * V0]
                    dve.wait_ge(prod_ready, 2 * i + 1)
                    dve.tensor_tensor(out[:, :, S0:VD], p(0, 0), p(1, 1), ALU.add).then_inc(prod_ready, 1)
                    for k in range(3):
                        a, b = (k + 1) % 3, (k + 2) % 3
                        dve.tensor_tensor(o3[:, :, k, 2 * V0:3 * V0], p(a, b), p(b, a), ALU.subtract)
                    dve.wait_ge(prod_ready, 2 * i + 2)
                    dve.tensor_tensor(out[:, :, S0:VD], out[:, :, S0:VD], p(2, 2), ALU.add).then_inc(dve_msgs, 1)
                else:
                    wv = w_ps[m][:, :, :, :].rearrange("p a b w -> p (a b) w")
                    pv = prod[:, 0, :, :].rearrange("p j (f k) -> p j f k", k=3)
                    dve.tensor_tensor(pv, v, e3.unsqueeze(2).broadcast_to([P, JB, V0, 3]), ALU.mult)\
                        .then_inc(prod_ready, 1)
                    dve.wait_ge(w_done, i + 1)
                    dve.tensor_tensor(w0f[:, :, :], wv[:, :, S0:2 * S0], r[:, :, 0:S0], ALU.mult)
                    dve.wait_ge(prod_ready, 3 * i + 1)
                    dve.tensor_reduce(dot[:, :, :], pv, AXX, ALU.add).then_inc(prod_ready, 1)
                    dve.wait_ge(act_msgs, i + 1)
                    sc = scaled[:, m, :, :]
                    dve.tensor_tensor(out[:, :, 0:S0], wv[:, :, 0:S0], sc[:, :, 0:S0], ALU.mult)
                    o3 = out[:, :, VD:4 * VD].rearrange("p j (k f) -> p j k f", k=3)
                    dve.tensor_tensor(o3[:, :, :, S0:VD], wv[:, :, 2 * S0:2 * S0 + V0].unsqueeze(2).broadcast_to([P, JB, 3, V0]),
                                      sc[:, :, S0:D].rearrange("p j (f k) -> p j k f", k=3), ALU.mult)
                    dve.wait_ge(prod_ready, 3 * i + 2)
                    dve.tensor_tensor(out[:, :, S0:VD], wv[:, :, 2 * S0 + V0:TW], dot[:, :, :], ALU.mult)\
                        .then_inc(prod_ready, 1)
                    dve.tensor_tensor(o3[:, :, :, 0:S0], w0f[:, :, :].unsqueeze(2).broadcast_to([P, JB, 3, S0]),
                                      e3.unsqueeze(3).broadcast_to([P, JB, 3, S0]), ALU.mult).then_inc(dve_msgs, 1)
                if has(j, u, -1):
                    add_up(j + (u - 1) // SL, (u - 1) % SL)
            steps(dve, body)
            add_up(NJ - 1, SL - 1)

        @block.tensor
        def _(pe):
            def attributes(j, u):
                i = SL * j + u
                pe.wait_ge(rec_loaded[u], 16 * j + 16)
                if has(j, u, -1):
                    pe.wait_ge(recT_ready, i)
                pe.transpose(recT_ps[:, :], recs[:, u, :, :].rearrange("p j w -> p (j w)"), net.ident[:, :])\
                    .then_inc(recT_done, 1)

            def hidden(j, u):
                i = SL * j + u
                pe.wait_ge(recT_ready, i + 1)
                if has(j, u, -1):
                    pe.wait_ge(hid_ready, i)
                for h in range(JB // 2):
                    last = pe.matmul(hid_ps[:, h, :], net.wfc1[:, h, :], recT[:, u % 2, :], start=True, stop=True)
                last.then_inc(hid_done, 1)

            def weights(j, u):
                i = SL * j + u
                pe.wait_ge(hid_ready, i + 1)
                if has(j, u, -2):
                    pe.wait_ge(dve_msgs, i - 1)
                for q in (0, 2, 1, 3):
                    half = slice(q // 2 * S0, (q // 2 + 1) * S0)
                    last = pe.matmul(w_ps[u % 2][:, q // 2, q % 2, 0:TW], hidT[half, u % 2, q % 2, :],
                                     net.wfc2[half, :], start=True, stop=True)
                last.then_inc(w_done, 1)

            if kind == "conv":
                for u in range(2):
                    attributes(0, u)
                    hidden(0, u)
                weights(0, 0)

            def body(j, u):
                i, m = SL * j + u, u % 2
                ahead = (j + (u + 2) // SL, (u + 2) % SL)
                if kind == "conv" and has(j, u, 1):
                    weights(j + (u + 1) // SL, (u + 1) % SL)
                if kind == "conv" and has(j, u, 2):
                    attributes(*ahead)
                pe.wait_ge(hot_ready, i + 1)
                if has(j, u, -2):
                    pe.wait_ge(acc_added, i - 1)
                if kind == "plain":
                    pe.wait_ge(gathered[u], 64 * j + 64)
                    for q in range(JB):
                        pe.matmul(agg_ps[m][:, 0:D], hot[:, m, q, :], rows[:, u, q, 0:D], start=(q == 0),
                                  stop=False, skip_group_check=True)
                        if q == 0:
                            pe.wait_ge(act_msgs, i + 1)
                            pe.wait_ge(dve_msgs, i + 1)
                        last = pe.matmul(agg_ps[m][:, D:C], hot[:, m, q, :], msg[:, m, q, :], start=False,
                                         stop=(q == JB - 1), skip_group_check=True)
                else:
                    pe.wait_ge(act_msgs, i + 1)
                    pe.wait_ge(dve_msgs, i + 1)
                    for q in range(JB):
                        last = pe.matmul(agg_ps[m][:, 0:C], hot[:, m, q, :], msg[:, m, q, 0:C], start=(q == 0),
                                         stop=(q == JB - 1))
                last.then_inc(agg_done, 1)
                if kind == "conv" and has(j, u, 2):
                    hidden(*ahead)
            steps(pe, body)



def outer_schedule(lay):
    w = {k: v[0] for k, v in lay["chunks"].items()}
    plan = []
    for b in range(NXB):
        if b < 4:
            first = [(2 * v + uu, w["ss"][:, 2 * b + uu, v, :], "ab"[uu]) for v in range(4) for uu in range(2)]
            second = [(4 * k + 2 * vi + uu, w["sv"][:, 2 * b + uu, vi, :], ("cd"[uu], k))
                      for vi in range(2) for uu in range(2) for k in range(3)]
        else:
            k, ub = (b - 4) // 2, 2 * ((b - 4) % 2)
            first = [(2 * v + uu, w["vs"][:, ub + uu, v, :], ("cd"[uu], k)) for v in range(4) for uu in range(2)]
            second = [(2 * vi + uu, w["vv"][:, ub + uu, vi, :], "ab"[uu]) for vi in range(2) for uu in range(2)]
        plan += [first, second]
    return plan


def outer_stage(net, tag, nxt, lay, prep, acc, C, table):
    nc = net.nc
    plan = outer_schedule(lay)
    NP_ = len(plan)
    with net.stage() as c:
        agg = net.sb(f"{tag}_agg", [P, GT, C], F32, c)
        xin = net.sb(f"{tag}_xin", [P, GT, D], F32, c)
        xnew = net.sb(f"{tag}_xnew", [P, 2, GT, D], F32, c)
        usum = net.sb(f"{tag}_usum", [P, 3, GN], F32, c)
        xa = net.sb(f"{tag}_xa", [P, 2, 3, GN], F32, c)
        arep = net.sb(f"{tag}_arep", [P, 2, NXB, GN], F32, c)
        even = net.sb(f"{tag}_even", [P, 2, 8, GN], F32, c)
        odd = net.sb(f"{tag}_odd", [P, 12, GN], F32, c)
        y = net.sb(f"{tag}_y", [P, GT, D], F32, c)
        stats = net.sb(f"{tag}_stats", [P, GT, 6], F32, c)
        mv = net.sb(f"{tag}_mv", [P, GT, 2], F32, c)
        sd = net.sb(f"{tag}_sd", [P, GT], F32, c)
        rstd = net.sb(f"{tag}_rstd", [P, GT], F32, c)
        nT = net.sb(f"{tag}_nT", [P, 4, GN], F32, c)
        trow = net.sb(f"{tag}_trow", [P, GT, TW], F32, c)
        aggT, vecT = nT[:, 0:2, :], usum[0:VD, :, :]
        t_ps, x_ps = net.ps(f"{tag}_t_ps", [P, 512], c), net.ps(f"{tag}_x_ps", [P, 512], c)
        v_ps = [net.ps(f"{tag}_v_ps{s}", [P, 512], c) for s in range(2)]
        rep_ps = [net.ps(f"{tag}_rep_ps{s}", [P, 2, GN], c) for s in range(2)]
        us_ps, uv_ps = net.ps(f"{tag}_us_ps", [P, 512], c), net.ps(f"{tag}_uv_ps", [P, 2, GN], c)
        next_ps = [x_ps, t_ps]

        loaded = net.sem(f"{tag}_loaded", c)
        zeroed = net.sem(f"{tag}_zeroed", c)
        transposed = net.sem(f"{tag}_transposed", c)
        opsT_ready = net.sem(f"{tag}_opsT_ready", c)
        lin_done = net.sem(f"{tag}_lin_done", c)
        a_ready = net.sem(f"{tag}_a_ready", c)
        arep_done = net.sem(f"{tag}_arep_done", c)
        arep_ready = net.sem(f"{tag}_arep_ready", c)
        xrep_done = net.sem(f"{tag}_xrep_done", c)
        prod_ready = net.sem(f"{tag}_prod_ready", c)
        prod_used = net.sem(f"{tag}_prod_used", c)
        usum_ready = net.sem(f"{tag}_usum_ready", c)
        nat_done = net.sem(f"{tag}_nat_done", c)
        y_ready = net.sem(f"{tag}_y_ready", c)
        stats_ready = net.sem(f"{tag}_stats_ready", c)
        var_ready = net.sem(f"{tag}_var_ready", c)
        sd_ready = net.sem(f"{tag}_sd_ready", c)
        rstd_ready = net.sem(f"{tag}_rstd_ready", c)
        x_new = net.sem(f"{tag}_x_new", c)
        new_transposed = net.sem(f"{tag}_new_transposed", c)
        nT_ready = net.sem(f"{tag}_nT_ready", c)
        next_done = net.sem(f"{tag}_next_done", c)
        row_ready = net.sem(f"{tag}_row_ready", c)
        base_ready = net.sem(f"{tag}_base_ready", c)
        stored = net.sem(f"{tag}_stored", c)
        block = c.enter_context(nc.Block())
        NJG = NG // 2
        assert NG % 2 == 1

        def groups(eng, body):
            body(0, 0)
            body(0, 1)
            with eng.Fori(1, NJG) as j:
                body(j, 0)
                body(j, 1)
            body(NJG, 0)

        def has(j, u, d):
            return not isinstance(j, int) or 0 <= 2 * j + u + d < NG

        def at(j, u, d):
            return j + (u + d) // 2, (u + d) % 2

        def v_of(ap):
            return ap.rearrange("p (f k) -> p k f", k=3)

        @block.sync
        def _(sp):
            def load(j, u):
                g = 2 * j + u
                if has(j, u, -1):
                    sp.wait_ge(transposed, g)
                sp.dma_start(xin[:, :, :], net.xres[:, bass.ds(GT * g, GT), :]).then_inc(loaded, 16)
                sp.dma_start(agg[:, :, :], acc[:, bass.ds(GT * g, GT), 0:C]).then_inc(loaded, 16)

            def store(j, u):
                g = 2 * j + u
                sp.wait_ge(row_ready, g + 1)
                sp.dma_start(table[bass.ds(g * GN, GN), :].rearrange("(h p) w -> p h w", p=P),
                             trow[:, :, :]).then_inc(stored, 16)

            load(0, 0)

            def body(j, u):
                if has(j, u, 1):
                    load(*at(j, u, 1))
                if has(j, u, -1):
                    store(*at(j, u, -1))
            groups(sp, body)
            store(NJG, 0)
            sp.wait_ge(stored, 16 * NG)

        @block.tensor
        def _(pe):
            def mm(to, lhsT, rhs, start=True, stop=True, **kw):
                return pe.matmul(to, lhsT, rhs, start=start, stop=stop, **kw)

            def front(j, u):
                g = 2 * j + u
                pe.wait_ge(loaded, 32 * g + 32)
                if has(j, u, -2):
                    pe.wait_ge(row_ready, g - 1)
                    if nxt == "conv":
                        pe.wait_ge(base_ready, g - 1)
                ident = net.ident[:, :]
                for h in range(GT):
                    n = slice(h * P, (h + 1) * P)
                    ag = agg[:, h, :]
                    for b in range(2):
                        mm(t_ps[S0 * b:S0 * (b + 1), n], ag[:, D * b:D * b + S0], ident)
                    pe.transpose(t_ps[0:V0, GN + h * P:GN + (h + 1) * P], ag[:, 2 * D:2 * D + V0], ident)
                    vecs = [ag[:, S0:D], ag[:, D + S0:2 * D], ag[:, 2 * D + V0:2 * D + V0 + VD]]
                    for b, ap in enumerate(vecs):
                        for k in range(3):
                            o = (k % 2) * GN + h * P
                            mm(v_ps[k // 2][V0 * b:V0 * (b + 1), o:o + P], v_of(ap)[:, k, :], ident)
                    xu = xin[:, h, :]
                    xv = v_of(xu[:, S0:D])
                    mm(x_ps[0:S0, n], xu[:, 0:S0], ident)
                    mm(x_ps[S0:S0 + V0, n], xv[:, 0, :], ident)
                    mm(x_ps[S0 + V0:P, n], xv[:, 1, :], ident)
                    last = pe.transpose(x_ps[0:V0, GN + h * P:GN + (h + 1) * P], xv[:, 2, :], ident)
                last.then_inc(transposed, 1)
                pe.wait_ge(opsT_ready, g + 1)
                mm(t_ps[0:S0, 0:GN], lay["m0"], aggT[:, 0, :], stop=False)
                mm(t_ps[0:S0, 0:GN], lay["mdot"], aggT[0:V0, 1, :], start=False)
                mm(t_ps[S0:S0 + V0, 0:GN], lay["m1"], vecT[:, 0, :])
                mm(t_ps[S0 + V0:P, 0:GN], lay["m1"], vecT[:, 1, :])
                mm(t_ps[V0:2 * V0, GN:2 * GN], lay["m1"], vecT[:, 2, :]).then_inc(lin_done, 1)

            def a_operands(j, u):
                g = 2 * j + u
                pe.wait_ge(a_ready, g + 1)
                for n in range(NXB // 2):
                    if n >= 2:
                        pe.wait_ge(arep_ready, NXB // 2 * g + n - 1)
                    for i in range(2):
                        m = 2 * n + i
                        part, sel = (1, m) if m < 8 else (2, m - 6)
                        last = mm(v_ps[n % 2][:, i * GN:(i + 1) * GN], net.sel_v[:, sel, :], xa[:, u, part, :])
                    last.then_inc(arep_done, 1)

            def x_operands(j, u, b):
                g = 2 * j + u
                if b >= 2 or has(j, u, -1):
                    pe.wait_ge(prod_ready, NP_ * g + 2 * b - 2)
                for i in range(2):
                    m = 2 * b + i
                    part, sel = (0, m) if m < 16 else (2, m - 16)
                    last = mm(rep_ps[b % 2][:, i, :], net.sel_u[:, sel, :], xa[:, u, part, :])
                last.then_inc(xrep_done, 1)

            where = {"a": (us_ps[0:S0, 0:GN], ("s", 0)), "b": (us_ps[S0:P, 0:GN], ("s", 1))}
            for k in range(3):
                where["c", k] = (uv_ps[V0 * k:V0 * (k + 1), 0, :], ("v", k))
                where["d", k] = (uv_ps[V0 * (k + 1):V0 * (k + 2), 1, :], ("v", k + 1))
            opened = {where[x][1] for x in ("a", ("c", 0), ("c", 1), ("c", 2))}
            firsts, lasts = {}, {}
            for n, chunks in enumerate(plan):
                for m, (_, _, region) in enumerate(chunks):
                    quarter = where[region][1]
                    if quarter not in opened:
                        firsts.setdefault(quarter, (n, m))
                    lasts[quarter] = (n, m)

            def sum_up(j, u, b):
                g = 2 * j + u
                kw = {"skip_group_check": True}
                if b == 0:
                    if has(j, u, -1):
                        pe.wait_ge(usum_ready, g)
                    mm(where["a"][0], lay["l0"], xa[:, u, 0, :], stop=False, **kw)
                    for k in range(3):
                        mm(where["c", k][0], lay["l1"][:, k, :], xa[:, u, 2 if k == 2 else 0, :], stop=False, **kw)
                for part in range(2):
                    n = 2 * b + part
                    pe.wait_ge(prod_ready, NP_ * g + n + 1)
                    for m, (chunk, w, region) in enumerate(plan[n]):
                        to, quarter = where[region]
                        last = mm(to, w, (odd[:, chunk, :] if part else even[:, b % 2, chunk, :]),
                                  start=firsts.get(quarter) == (n, m), stop=lasts[quarter] == (n, m), **kw)
                    last.then_inc(prod_used, 1)

            def natural(j, u):
                g = 2 * j + u
                pe.wait_ge(usum_ready, g + 1)
                for h in range(GT):
                    n = slice(h * P, (h + 1) * P)
                    mm(x_ps[:, D * h:D * h + S0], usum[:, 0, n], net.merge[:, :])
                    mm(x_ps[:, D * h + S0:D * (h + 1)], usum[:, 1, n], net.ident[:, 0:VD], stop=False)
                    last = mm(x_ps[:, D * h + S0:D * (h + 1)], usum[:, 2, n], net.ident[:, V0:P], start=False)
                last.then_inc(nat_done, 1)

            def prepare(j, u):
                g = 2 * j + u
                pe.wait_ge(x_new, g + 1)
                for h in range(GT):
                    xv = v_of(xnew[:, u, h, S0:D])
                    mm(v_ps[0][0:S0, h * P:(h + 1) * P], xnew[:, u, h, 0:S0], net.ident[:, :])
                    for k in range(3):
                        o = ((k + 1) % 2) * GN + h * P
                        last = pe.transpose(v_ps[(k + 1) // 2][0:V0, o:o + P], xv[:, k, :], net.ident[:, :])
                last.then_inc(new_transposed, 1)
                pe.wait_ge(nT_ready, g + 1)
                for h in range(GT):
                    n = slice(h * P, (h + 1) * P)
                    if nxt == "conv":
                        mm(next_ps[h][:, 192:320], nT[0:S0, 0, n], prep["ws"])
                        for k in range(3):
                            last = mm(next_ps[h][:, 320 + 64 * k:384 + 64 * k], nT[0:V0, k + 1, n], prep["wv"])
                    else:
                        last = mm(next_ps[h][:, 192:224], nT[0:S0, 0, n], prep["ws"])
                last.then_inc(next_done, 1)

            pe.wait_ge(zeroed, 1)
            front(0, 0)
            a_operands(0, 0)

            def body(j, u):
                past, coming = has(j, u, -1), has(j, u, 1)
                for b in range(NXB):
                    x_operands(j, u, b)
                    if b >= 1:
                        sum_up(j, u, b - 1)
                    elif past:
                        sum_up(*at(j, u, -1), NXB - 1)
                    if b == 1 and past:
                        natural(*at(j, u, -1))
                    if b == 5 and past:
                        prepare(*at(j, u, -1))
                    if b == 7 and coming:
                        front(*at(j, u, 1))
                    if b == 9 and coming:
                        a_operands(*at(j, u, 1))
            groups(pe, body)
            sum_up(NJG, 0, NXB - 1)
            natural(NJG, 0)
            prepare(NJG, 0)

        @block.scalar
        def _(act):
            def copy(to, frm, **kw):
                return act.activation(to, frm, ACT.Copy, **kw)

            def front(j, u):
                g = 2 * j + u
                act.wait_ge(transposed, g + 1)
                if has(j, u, -2):
                    act.wait_ge(nat_done, g - 1)
                copy(aggT[:, 0, :], t_ps[:, 0:GN])
                copy(aggT[0:V0, 1, :], t_ps[0:V0, GN:2 * GN])
                copy(vecT[:, 0:2, :], v_ps[0][0:VD, :].rearrange("p (k n) -> p k n", k=2))
                copy(vecT[:, 2, :], v_ps[1][0:VD, 0:GN])
                if has(j, u, -2):
                    act.wait_ge(prod_used, NP_ * (g - 1))
                copy(xa[:, u, 0, :], x_ps[:, 0:GN])
                copy(xa[0:V0, u, 2, :], x_ps[0:V0, GN:2 * GN]).then_inc(opsT_ready, 1)
                act.wait_ge(lin_done, g + 1)
                copy(xa[:, u, 1, :], t_ps[:, 0:GN])
                copy(xa[V0:2 * V0, u, 2, :], t_ps[V0:2 * V0, GN:2 * GN]).then_inc(a_ready, 1)

            def a_operands(j, u):
                g = 2 * j + u
                if has(j, u, -2):
                    act.wait_ge(prod_ready, NP_ * (g - 1))
                for n in range(NXB // 2):
                    act.wait_ge(arep_done, NXB // 2 * g + n + 1)
                    copy(arep[:, u, 2 * n:2 * n + 2, :], v_ps[n % 2][:, :].rearrange("p (k n) -> p k n", k=2))\
                        .then_inc(arep_ready, 1)

            def finish(j, u):
                g = 2 * j + u
                act.wait_ge(prod_used, NP_ * (g + 1))
                if has(j, u, -1):
                    act.wait_ge(nat_done, g)
                copy(usum[:, 0, :], us_ps[:, 0:GN])
                copy(usum[0:VD, 1, :], uv_ps[0:VD, 0, :])
                copy(usum[V0:2 * V0, 2, :], uv_ps[V0:2 * V0, 1, :])
                copy(usum[2 * V0:P, 2, :], uv_ps[2 * V0:P, 1, :]).then_inc(usum_ready, 1)
                act.wait_ge(var_ready, g + 1)
                if has(j, u, -1):
                    act.wait_ge(rstd_ready, g)
                act.activation(sd[:, :], mv[:, :, 1], ACT.Sqrt, bias=net.eps[:, 0:1]).then_inc(sd_ready, 1)

            def prepare(j, u):
                g = 2 * j + u
                act.wait_ge(new_transposed, g + 1)
                copy(nT[0:S0, 0, :], v_ps[0][0:S0, 0:GN])
                copy(nT[0:V0, 1, :], v_ps[0][0:V0, GN:2 * GN])
                copy(nT[0:V0, 2:4, :], v_ps[1][0:V0, :].rearrange("p (k n) -> p k n", k=2)).then_inc(nT_ready, 1)
                if has(j, u, -1):
                    act.wait_ge(stored, 16 * g)
                act.wait_ge(next_done, g + 1)
                for h in range(GT):
                    row, q = trow[:, h, :], next_ps[h]
                    if nxt == "conv":
                        by = net.nodea[:, bass.ds(GT * g + h, 1)]
                        copy(row[:, 0:S0], q[:, 192:256], scale=by)
                        last = copy(v_of(row[:, S0:D]),
                                    q[:, 320:512].rearrange("p (k h f) -> p k h f", k=3, h=2)[:, :, 0, :], scale=by)
                    else:
                        copy(row[:, 0:D], xnew[:, u, h, :])
                        last = copy(row[:, D:TW], q[:, 192:224])
                last.then_inc(row_ready, 1)

            act.wait_ge(zeroed, 1)
            front(0, 0)
            a_operands(0, 0)

            def body(j, u):
                if has(j, u, -1):
                    finish(*at(j, u, -1))
                    prepare(*at(j, u, -1))
                if has(j, u, 1):
                    front(*at(j, u, 1))
                    a_operands(*at(j, u, 1))
            groups(act, body)
            finish(NJG, 0)
            prepare(NJG, 0)

        @block.vector
        def _(dve):
            counts = Count(dve, f"{tag}_counts", 0)
            dve.memset(xa[2 * V0:P, :, 2, :], 0.0)
            dve.memset(usum[:, 1:3, :], 0.0)
            if nxt == "conv":
                dve.memset(trow[:, :, D:TW], 0.0)
            dve.memset(stats[:, :, :], 0.0).then_inc(zeroed, 1)

            def products(j, u, b):
                g = 2 * j + u
                if b == 0:
                    dve.wait_ge(arep_ready, NXB // 2 * (g + 1))
                dve.wait_ge(xrep_done, NXB * g + b + 1)
                x2 = rep_ps[b % 2][:, :, :]
                if b < 4:
                    sets = [(0, 4), (4, 6)]
                else:
                    sets = [(0, 4), (4 + 2 * ((b - 4) // 2), 2)]
                for part, (first, n) in enumerate(sets):
                    if part == 0 and (b >= 2 or has(j, u, -1)):
                        dve.wait_ge(prod_used, NP_ * g + 2 * b - 3)
                    if part == 1 and (b >= 1 or has(j, u, -1)):
                        dve.wait_ge(prod_used, NP_ * g + 2 * b)
                    to = (odd[:, 0:2 * n, :] if part else even[:, b % 2, 0:2 * n, :])\
                        .rearrange("p (v i) n -> p v i n", i=2)
                    dve.tensor_tensor(to, x2.unsqueeze(1).broadcast_to([P, n, 2, GN]),
                                      arep[:, u, first:first + n, :].unsqueeze(2).broadcast_to([P, n, 2, GN]),
                                      ALU.mult).then_inc(prod_ready, 1)

            def result(j, u):
                g = 2 * j + u
                dve.wait_ge(nat_done, g + 1)
                if has(j, u, -1):
                    dve.wait_ge(x_new, g)
                for h in range(GT):
                    x = net.xres[:, bass.ds(GT * g + h, 1), :].rearrange("p a f -> p (a f)")
                    ys = y[:, h, :]
                    dve.scalar_tensor_tensor(ys[:, 0:S0], x[:, 0:S0], 2.0, x_ps[:, D * h:D * h + S0], ALU.mult, ALU.add)
                    last = dve.scalar_tensor_tensor(
                        v_of(ys[:, S0:D]), v_of(x[:, S0:D]), 2.0,
                        x_ps[:, D * h + S0:D * (h + 1)].rearrange("p (k f) -> p k f", k=3), ALU.mult, ALU.add)
                last.then_inc(y_ready, 1)
                dve.wait_ge(y_ready, g + 1)
                for h in range(GT):
                    last = dve.bn_stats(stats[:, h, :], y[:, h, :])
                last.then_inc(stats_ready, 1)
                counts.up(1)
                dve.wait_ge(loaded, 16)
                dve.wait_ge(stats_ready, counts.reg)
                for h in range(GT):
                    last = dve.bn_aggr(mv[:, h, :], stats[:, h, :])
                last.then_inc(var_ready, 1)

            def norm(j, u):
                g = 2 * j + u
                dve.wait_ge(sd_ready, g + 1)
                dve.reciprocal(rstd[:, :], sd[:, :]).then_inc(rstd_ready, 1)
                dve.wait_ge(rstd_ready, g + 1)
                if has(j, u, -2):
                    dve.wait_ge(row_ready, g - 1)
                for h in range(GT):
                    to = net.xres[:, bass.ds(GT * g + h, 1), :].rearrange("p a f -> p (a f)")
                    dve.tensor_scalar(to, y[:, h, :], mv[:, h, 0:1], rstd[:, h:h + 1], ALU.subtract, ALU.mult)
                    last = dve.tensor_scalar(xnew[:, u, h, :], y[:, h, :], mv[:, h, 0:1], rstd[:, h:h + 1],
                                             ALU.subtract, ALU.mult)
                last.then_inc(x_new, 1)

            def base(j, u):
                g = 2 * j + u
                dve.wait_ge(row_ready, g + 1)
                for h in range(GT):
                    by, q, xn = net.nodea[:, bass.ds(GT * g + h, 1)], next_ps[h], xnew[:, u, h, :]
                    to = net.base[:, bass.ds(GT * g + h, 1), :].rearrange("p a f -> p (a f)")
                    dve.scalar_tensor_tensor(to[:, 0:S0], q[:, 256:320], by, xn[:, 0:S0], ALU.mult, ALU.add)
                    last = dve.scalar_tensor_tensor(
                        v_of(to[:, S0:D]), q[:, 320:512].rearrange("p (k h f) -> p k h f", k=3, h=2)[:, :, 1, :],
                        by, v_of(xn[:, S0:D]), ALU.mult, ALU.add)
                last.then_inc(base_ready, 1)

            def body(j, u):
                past = has(j, u, -1)
                for b in range(NXB):
                    products(j, u, b)
                    if b == 2 and past:
                        result(*at(j, u, -1))
                    if b == 3 and past:
                        norm(*at(j, u, -1))
                    if b == 6 and past and nxt == "conv":
                        base(*at(j, u, -1))
            groups(dve, body)
            result(NJG, 0)
            norm(NJG, 0)
            if nxt == "conv":
                base(NJG, 0)


def node_stage(net, tag, kind, nxt, lay, prep, acc, C, table, out):
    nc = net.nc
    with net.stage() as c:
        agg = net.sb(f"{tag}_agg", [P, 2, C], F32, c)
        xin = net.sb(f"{tag}_xin", [P, 2, D], F32, c)
        xnew = net.sb(f"{tag}_xnew", [P, 2, D], F32, c)
        aggT = net.sb(f"{tag}_aggT", [P, 2 * P], F32, c)
        vecT = net.sb(f"{tag}_vecT", [VD, 3 * P], F32, c)
        xT = net.sb(f"{tag}_xT", [S0, 4 * P], F32, c)
        a_nat = net.sb(f"{tag}_a_nat", [P, D], F32, c)
        y = net.sb(f"{tag}_y", [P, 2, D], F32, c)
        stats = net.sb(f"{tag}_stats", [P, 6], F32, c)
        mv = net.sb(f"{tag}_mv", [P, 2], F32, c)
        sd = net.sb(f"{tag}_sd", [P, 1], F32, c)
        rstd = net.sb(f"{tag}_rstd", [P, 1], F32, c)
        small = net.sb(f"{tag}_small", [P, 8], F32, c)
        nT = net.sb(f"{tag}_nT", [S0, 4 * P], F32, c)
        trow = net.sb(f"{tag}_trow", [P, 2, TW], F32, c)
        aggT_ps = net.ps(f"{tag}_aggT_ps", [P, 512], c)
        vecT_ps = net.ps(f"{tag}_vecT_ps", [P, 512], c)
        xT_ps = net.ps(f"{tag}_xT_ps", [P, 512], c)
        lin_ps = net.ps(f"{tag}_lin_ps", [P, 512], c)
        next_ps = net.ps(f"{tag}_next_ps", [P, 512], c)
        nT_ps = net.ps(f"{tag}_nT_ps", [P, 512], c)
        loaded = [net.sem(f"{tag}_loaded{s}", c) for s in range(2)]
        agg_transposed = net.sem(f"{tag}_agg_transposed", c)
        aggT_ready = net.sem(f"{tag}_aggT_ready", c)
        x_transposed = net.sem(f"{tag}_x_transposed", c)
        xT_ready = net.sem(f"{tag}_xT_ready", c)
        lin_done = net.sem(f"{tag}_lin_done", c)
        a_ready = net.sem(f"{tag}_a_ready", c)
        rstd_ready = net.sem(f"{tag}_rstd_ready", c)
        relu_ready = net.sem(f"{tag}_relu_ready", c)
        dve_step = net.sem(f"{tag}_dve_step", c)
        var_ready = net.sem(f"{tag}_var_ready", c)
        sd_ready = net.sem(f"{tag}_sd_ready", c)
        x_new = net.sem(f"{tag}_x_new", c)
        new_transposed = net.sem(f"{tag}_new_transposed", c)
        nT_ready = net.sem(f"{tag}_nT_ready", c)
        next_done = net.sem(f"{tag}_next_done", c)
        row_ready = net.sem(f"{tag}_row_ready", c)
        stored = [net.sem(f"{tag}_stored{s}", c) for s in range(2)]
        block = c.enter_context(nc.Block())

        NJT = NT // 2
        assert NT % 2 == 1

        def tiles(eng, body):
            body(0, 0)
            body(0, 1)
            with eng.Fori(1, NJT) as j:
                body(j, 0)
                body(j, 1)
            body(NJT, 0)

        def has(j, u, d):
            return not isinstance(j, int) or 0 <= 2 * j + u + d

        def prev(j, u):
            return j + (u - 1) // 2, (u - 1) % 2

        NLOAD = 1 if kind == "first" else 2

        @block.sync
        def _(sp):
            def body(j, u):
                t = 2 * j + u
                if has(j, u, -2):
                    sp.wait_ge(row_ready if kind == "first" else x_new, t - 1)
                sp.dma_start((xnew if kind == "first" else xin)[:, u, :],
                             net.xres[:, bass.ds(t, 1), :].rearrange("p a f -> p (a f)")).then_inc(loaded[u], 16)
                if kind != "first":
                    sp.dma_start(agg[:, u, :], acc[:, bass.ds(t, 1), 0:C].rearrange("p a f -> p (a f)"))\
                        .then_inc(loaded[u], 16)
                if has(j, u, -1):
                    store(*prev(j, u))

            def store(j, u):
                t = 2 * j + u
                if nxt is not None:
                    sp.wait_ge(row_ready, t + 1)
                    sp.dma_start(table[bass.ds(t * P, P), :], trow[:, u, :]).then_inc(stored[u], 16)
                else:
                    sp.wait_ge(x_new, t + 1)
                    rows = TAIL if isinstance(j, int) and t == NT - 1 else P
                    sp.dma_start(out[bass.ds(t * P, rows), :], xnew[0:rows, u, :]).then_inc(stored[u], 16)
            tiles(sp, body)
            store(NJT, 0)
            sp.wait_ge(stored[0], 16 * (NJT + 1))
            sp.wait_ge(stored[1], 16 * NJT)

        def v_of(ap):
            return ap.rearrange("p (f k) -> p k f", k=3)

        def k_of(ap):
            return ap.rearrange("p (k f) -> p k f", k=3)

        @block.tensor
        def _(pe):
            mm = pe.matmul

            def transpose(to, frm):
                return mm(to, frm, net.ident[:, :], start=True, stop=True)

            def prepare(j, u):
                t = 2 * j + u
                if kind == "first":
                    pe.wait_ge(loaded[u], 16 * j + 16)
                else:
                    pe.wait_ge(x_new, t + 1)
                if has(j, u, -1):
                    pe.wait_ge(nT_ready, t)
                transpose(nT_ps[0:S0, 0:P], xnew[:, u, 0:S0])
                xv = v_of(xnew[:, u, S0:D])
                for k in range(3):
                    last = transpose(nT_ps[0:V0, (k + 1) * P:(k + 2) * P], xv[:, k, :])
                last.then_inc(new_transposed, 1)
                pe.wait_ge(nT_ready, t + 1)
                if has(j, u, -1):
                    pe.wait_ge(row_ready, t)
                mm(next_ps[:, 0:V0], nT[:, 0:P], prep["ws"], start=True, stop=True).then_inc(next_done, 1)

            def body(j, u):
                t = 2 * j + u
                if kind == "first":
                    prepare(j, u)
                    return
                pe.wait_ge(loaded[u], 32 * j + 32)
                if has(j, u, -1):
                    pe.wait_ge(aggT_ready, t)
                ag = agg[:, u, :]
                transpose(aggT_ps[0:VD, 0:P], ag[:, 0:VD])
                for k in range(3):
                    last = transpose(vecT_ps[0:VD, k * P:(k + 1) * P], ag[:, VD * (k + 1):VD * (k + 2)])
                last.then_inc(agg_transposed, 1)
                pe.wait_ge(aggT_ready, t + 1)
                if kind == "conv":
                    if has(j, u, -1):
                        pe.wait_ge(a_ready, t)
                    mm(lin_ps[:, 0:S0 + 1], aggT[0:VD, 0:P], lay["scal"], start=True, stop=True)
                    for k in range(3):
                        last = mm(lin_ps[:, 65 + V0 * k:65 + V0 * (k + 1)], vecT[:, k * P:(k + 1) * P],
                                  lay["vec"], start=True, stop=True)
                    last.then_inc(lin_done, 1)
                else:
                    if has(j, u, -1):
                        pe.wait_ge(xT_ready, t)
                    mm(xT_ps[0:S0, 0:P], lay["scal"], aggT[0:VD, 0:P], start=True, stop=True)
                    mm(xT_ps[0:V0, P:4 * P], lay["vec"], vecT[:, :], start=True, stop=True).then_inc(x_transposed, 1)
                    pe.wait_ge(xT_ready, t + 1)
                    if has(j, u, -1):
                        pe.wait_ge(relu_ready, t)
                    mm(lin_ps[:, 0:S0], xT[:, 0:P], lay["hs"], start=True, stop=True)
                    for k in range(3):
                        last = mm(lin_ps[:, S0 + V0 * k:S0 + V0 * (k + 1)], xT[0:V0, (k + 1) * P:(k + 2) * P],
                                  lay["hv"], start=True, stop=True)
                    last.then_inc(lin_done, 1)
                if nxt is not None and has(j, u, -1):
                    prepare(*prev(j, u))
            tiles(pe, body)
            if kind != "first" and nxt is not None:
                prepare(NJT, 0)

        @block.scalar
        def _(act):
            def copy(to, frm, **kw):
                return act.activation(to, frm, ACT.Copy, **kw)

            def prepare(j, u):
                t = 2 * j + u
                act.wait_ge(new_transposed, t + 1)
                if has(j, u, -1):
                    act.wait_ge(next_done, t)
                copy(nT[:, 0:P], nT_ps[0:S0, 0:P])
                copy(nT[0:V0, P:4 * P], nT_ps[0:V0, P:4 * P]).then_inc(nT_ready, 1)
                if has(j, u, -2):
                    act.wait_ge(stored[u], 16 * j)
                act.wait_ge(next_done, t + 1)
                copy(trow[:, u, 0:D], xnew[:, u, :])
                copy(trow[:, u, D:TW], next_ps[:, 0:V0]).then_inc(row_ready, 1)

            def body(j, u):
                t = 2 * j + u
                if kind == "first":
                    act.wait_ge(loaded[u], 16 * j + 16)
                    prepare(j, u)
                    return
                act.wait_ge(agg_transposed, t + 1)
                if has(j, u, -1):
                    act.wait_ge(lin_done, t)
                copy(aggT[0:VD, 0:P], aggT_ps[0:VD, 0:P])
                copy(vecT[:, :], vecT_ps[0:VD, 0:3 * P]).then_inc(aggT_ready, 1)
                if kind == "cross":
                    act.wait_ge(x_transposed, t + 1)
                    copy(xT[:, 0:P], xT_ps[0:S0, 0:P])
                    copy(xT[0:V0, P:4 * P], xT_ps[0:V0, P:4 * P]).then_inc(xT_ready, 1)
                    act.wait_ge(lin_done, t + 1)
                    if has(j, u, -1):
                        act.wait_ge(var_ready, t)
                    act.activation(a_nat[:, 0:S0], lin_ps[:, 0:S0], ACT.Relu)
                    act.activation(v_of(a_nat[:, S0:D]), k_of(lin_ps[:, S0:D]), ACT.Relu).then_inc(relu_ready, 1)
                if nxt is not None and has(j, u, -1):
                    prepare(*prev(j, u))
                act.wait_ge(var_ready, t + 1)
                act.activation(sd[:, :], mv[:, 1:2], ACT.Sqrt, bias=net.eps[:, 0:1]).then_inc(sd_ready, 1)
            tiles(act, body)
            if kind != "first" and nxt is not None:
                prepare(NJT, 0)

        @block.vector
        def _(dve):
            stats_count = Count(dve, f"{tag}_stats_count", 0)
            CHAIN = {"first": 0, "conv": 6, "cross": 2}[kind]

            def body(j, u):
                t = 2 * j + u
                if kind == "first":
                    return
                n_own = [0]

                def step(ins):
                    n_own[0] += 1
                    ins.then_inc(dve_step, 1)
                    dve.wait_ge(dve_step, CHAIN * t + n_own[0])

                x, ys = xin[:, u, :], y[:, u, :]
                if kind == "conv":
                    b = net.base[:, bass.ds(t, 1), :].rearrange("p a f -> p (a f)")
                    dve.wait_ge(loaded[u], 32 * j + 32)
                    step(dve.tensor_scalar(small[:, 0:1], agg[:, u, 4 * VD:C], 1.0, None, ALU.max))
                    step(dve.reciprocal(small[:, 1:2], small[:, 0:1]))
                    step(dve.scalar_tensor_tensor(small[:, 2:3], small[:, 1:2], 1.0 / math.sqrt(VD),
                                                  net.nodea[:, bass.ds(t, 1)], ALU.mult, ALU.mult))
                    dve.wait_ge(lin_done, t + 1)
                    step(dve.tensor_tensor(small[:, 3:4], lin_ps[:, S0:S0 + 1], small[:, 2:3], ALU.mult))
                    step(dve.tensor_tensor(small[:, 4:5], small[:, 3:4], small[:, 2:3], ALU.mult))
                    dve.scalar_tensor_tensor(ys[:, 0:S0], lin_ps[:, 0:S0], small[:, 4:5], b[:, 0:S0],
                                             ALU.mult, ALU.add)
                    step(dve.scalar_tensor_tensor(v_of(ys[:, S0:D]), k_of(lin_ps[:, S0 + 1:D + 1]), small[:, 4:5],
                                                  v_of(b[:, S0:D]), ALU.mult, ALU.add))
                else:
                    dve.wait_ge(loaded[u], 32 * j + 32)
                    dve.wait_ge(relu_ready, t + 1)
                    step(dve.scalar_tensor_tensor(ys, x, 2.0, a_nat[:, :], ALU.mult, ALU.add))
                dve.bn_stats(stats[:, :], ys).then_inc(a_ready if kind == "conv" else dve_step, 1)
                stats_count.up(1 if kind == "conv" else CHAIN)
                dve.wait_ge(loaded[0], 16)
                dve.wait_ge(a_ready if kind == "conv" else dve_step, stats_count.reg)
                dve.bn_aggr(mv[:, :], stats[:, :]).then_inc(var_ready, 1)
                dve.wait_ge(sd_ready, t + 1)
                dve.reciprocal(rstd[:, :], sd[:, :]).then_inc(rstd_ready, 1)
                dve.wait_ge(rstd_ready, t + 1)
                if has(j, u, -2):
                    if nxt is not None:
                        dve.wait_ge(row_ready, t - 1)
                    else:
                        dve.wait_ge(stored[u], 16 * j)
                if nxt is not None:
                    dve.tensor_scalar(net.xres[:, bass.ds(t, 1), :].rearrange("p a f -> p (a f)"), ys,
                                      mv[:, 0:1], rstd[:, 0:1], ALU.subtract, ALU.mult)
                dve.tensor_scalar(xnew[:, u, :], ys, mv[:, 0:1], rstd[:, 0:1], ALU.subtract, ALU.mult)\
                    .then_inc(x_new, 1)
            tiles(dve, body)


def gnn_kernel(nc, ins, out):
    with ExitStack() as ctx:
        net = Net(nc, ctx)
        ctx.enter_context(nc.allow_non_contiguous_dma(reason="small tables, one value a node"))
        g = lambda n: ins[n]
        rec_src = net.dram("rec_src", [E + GE, 6])
        rec_dst = net.dram("rec_dst", [E + GE, 22])
        net.pads = [(rec_src, 6), (rec_dst, 22)]
        table = net.dram("table", [NTP * P, TW])
        net.xres = net.sb("xres", [P, NTP, D])
        net.base = net.sb("base", [P, NTP, D])
        net.nodea = net.sb("nodea", [P, NTP])
        net.wfc1 = net.sb("wfc1", [JB * 22, JB // 2, 2 * S0])
        net.wfc2 = net.sb("wfc2", [2 * S0, TW])

        def full_layer(n, ss, vv, sv, vs, l0, l1, m0d, m1d, m0, m1, mdot, f, msv, fsv):
            t = {k: net.sb(f"w{n}_{k}", shape) for k, shape in (
                ("ss", [P, 8, 4, S0]), ("vv", [P, 4, 2, S0]), ("sv", [P, 8, 2, V0]), ("vs", [P, 4, 4, V0]),
                ("l0", [P, S0]), ("l1", [P, 3, V0]), ("m0", [2 * S0, S0]), ("m1", [VD, V0]), ("mdot", [V0, S0]),
                ("msv", [S0, V0]))}
            lay = {"chunks": {"ss": (t["ss"], ss), "vv": (t["vv"], vv), "sv": (t["sv"], sv), "vs": (t["vs"], vs)},
                   "plain": [(t["l0"][0:S0, :], l0), (t["l1"][S0:S0 + V0, 0, :], l1),
                             (t["l1"][S0 + V0:P, 1, :], l1), (t["l1"][0:V0, 2, :], l1),
                             (t["m0"][0:S0, :], m0), (t["m0"][S0:2 * S0, :], m0d),
                             (t["m1"][0:V0, :], m1), (t["m1"][V0:2 * V0, :], m1d), (t["mdot"][:, :], mdot),
                             (t["msv"][:, :], msv)],
                   "scales": [(t["ss"][:, :, :, :], f["ss"]), (t["vv"][:, :, :, :], f["vv"]),
                              (t["sv"][:, :, :, :], f["uv"]), (t["vs"][:, :, :, :], f["uv"]),
                              (t["l0"][:, :], f["l0"]), (t["l1"][:, :, :], f["l1"]), (t["m0"][0:S0, :], f["m0"]),
                              (t["m0"][S0:2 * S0, :], f["m0d"]), (t["m1"][0:V0, :], f["m1"]),
                              (t["m1"][V0:2 * V0, :], f["m1d"]), (t["mdot"][:, :], f["mdot"]), (t["msv"][:, :], fsv)]}
            for k in ("l0", "m0", "m1", "mdot"):
                lay[k] = t[k][:, :]
            lay["l1"] = t["l1"]
            lay["prep"] = {"ws": t["msv"][:, :]}
            return lay

        i64, i32, i96 = 1.0 / 8, 1.0 / math.sqrt(V0), 1.0 / math.sqrt(VD)
        fan0, fan1 = S0 * S0 + V0 * V0, 2 * S0 * V0
        lay0 = full_layer(0, g("L0_gnn_wu000"), g("L0_gnn_wu110"), g("L0_gnn_wu011"), g("L0_gnn_wu101"),
                          g("L0_gnn_lu0"), g("L0_gnn_lu1"),
                          g("L0_gnn_wm000").rearrange("u o w -> u (o w)"), g("L0_gnn_wm101").rearrange("u o w -> u (o w)"),
                          g("L0_gnn_lm0"), g("L0_gnn_lm1"), g("L0_gnn_wm110").rearrange("u o w -> u (o w)"),
                          dict(ss=1 / math.sqrt(fan0), vv=K3 / math.sqrt(fan0), uv=1 / math.sqrt(fan1), l0=i64, l1=i32,
                               m0=i64, m0d=i96, m1=i32, m1d=i96, mdot=K3 * i96),
                          g("L0_gnn_wm011").rearrange("u o w -> u (o w)"), i96)
        lay2 = full_layer(2, g("L2_gnn_Wu_ss"), g("L2_gnn_Wu_vv"), g("L2_gnn_Wu_sv"), g("L2_gnn_Wu_vs"),
                          g("L2_gnn_Lu_s"), g("L2_gnn_Lu_v"), g("L2_gnn_Wm_ss"), g("L2_gnn_Wm_vs"),
                          g("L2_gnn_Lm_s"), g("L2_gnn_Lm_v"), g("L2_gnn_Wm_vv"),
                          dict(ss=0.015625, vv=K3 * 0.03125, uv=1 / math.sqrt(2048), l0=i64, l1=i32,
                               m0=i64, m0d=i64, m1=i32, m1d=i32, mdot=K3 * i32),
                          g("L2_gnn_Wm_sv"), i64)
        w1 = {k: net.sb(f"w1_{k}", s) for k, s in (("ws", [S0, 2 * S0]), ("wv", [V0, 2 * V0]),
                                                  ("scal", [VD, S0 + 1]), ("vec", [VD, V0]))}
        lay1 = {"chunks": {}, "plain": [
                    (w1["ws"][:, 0:S0], g("L1_gnn_Wl1_0")), (w1["ws"][:, S0:2 * S0], g("L1_gnn_Wsc0")),
                    (w1["wv"][:, 0:V0], g("L1_gnn_Wl1_1")), (w1["wv"][:, V0:2 * V0], g("L1_gnn_Wsc1")),
                    (w1["scal"][:, 0:S0], g("L1_gnn_Wl2_s")), (w1["scal"][:, S0:S0 + 1], g("L1_gnn_Wa")),
                    (w1["vec"][:, :], g("L1_gnn_Wl2_v")),
                    *[(net.wfc1[22 * q + 6:22 * (q + 1), q % 2, q // 2 * S0:(q // 2 + 1) * S0], g("L1_gnn_Wfc1"))
                      for q in range(JB)],
                    (net.wfc2[0:S0, :], g("L1_gnn_Wfc2")), (net.wfc2[S0:2 * S0, :], g("L1_gnn_Wfc2")),
                    (net.xres[:, 0:NT - 1, :], g("x")[0:(NT - 1) * P, :].rearrange("(t p) f -> p t f", p=P)),
                    (net.xres[0:TAIL, NT - 1, :], g("x")[(NT - 1) * P:N, :]),
                    (net.nodea[:, 0:NT - 1].rearrange("p (t o) -> p t o", o=1),
                     g("node_vec1")[0:(NT - 1) * P, :].rearrange("(t p) o -> p t o", p=P)),
                    (net.nodea[0:TAIL, NT - 1:NT], g("node_vec1")[(NT - 1) * P:N, :])],
                "scales": [(w1["ws"][:, :], i64), (w1["wv"][:, :], i32), (net.wfc1[:, :, :], 0.25),
                           (net.wfc2[:, 0:TW - V0], i64), (net.wfc2[:, TW - V0:TW], i64 * K3)],
                "scal": w1["scal"][:, :], "vec": w1["vec"][:, :],
                "prep": {"ws": w1["ws"][:, :], "wv": w1["wv"][:, :]}}
        w3 = {k: net.sb(f"w3_{k}", s) for k, s in (("w3", [S0, V0]), ("scal", [VD, S0]), ("vec", [VD, V0]),
                                                  ("hs", [S0, S0]), ("hv", [V0, V0]))}
        C0, C1 = 1 / math.sqrt(S0 + V0), math.sqrt(3.0 / (S0 + 2 * V0))
        lay3 = {"chunks": {}, "plain": [
                    (w3["w3"][:, :], g("L3_gnn_W3")), (w3["scal"][0:S0, :], g("L3_gnn_W1")),
                    (w3["scal"][S0:VD, :], g("L3_gnn_W2")), (w3["vec"][0:V0, :], g("L3_gnn_W4")),
                    (w3["vec"][2 * V0:VD, :], g("L3_gnn_W5")), (w3["hs"][:, :], g("L3_gnn_Ws")),
                    (w3["hv"][:, :], g("L3_gnn_Wv"))],
                "scales": [(w3["w3"][:, :], C1 * K3), (w3["scal"][0:S0, :], C0), (w3["scal"][S0:VD, :], C0 * K3),
                           (w3["vec"][0:V0, :], C1 * K3), (w3["vec"][2 * V0:VD, :], C1 / math.sqrt(6.0)),
                           (w3["hs"][:, :], i64), (w3["hv"][:, :], i32)],
                "scal": w3["scal"][:, :], "vec": w3["vec"][:, :], "hs": w3["hs"][:, :], "hv": w3["hv"][:, :],
                "prep": {"ws": w3["w3"][:, :]}}

        with ExitStack() as c:
            block = c.enter_context(nc.Block())

            @block.vector
            def _(dve):
                dve.memset(net.xres[:, NT - 1:NTP, :], 0.0)
                dve.memset(net.nodea[:, NT - 1:NTP], 0.0)
                dve.memset(net.wfc1[:, :, :], 0.0)
                for lay in (lay0, lay2):
                    dve.memset(lay["l0"], 0.0)
                    dve.memset(lay["l1"][:, :, :], 0.0)

        constants(net)

        def schedule(tag):
            return (net.sb(f"{tag}_erow", [1, NIP], I32), net.sb(f"{tag}_trow", [1, NIP], I32),
                    net.sb(f"{tag}_tbase", [P, NIP], F32))

        by_src, by_dst = schedule("src"), schedule("dst")
        fills = [(w3["vec"][V0:2 * V0, :], net.ident[V0:2 * V0, V0:2 * V0])]
        fills += [(lay["m1"][2 * V0:VD, :], net.ident[2 * V0:VD, 2 * V0:VD]) for lay in (lay0, lay2)]
        prepare_edges(net, ins, rec_src, rec_dst, by_src, by_dst, [lay0, lay1, lay2, lay3], fills)
        CM = 2 * D + V0 + VD
        acc = net.sb("acc", [P, NT + 1, CM])

        node_stage(net, "n", "first", "plain", None, lay0["prep"], acc, CM, table, out)
        edge_loop(net, "e0", "plain", rec_src, by_src, table, acc, CM)
        outer_stage(net, "n0", "conv", lay0, lay1["prep"], acc, CM, table)
        edge_loop(net, "e1", "conv", rec_dst, by_dst, table, acc, 4 * VD + 1)
        node_stage(net, "n1", "conv", "plain", lay1, lay2["prep"], acc, 4 * VD + 1, table, out)
        edge_loop(net, "e2", "plain", rec_src, by_src, table, acc, CM)
        outer_stage(net, "n2", "cross", lay2, lay3["prep"], acc, CM, table)
        edge_loop(net, "e3", "cross", rec_dst, by_dst, table, acc, 4 * VD)
        node_stage(net, "n3", "cross", None, lay3, None, acc, 4 * VD, table, out)


def kernel(**inputs):
    import numpy as _np
    import concourse.bacc as _bacc
    from concourse import mybir as _mybir
    from concourse.bass_utils import run_bass_kernel_spmd as _run

    nc = _bacc.Bacc("TRN2", target_bir_lowering=False, num_devices=1)
    arrays, args = {}, {}
    for name in inputs:
        a = _np.ascontiguousarray(inputs[name])
        arrays[f"in_{name}"] = a
        args[name] = nc.dram_tensor(f"in_{name}", a.shape, _mybir.dt.from_np(a.dtype), kind="ExternalInput").ap()
    out = nc.dram_tensor("out_x", (N, D), F32, kind="ExternalOutput").ap()
    gnn_kernel(nc, args, out)
    r = _run(nc, [arrays], core_ids=[0])
    return r.results[0]["out_x"]
```

```python
import math
from contextlib import ExitStack, contextmanager

import concourse.bass as bass
from concourse import mybir

F32 = mybir.dt.float32
I32 = mybir.dt.int32
ALU = mybir.AluOpType
ACT = mybir.ActivationFunctionType
AXX = mybir.AxisListType.X

P = 128
N, D = 3125, 160
S0, V0, VD = 64, 32, 96
E = 100000
NT = (N + P - 1) // P
TAIL = N - (NT - 1) * P
EP, EC = 125, 800
JB = 4
GE = JB * P
NI = (E + NT * (GE - 1)) // GE
SL = 4
NJ = NI // SL
assert NI % SL == 0 and EP * EC == E
NIP = 2 * P
GT = 2
GN = GT * P
NG = (NT + GT - 1) // GT
NXB = 10
NTP = GT * NG
TW = 192
UP, VP = 8, 16
EPS = 1e-5
GC = 8
K3 = 1.0 / math.sqrt(3.0)


class Count:

    def __init__(self, eng, name, start):
        self.eng, self.reg = eng, eng.alloc_register(name)
        eng.reg_mov(self.reg, start)

    def up(self, by):
        self.eng.reg_add(self.reg, self.reg, by)


class Net:

    def __init__(self, nc, ctx):
        self.nc, self.ctx = nc, ctx

    def sb(self, name, shape, dt=F32, ctx=None):
        return (ctx or self.ctx).enter_context(self.nc.sbuf_tensor(name, shape, dt))

    def ps(self, name, shape, ctx):
        return ctx.enter_context(self.nc.psum_tensor(name, shape, F32))

    def sem(self, name, ctx):
        self.stage_sems.append(self.nc.alloc_semaphore(name=name))
        return self.stage_sems[-1]

    @contextmanager
    def stage(self):
        self.stage_sems = []
        with ExitStack() as c:
            yield c
        self.nc.clear_and_free_semaphores(self.stage_sems)
        self.nc.all_engine_barrier()

    def dram(self, name, shape, dt=F32):
        return self.nc.dram_tensor(name, shape, dt, kind="Internal").ap()


def constants(net):
    nc = net.nc
    net.ident = net.sb("ident", [P, P])
    net.ramp = net.sb("ramp", [P, P])
    net.part = net.sb("part", [P, 1])
    net.eps = net.sb("eps", [P, 1])
    net.merge = net.sb("merge", [P, S0])
    net.sel_u = net.sb("sel_u", [P, P // UP, P])
    net.sel_v = net.sb("sel_v", [P, P // VP, P])
    with net.stage() as c:
        ramp_i = net.sb("ramp_i", [P, P], I32, c)
        part_i = net.sb("part_i", [P, 1], I32, c)
        uv_i = net.sb("uv_i", [P, 2, P], I32, c)
        uv_f = net.sb("uv_f", [P, 2, P], F32, c)
        pad = net.sb("pad", [P, GE // P * 22], F32, c)
        uv_split = net.sem("uv_split", c)
        ramps_made = net.sem("ramps_made", c)
        floats_made = net.sem("floats_made", c)
        ident_made = net.sem("ident_made", c)
        pad_zero = net.sem("pad_zero", c)
        pad_keys = net.sem("pad_keys", c)
        pads_stored = net.sem("pads_stored", c)
        block = c.enter_context(nc.Block())

        @block.gpsimd
        def _(pool):
            pool.iota(ramp_i[:, :], pattern=[[1, P]], base=0, channel_multiplier=0)
            pool.iota(part_i[:, :], pattern=[[0, 1]], base=0, channel_multiplier=1).then_inc(ramps_made, 1)

        @block.vector
        def _(dve):
            dve.memset(net.eps[:, :], EPS)
            dve.memset(pad[:, :], 0.0).then_inc(pad_zero, 1)
            dve.wait_ge(pad_zero, 1)
            dve.memset(pad[:, :].rearrange("p (j w) -> p j w", w=22)[:, :, 0:1], -1.0).then_inc(pad_keys, 1)
            dve.wait_ge(ramps_made, 1)
            dve.tensor_copy(net.ramp[:, :], ramp_i[:, :])
            dve.tensor_copy(net.part[:, :], part_i[:, :])
            dve.tensor_scalar(uv_i[:, 0, :], ramp_i[:, :], int(math.log2(VP)), None, ALU.logical_shift_right)
            dve.tensor_scalar(uv_i[:, 1, :], ramp_i[:, :], VP - 1, None, ALU.bitwise_and).then_inc(uv_split, 1)
            dve.wait_ge(uv_split, 1)
            dve.tensor_copy(uv_f[:, :, :], uv_i[:, :, :]).then_inc(floats_made, 1)
            dve.wait_ge(floats_made, 1)
            dve.tensor_scalar(net.ident[:, :], net.ramp[:, :], net.part[:, 0:1], None, ALU.is_equal)\
                .then_inc(ident_made, 1)
            for b in range(P // UP):
                dve.tensor_scalar(net.sel_u[:, b, :], uv_f[:, 0, :], float(UP * b), net.part[:, 0:1],
                                  ALU.add, ALU.is_equal)
            for b in range(P // VP):
                dve.tensor_scalar(net.sel_v[:, b, :], uv_f[:, 1, :], float(VP * b), net.part[:, 0:1],
                                  ALU.add, ALU.is_equal)
            dve.wait_ge(ident_made, 1)
            for h in range(2):
                half = slice(h * S0, (h + 1) * S0)
                dve.tensor_copy(net.merge[half, :], net.ident[half, half])

        @block.sync
        def _(sp):
            sp.wait_ge(pad_keys, 1)
            pv = pad[:, :].rearrange("p (j w) -> p j w", w=22)
            for rec, w in net.pads:
                sp.dma_start(rec[E:E + GE, :].rearrange("(p j) w -> p j w", j=GE // P),
                             pv[:, :, 0:w]).then_inc(pads_stored, 16)
            sp.wait_ge(pads_stored, 16 * len(net.pads))


def prepare_edges(net, ins, rec_src, rec_dst, by_src, by_dst, layers, fills, first_w, table):
    nc = net.nc
    W = {"src": 6, "dst": 22}
    PC = 50
    NQ = EC // PC
    rec_raw = net.dram("rec_raw", [E, W["dst"]])
    with ExitStack() as kept:
        pos = {t: net.sb(f"{t}_pos", [EP, EC], F32, kept) for t in W}
        moved_i = net.sb("moved_i", [1, 1], I32, kept)
        with net.stage() as c:
            below = net.sb("below", [P, P], F32, c)
            ones = net.sb("ones", [P, P], F32, c)
            step_i = net.sb("step_i", [P, 2], I32, c)
            step_no = net.sb("step_no", [P, 2], F32, c)
            key_i = {t: net.sb(f"{t}_key_i", [EP, EC], I32, c) for t in W}
            place_i = net.sb("place_i", [EP, EC], I32, c)
            bin_i = net.sb("bin_i", [EP, EC], I32, c)
            bin_f = net.sb("bin_f", [EP, EC], F32, c)
            mask = net.sb("mask", [EP, 2, EC], I32, c)
            rank = net.sb("rank", [EP, 2, EC], F32, c)
            a4 = net.sb("a4", [EP, EC, 4], F32, c)
            a16 = net.sb("a16", [EP, 2, PC, 16], F32, c)
            recs = net.sb("src_recs", [EP, EC, W["src"]], F32, c)
            piece = net.sb("dst_piece", [EP, 2, PC, W["dst"]], F32, c)
            stage_rec = net.sb("stage_rec", [EP, 2, GC, W["src"]], F32, c)
            stage_pos = net.sb("stage_pos", [EP, 2, GC], I32, c)
            moved = net.sb("moved", [EP, 1], F32, c)
            m = {}
            for t in W:
                m[t] = {n: net.sb(f"{t}_{n}", [P, w], dt, c) for n, w, dt in (
                    ("count", NT, F32), ("first", NT, F32), ("total", NT, F32), ("t_end", NT, F32),
                    ("steps_f", NT, F32), ("steps_i", 2 * NT, I32), ("s_first", NT + 1, F32),
                    ("e_first", NT + 1, F32), ("shift", NT + 1, F32), ("dshift", NT + 1, F32),
                    ("junk", 4 * (NT + 1), F32), ("sums", 2, F32), ("step_e", 2, F32), ("step_ei", 2, I32),
                    ("step_t", 2, F32), ("step_ti", 2, I32), ("step_b", 2, F32))}
                m[t]["dram"] = [net.dram(f"{t}_steps{n}", [NIP], dt) for n, dt in enumerate((I32, I32, F32))]
            counts_ps = {t: [net.ps(f"{t}_counts_ps{n}", [P, 512], c) for n in range(2)] for t in W}
            moved_ps = net.ps("moved_ps", [P, 512], c)
            XB = 4
            xT_ps = net.ps("first_xT_ps", [S0, XB * P], c)
            row_ps = net.ps("first_row_ps", [P, 512], c)
            xT = net.sb("first_xT", [S0, XB * P], F32, c)
            row = net.sb("first_row", [P, NT, V0], F32, c)
            batches = [range(t, min(t + XB, NT)) for t in range(0, NT, XB)]

            keys_loaded = {t: net.sem(f"{t}_keys_loaded", c) for t in W}
            a4_loaded = net.sem("a4_loaded", c)
            a16_loaded = [net.sem(f"a16_loaded{s}", c) for s in range(2)]
            ramps_made = net.sem("prep_ramps_made", c)
            dve_step = net.sem("prep_dve_step", c)
            counted = net.sem("counted", c)
            summed = net.sem("summed", c)
            sched_made = net.sem("sched_made", c)
            sched_stored = net.sem("sched_stored", c)
            sched_loaded = net.sem("sched_loaded", c)
            placed = net.sem("placed", c)
            recs_made = net.sem("recs_made", c)
            staged = net.sem("staged", c)
            scattered = [net.sem(f"scattered{s}", c) for s in range(2)]
            piece_made = net.sem("piece_made", c)
            piece_stored = [net.sem(f"piece_stored{s}", c) for s in range(2)]
            moved_counted = net.sem("moved_counted", c)
            moved_summed = net.sem("moved_summed", c)
            weights_loaded = net.sem("weights_loaded", c)
            scaled = net.sem("weights_scaled", c)
            x_turned = net.sem("first_x_turned", c)
            xT_ready = net.sem("first_xT_ready", c)
            row_done = net.sem("first_row_done", c)
            row_ready = net.sem("first_row_ready", c)
            rows_stored = net.sem("first_rows_stored", c)
            block = c.enter_context(nc.Block())

            @block.sync
            def _(sp):
                def load_piece(q):
                    if q >= 2:
                        sp.wait_ge(piece_made, q - 1)
                    sp.dma_start(a16[:, q % 2, :, :],
                                 ins["edge_attr_16"].rearrange("(p c) k -> p c k", p=EP)[:, q * PC:(q + 1) * PC, :])\
                        .then_inc(a16_loaded[q % 2], 16)

                def schedule(t, sched, n):
                    s = m[t]
                    sp.wait_ge(sched_made, n)
                    for d, name in zip(s["dram"], ("step_ei", "step_ti", "step_b")):
                        sp.dma_start(d.rearrange("(h p o) -> p h o", p=P, o=1),
                                     s[name][:, :].rearrange("p (h o) -> p h o", o=1)).then_inc(sched_stored, 16)
                    sp.wait_ge(sched_stored, 48 * n)
                    row = [d.rearrange("(o n) -> o n", o=1) for d in s["dram"]]
                    sp.dma_start(sched[0][:, :], row[0]).then_inc(sched_loaded, 16)
                    sp.dma_start(sched[1][:, :], row[1]).then_inc(sched_loaded, 16)
                    sp.dma_start(sched[2][:, :], row[2].broadcast_to([P, NIP])).then_inc(sched_loaded, 16)

                for t in W:
                    sp.dma_start(key_i[t][:, :], ins[t].rearrange("(p c) -> p c", p=EP)).then_inc(keys_loaded[t], 16)
                sp.dma_start(a4[:, :, :], ins["edge_attr_4"].rearrange("(p c) k -> p c k", p=EP)).then_inc(a4_loaded, 16)
                load_piece(0)
                load_piece(1)
                n = 0
                for lay in layers:
                    for tile, w in lay["chunks"].values():
                        u = w.shape[0]
                        for ui in range(UP):
                            src = w.rearrange("(a b) (c d) w -> b d a c w", b=UP, d=VP)[ui]
                            for a in range(u // UP):
                                sp.dma_start(tile[ui * VP:(ui + 1) * VP, a, :, :], src[:, a])\
                                    .then_inc(weights_loaded, 16)
                                n += 1
                    for dst, src in lay["plain"]:
                        sp.dma_start(dst, src).then_inc(weights_loaded, 16)
                        n += 1
                schedule("src", by_src, 1)
                raw, by_place = (r[0:E, :].rearrange("(p c) w -> p c w", p=EP) for r in (rec_raw, rec_dst))
                for q in range(NQ):
                    sp.wait_ge(piece_made, q + 1)
                    for to in (raw, by_place):
                        sp.dma_start(to[:, q * PC:(q + 1) * PC, :], piece[:, q % 2, :, :])\
                            .then_inc(piece_stored[q % 2], 16)
                    if q + 2 < NQ:
                        load_piece(q + 2)
                schedule("dst", by_dst, 2)
                sp.wait_ge(sched_loaded, 96)
                for s in range(2):
                    sp.wait_ge(piece_stored[s], 32 * NQ // 2)
                sp.wait_ge(weights_loaded, 16 * n)
                to = table[0:NT * P, :].rearrange("(t p) w -> p t w", p=P)
                sp.dma_start(to[:, :, 0:D], net.xres[:, 0:NT, :]).then_inc(rows_stored, 16)
                sp.wait_ge(row_ready, len(batches))
                sp.dma_start(to[:, :, D:TW], row[:, :, :]).then_inc(rows_stored, 16)
                sp.wait_ge(rows_stored, 32)

            n_weights = sum(UP * (w.shape[0] // UP) for lay in layers for _, w in lay["chunks"].values()) \
                + sum(len(lay["plain"]) for lay in layers)

            @block.scalar
            def _(act):
                act.wait_ge(keys_loaded["src"], 16)
                act.activation(recs[:, :, 0], key_i["src"][:, :], ACT.Copy)
                act.wait_ge(keys_loaded["dst"], 16)
                act.activation(recs[:, :, 1], key_i["dst"][:, :], ACT.Copy)
                act.wait_ge(a4_loaded, 16)
                act.activation(recs[:, :, 2:6], a4[:, :, :], ACT.Copy).then_inc(recs_made, 1)
                act.wait_ge(recs_made, 1)
                act.wait_ge(placed, 1)

                def stage(j, s, free):
                    if free is not None:
                        act.wait_ge(scattered[s], free)
                    col = (2 * j + s) * GC
                    act.activation(stage_pos[:, s, :], pos["src"][:, bass.ds(col, GC)], ACT.Copy)
                    act.activation(stage_rec[:, s, :, :], recs[:, bass.ds(col, GC), :], ACT.Copy).then_inc(staged, 1)

                for s in range(2):
                    stage(0, s, None)
                with act.Fori(1, EC // GC // 2) as j:
                    for s in range(2):
                        stage(j, s, 16 * GC * j)

            @block.tensor
            def _(pe):
                for n, t in enumerate(W):
                    pe.wait_ge(counted, n + 1)
                    count = m[t]["count"][0:EP, :]
                    pe.matmul(counts_ps[t][0][0:EP, 0:NT], below[0:EP, 0:EP], count, start=True, stop=True)
                    pe.matmul(counts_ps[t][1][:, 0:NT], ones[0:EP, :], count, start=True, stop=True).then_inc(summed, 1)
                pe.wait_ge(moved_counted, 1)
                pe.matmul(moved_ps[:, 0:1], ones[0:EP, :], moved[:, :], start=True, stop=True).then_inc(moved_summed, 1)
                pe.wait_ge(scaled, 1)
                for q, tiles in enumerate(batches):
                    if q > 0:
                        pe.wait_ge(row_ready, q)
                    for h, t in enumerate(tiles):
                        last = pe.matmul(xT_ps[:, h * P:(h + 1) * P], net.xres[:, t, 0:S0], net.ident[:, :],
                                         start=True, stop=True)
                    last.then_inc(x_turned, 1)
                    pe.wait_ge(xT_ready, q + 1)
                    for h, t in enumerate(tiles):
                        last = pe.matmul(row_ps[:, h * V0:(h + 1) * V0], xT[:, h * P:(h + 1) * P], first_w,
                                         start=True, stop=True)
                    last.then_inc(row_done, 1)

            @block.gpsimd
            def _(pool):
                pool.iota(step_i[:, :], pattern=[[P, 2]], base=0, channel_multiplier=1)
                pool.iota(place_i[:, :], pattern=[[1, EC]], base=0, channel_multiplier=EC).then_inc(ramps_made, 1)
                scatter_columns(pool, "src", rec_src, stage_pos, stage_rec, staged, scattered)

            @block.vector
            def _(dve):
                done = [0]

                def step(ins):
                    done[0] += 1
                    ins.then_inc(dve_step, 1)
                    dve.wait_ge(dve_step, done[0])

                def places(t, n):
                    s = {k: v[:, :] for k, v in m[t].items() if k != "dram"}
                    steps_i = s["steps_i"].rearrange("p (a n) -> p a n", a=2)
                    junk = s["junk"].rearrange("p (h a n) -> p h a n", h=2, a=2)
                    dve.wait_ge(keys_loaded[t], 16)
                    step(dve.tensor_scalar(bin_i[:, :], key_i[t][:, :], int(math.log2(P)), None, ALU.logical_shift_right))
                    step(dve.tensor_copy(bin_f[:, :], bin_i[:, :]))
                    for k in range(NT):
                        step(dve.tensor_scalar(rank[:, k % 2, :], bin_f[:, :], float(k), 0.0, ALU.is_equal, ALU.add,
                                               accum_out=s["count"][0:EP, k:k + 1]))
                    dve.sem_inc(counted, 1)
                    dve.wait_ge(summed, n)
                    step(dve.tensor_copy(s["total"], counts_ps[t][1][:, 0:NT]))
                    step(dve.tensor_tensor_scan(s["t_end"], s["total"], s["total"], 0.0, ALU.add, ALU.max))
                    dve.memset(s["e_first"][:, 0:1], 0.0)
                    step(dve.tensor_copy(s["e_first"][:, 1:NT + 1], s["t_end"]))
                    step(dve.tensor_tensor(s["first"][0:EP, :], counts_ps[t][0][0:EP, 0:NT], s["e_first"][0:EP, 0:NT],
                                           ALU.add))
                    for k in range(NT):
                        h = k % 2
                        step(dve.tensor_scalar(mask[:, h, :], bin_f[:, :], float(k), None, ALU.is_equal))
                        step(dve.tensor_tensor_scan(rank[:, h, :], mask[:, h, :], mask[:, h, :],
                                                    s["first"][0:EP, k:k + 1], ALU.add, ALU.max))
                        step(dve.copy_predicated(pos[t][:, :], mask[:, h, :], rank[:, h, :]))
                    step(dve.tensor_scalar(pos[t][:, :], pos[t][:, :], -1.0, None, ALU.add))
                    dve.sem_inc(placed, 1)
                    step(dve.tensor_scalar(steps_i[:, 0, :], s["total"], float(GE - 1), None, ALU.add))
                    step(dve.tensor_scalar(steps_i[:, 1, :], steps_i[:, 0, :], int(math.log2(GE)), None,
                                           ALU.logical_shift_right))
                    step(dve.tensor_copy(s["steps_f"], steps_i[:, 1, :]))
                    dve.memset(s["s_first"][:, 0:1], 0.0)
                    step(dve.tensor_tensor_scan(s["s_first"][:, 1:NT + 1], s["steps_f"], s["steps_f"], 0.0,
                                                ALU.add, ALU.max))
                    step(dve.scalar_tensor_tensor(s["shift"], s["s_first"], -float(GE), s["e_first"], ALU.mult, ALU.add))
                    dve.memset(s["dshift"][:, 0:1], 0.0)
                    step(dve.tensor_tensor(s["dshift"][:, 1:NT + 1], s["shift"][:, 1:NT + 1], s["shift"][:, 0:NT],
                                           ALU.subtract))
                    for h in range(2):
                        dve.tensor_scalar(junk[:, h, 0, :], s["s_first"], step_no[:, h:h + 1], -1.0, ALU.is_le, ALU.add,
                                          accum_out=s["step_t"][:, h:h + 1])
                        step(dve.scalar_tensor_tensor(junk[:, h, 1, :], s["s_first"], step_no[:, h:h + 1], s["dshift"],
                                                      ALU.is_le, ALU.mult, accum_out=s["sums"][:, h:h + 1]))
                    step(dve.scalar_tensor_tensor(s["step_e"], step_no[:, :], float(GE), s["sums"], ALU.mult, ALU.add))
                    dve.tensor_scalar(s["step_ei"], s["step_e"], float(E), None, ALU.min)
                    dve.tensor_copy(s["step_ti"], s["step_t"])
                    dve.tensor_scalar(s["step_b"], s["step_t"], float(P), None, ALU.mult).then_inc(sched_made, 1)

                dve.memset(ones[:, :], 1.0)
                dve.wait_ge(ramps_made, 1)
                dve.tensor_copy(step_no[:, :], step_i[:, :])
                step(dve.tensor_scalar(below[:, :], net.ramp[:, :], net.part[:, 0:1], None, ALU.is_gt))
                places("src", 1)
                places("dst", 2)
                step(dve.tensor_copy(bin_f[:, :], place_i[:, :]))
                step(dve.tensor_tensor(rank[:, 0, :], bin_f[:, :], pos["dst"][:, :], ALU.not_equal))
                dve.tensor_reduce(moved[:, :], rank[:, 0, :], AXX, ALU.add).then_inc(moved_counted, 1)
                dve.wait_ge(a4_loaded, 16)
                for q in range(NQ):
                    cols = slice(q * PC, (q + 1) * PC)
                    to = piece[:, q % 2, :, :]
                    if q >= 2:
                        dve.wait_ge(piece_stored[q % 2], 32 * (q // 2))
                    dve.tensor_copy(to[:, :, 0], key_i["dst"][:, cols])
                    dve.tensor_copy(to[:, :, 1], key_i["src"][:, cols])
                    dve.tensor_copy(to[:, :, 2:6], a4[:, cols, :])
                    dve.wait_ge(a16_loaded[q % 2], 16 * (q // 2 + 1))
                    dve.tensor_copy(to[:, :, 6:22], a16[:, q % 2, :, :]).then_inc(piece_made, 1)
                dve.wait_ge(moved_summed, 1)
                dve.tensor_copy(moved_i[:, :], moved_ps[0:1, 0:1])
                dve.wait_ge(weights_loaded, 16 * n_weights)
                for lay in layers:
                    for ap, factor in lay["scales"]:
                        last = dve.tensor_scalar(ap, ap, factor, None, ALU.mult)
                last.then_inc(scaled, 1)
                dve.wait_ge(scaled, 1)
                for to, frm in fills:
                    dve.tensor_copy(to, frm)
                for q, tiles in enumerate(batches):
                    n = len(tiles)
                    dve.wait_ge(x_turned, q + 1)
                    dve.tensor_copy(xT[:, 0:n * P], xT_ps[:, 0:n * P]).then_inc(xT_ready, 1)
                    dve.wait_ge(row_done, q + 1)
                    dve.tensor_copy(row[:, tiles[0]:tiles[0] + n, :].rearrange("p t w -> p (t w)"),
                                    row_ps[:, 0:n * V0]).then_inc(row_ready, 1)

        with net.stage() as c:
            raw_rec = net.sb("raw_rec", [EP, 2, GC, W["dst"]], F32, c)
            raw_pos = net.sb("raw_pos", [EP, 2, GC], I32, c)
            raw_loaded = [net.sem(f"raw_loaded{s}", c) for s in range(2)]
            pos_ready = net.sem("pos_ready", c)
            moves = [net.sem(f"moves{s}", c) for s in range(2)]
            block = c.enter_context(nc.Block())

            def if_moved(eng, then):
                with eng.If(eng.value_load(moved_i[0:1, 0:1], min_val=0, max_val=E) != 0):
                    then()

            @block.sync
            def _(sp):
                raw = rec_raw.rearrange("(p c) w -> p c w", p=EP)

                def load(j, s, free):
                    if free is not None:
                        sp.wait_ge(moves[s], free)
                    sp.dma_start(raw_rec[:, s, :, :], raw[:, bass.ds((2 * j + s) * GC, GC), :])\
                        .then_inc(raw_loaded[s], 16)

                def loads():
                    for s in range(2):
                        load(0, s, None)
                    with sp.Fori(1, EC // GC // 2) as j:
                        for s in range(2):
                            load(j, s, 16 * GC * j)
                if_moved(sp, loads)

            @block.scalar
            def _(act):
                def place(j, s, free):
                    if free is not None:
                        act.wait_ge(moves[s], free)
                    act.wait_ge(raw_loaded[s], 16 * j + 16)
                    act.activation(raw_pos[:, s, :], pos["dst"][:, bass.ds((2 * j + s) * GC, GC)], ACT.Copy)\
                        .then_inc(pos_ready, 1)

                def all_places():
                    for s in range(2):
                        place(0, s, None)
                    with act.Fori(1, EC // GC // 2) as j:
                        for s in range(2):
                            place(j, s, 16 * GC * j)
                if_moved(act, all_places)

            @block.gpsimd
            def _(pool):
                if_moved(pool, lambda: scatter_columns(pool, "dst", rec_dst, raw_pos, raw_rec, pos_ready, moves))


def scatter_columns(pool, tag, rec, places, recs, ready, scattered):
    turn = Count(pool, f"{tag}_turn", 0)
    with pool.Fori(0, EC // GC // 2):
        for s in range(2):
            turn.up(1)
            pool.wait_ge(ready, 1)
            pool.wait_ge(ready, turn.reg)
            for q in range(GC):
                pool.indirect_dma_start(rec, bass.IndirectOffsetOnAxis(ap=places[:, s, q:q + 1], axis=0),
                                        recs[:, s, q, :], None).then_inc(scattered[s], 16)
    for s in range(2):
        pool.wait_ge(scattered[s], 16 * EC // 2)



def edge_loop(net, tag, kind, rec, sched, table, acc, C):
    nc = net.nc
    W = rec.shape[1]
    erow, trow, tbase = sched
    MC = {"plain": C - D, "conv": C, "cross": C}[kind]
    dist, vec = {"plain": (5, 2), "conv": (2, 3), "cross": (2, 3)}[kind]
    with net.stage() as c:
        recs = net.sb(f"{tag}_recs", [P, SL, JB, W], F32, c)
        far = net.sb(f"{tag}_far", [P, SL, JB], I32, c)
        rows = net.sb(f"{tag}_rows", [P, SL, JB, TW], F32, c)
        rel = net.sb(f"{tag}_rel", [P, 2, JB], F32, c)
        hot = net.sb(f"{tag}_hot", [P, 2, JB, P], F32, c)
        msg = net.sb(f"{tag}_msg", [P, 2, JB, MC], F32, c)
        prod = net.sb(f"{tag}_prod", [P, 3, JB, VD], F32, c)
        agg_ps = [net.ps(f"{tag}_agg_ps{s}", [P, 512], c) for s in range(2)]
        if kind == "conv":
            scaled = net.sb(f"{tag}_scaled", [P, 2, JB, D], F32, c)
            w0f = net.sb(f"{tag}_w0f", [P, JB, S0], F32, c)
            dot = net.sb(f"{tag}_dot", [P, JB, V0], F32, c)
            recT = net.sb(f"{tag}_recT", [JB * W, 2, P], F32, c)
            hidT = net.sb(f"{tag}_hidT", [2 * S0, 2, JB // 2, P], F32, c)
            recT_ps = net.ps(f"{tag}_recT_ps", [JB * W, P], c)
            hid_ps = net.ps(f"{tag}_hid_ps", [2 * S0, JB // 2, P], c)
            w_ps = [net.ps(f"{tag}_w_ps{s}", [P, 2, 2, 256], c) for s in range(2)]

        acc_zero = net.sem(f"{tag}_acc_zero", c)
        rec_loaded = [net.sem(f"{tag}_rec_loaded{s}", c) for s in range(SL)]
        far_ready = net.sem(f"{tag}_far_ready", c)
        gathered = [net.sem(f"{tag}_gathered{s}", c) for s in range(SL)]
        rel_ready = net.sem(f"{tag}_rel_ready", c)
        hot_ready = net.sem(f"{tag}_hot_ready", c)
        prod_ready = net.sem(f"{tag}_prod_ready", c)
        act_msgs = net.sem(f"{tag}_act_msgs", c)
        dve_msgs = net.sem(f"{tag}_dve_msgs", c)
        agg_done = net.sem(f"{tag}_agg_done", c)
        acc_added = net.sem(f"{tag}_acc_added", c)
        if kind == "conv":
            recT_done = net.sem(f"{tag}_recT_done", c)
            recT_ready = net.sem(f"{tag}_recT_ready", c)
            hid_done = net.sem(f"{tag}_hid_done", c)
            hid_ready = net.sem(f"{tag}_hid_ready", c)
            w_done = net.sem(f"{tag}_w_done", c)
        block = c.enter_context(nc.Block())

        def steps(eng, body):
            for u in range(SL):
                body(0, u)
            with eng.Fori(1, NJ - 1) as j:
                for u in range(SL):
                    body(j, u)
            for u in range(SL):
                body(NJ - 1, u)

        def has(j, u, d):
            return not isinstance(j, int) or 0 <= SL * j + u + d < NI

        @block.sync
        def _(sp):
            def load(j, u):
                i = SL * j + u
                if has(j, u, -SL):
                    sp.wait_ge(agg_done, i - SL + 1)
                e = sp.value_load(erow[0:1, bass.ds(i, 1)], min_val=0, max_val=E)
                sp.dma_start(recs[:, u, :, :], rec[bass.ds(e, GE), :].rearrange("(p j) w -> p j w", j=JB))\
                    .then_inc(rec_loaded[u], 16)
            steps(sp, load)

        @block.gpsimd
        def _(pool):
            this, past = Count(pool, f"{tag}_this", 0), Count(pool, f"{tag}_past", 0)

            def gather(j, u):
                i = SL * j + u
                this.up(1)
                if has(j, u, -SL):
                    past.up(1)
                pool.wait_ge(far_ready, 1)
                pool.wait_ge(far_ready, this.reg)
                if has(j, u, -SL):
                    pool.wait_ge(agg_done, past.reg)
                for q in range(JB):
                    pool.indirect_dma_start(rows[:, u, q, :], None, table[0:NT * P, :],
                                            bass.IndirectOffsetOnAxis(ap=far[:, u, q:q + 1], axis=0))\
                        .then_inc(gathered[u], 16)
            steps(pool, gather)

        @block.scalar
        def _(act):
            AHEAD = 2

            def convert(j, u):
                act.wait_ge(rec_loaded[u], 16 * j + 16)
                act.activation(far[:, u, :], recs[:, u, :, 1], ACT.Copy).then_inc(far_ready, 1)

            def attributes(j, u):
                i = SL * j + u
                act.wait_ge(recT_done, i + 1)
                if has(j, u, -2):
                    act.wait_ge(hid_done, i - 1)
                act.activation(recT[:, u % 2, :], recT_ps[:, :], ACT.Copy).then_inc(recT_ready, 1)

            def hidden(j, u):
                i = SL * j + u
                act.wait_ge(hid_done, i + 1)
                if has(j, u, -2):
                    act.wait_ge(w_done, i - 1)
                act.activation(hidT[:, u % 2, :, :], hid_ps[:, :, :], ACT.Silu).then_inc(hid_ready, 1)

            def scale_rows(j, u):
                i = SL * j + u
                act.wait_ge(gathered[u], 64 * j + 64)
                if has(j, u, -2):
                    act.wait_ge(dve_msgs if kind == "conv" else agg_done, i - 1)
                for q in range(JB):
                    by = recs[:, u, q, dist:dist + 1]
                    if kind == "plain":
                        last = act.activation(msg[:, u % 2, q, 0:D], rows[:, u, q, 0:D], ACT.Copy, scale=by)
                    elif kind == "conv":
                        last = act.activation(scaled[:, u % 2, q, :], rows[:, u, q, 0:D], ACT.Copy, scale=by)
                    else:
                        act.activation(msg[:, u % 2, q, 0:S0], rows[:, u, q, 0:S0], ACT.Copy, scale=by)
                        last = act.activation(
                            msg[:, u % 2, q, VD:4 * VD].rearrange("p (k f) -> p k f", k=3)[:, :, 0:V0],
                            rows[:, u, q, S0:D].rearrange("p (f k) -> p k f", k=3), ACT.Copy, scale=by)
                last.then_inc(act_msgs, 1)

            for u in range(AHEAD):
                convert(0, u)
            if kind == "conv":
                for u in range(AHEAD):
                    attributes(0, u)
                    hidden(0, u)
                scale_rows(0, 0)
                attributes(0, 2)

            def body(j, u):
                ahead = (j + (u + AHEAD) // SL, (u + AHEAD) % SL)
                coming = has(j, u, AHEAD)
                if coming:
                    convert(*ahead)
                if kind == "conv":
                    if has(j, u, 1):
                        scale_rows(j + (u + 1) // SL, (u + 1) % SL)
                    if coming:
                        hidden(*ahead)
                    if has(j, u, 3):
                        attributes(j + (u + 3) // SL, (u + 3) % SL)
                else:
                    scale_rows(j, u)
            steps(act, body)

        @block.vector
        def _(dve):
            dve.memset(acc[:, :, :], 0.0).then_inc(acc_zero, 1)
            if kind == "conv":
                dve.memset(msg[:, :, :, 4 * VD:C], 1.0)
            dve.wait_ge(acc_zero, 1)

            def add_up(j, u):
                i = SL * j + u
                t = dve.value_load(trow[0:1, bass.ds(i, 1)], min_val=0, max_val=NT)
                dve.wait_ge(agg_done, i + 1)
                if has(j, u, -1):
                    dve.wait_ge(acc_added, i)
                to = acc[:, bass.ds(t, 1), :].rearrange("p a b -> p (a b)")[:, 0:C]
                dve.tensor_tensor(to, to, agg_ps[u % 2][:, 0:C], ALU.add).then_inc(acc_added, 1)

            def relate(j, u):
                i = SL * j + u
                dve.wait_ge(rec_loaded[u], 16 * j + 16)
                dve.tensor_scalar(rel[:, u % 2, :], recs[:, u, :, 0], tbase[:, bass.ds(i, 1)], None, ALU.subtract)\
                    .then_inc(rel_ready, 1)

            def body(j, u):
                i, m = SL * j + u, u % 2
                if not has(j, u, -1):
                    relate(j, u)
                if has(j, u, -2):
                    dve.wait_ge(agg_done, i - 1)
                dve.wait_ge(rel_ready, i + 1)
                dve.tensor_tensor(hot[:, m, :, :], net.ramp[:, :].unsqueeze(1).broadcast_to([P, JB, P]),
                                  rel[:, m, :].unsqueeze(2).broadcast_to([P, JB, P]), ALU.is_equal)\
                    .then_inc(hot_ready, 1)
                dve.wait_ge(gathered[u], 64 * j + 64)
                r = rows[:, u, :, :]
                out = msg[:, m, :, :]
                e3 = recs[:, u, :, vec:vec + 3]
                v = r[:, :, S0:D].rearrange("p j (f k) -> p j f k", k=3)
                if kind == "plain":
                    pv = prod[:, 0, :, :].rearrange("p j (f k) -> p j f k", k=3)
                    dve.tensor_tensor(pv, v, e3.unsqueeze(2).broadcast_to([P, JB, V0, 3]), ALU.mult)\
                        .then_inc(prod_ready, 1)
                    dve.tensor_tensor(out[:, :, D + V0:D + V0 + VD].rearrange("p j (f k) -> p j f k", k=3),
                                      r[:, :, D:TW].unsqueeze(3).broadcast_to([P, JB, V0, 3]),
                                      e3.unsqueeze(2).broadcast_to([P, JB, V0, 3]), ALU.mult)
                    dve.wait_ge(prod_ready, i + 1)
                    dve.tensor_reduce(out[:, :, D:D + V0], pv, AXX, ALU.add).then_inc(dve_msgs, 1)
                elif kind == "cross":
                    vk = r[:, :, S0:D].rearrange("p j (f k) -> p j k f", k=3)
                    for b in range(3):
                        last = dve.tensor_tensor(prod[:, b, :, :].rearrange("p j (k f) -> p j k f", k=3), vk,
                                                 e3[:, :, b:b + 1].unsqueeze(3).broadcast_to([P, JB, 3, V0]), ALU.mult)
                    last.then_inc(prod_ready, 1)
                    o3 = out[:, :, VD:4 * VD].rearrange("p j (k f) -> p j k f", k=3)
                    dve.tensor_tensor(o3[:, :, :, V0:2 * V0], r[:, :, D:TW].unsqueeze(2).broadcast_to([P, JB, 3, V0]),
                                      e3.unsqueeze(3).broadcast_to([P, JB, 3, V0]), ALU.mult)

                    def p(a, b):
                        return prod[:, b, :, a * V0:(a + 1) * V0]
                    dve.wait_ge(prod_ready, 2 * i + 1)
                    dve.tensor_tensor(out[:, :, S0:VD], p(0, 0), p(1, 1), ALU.add).then_inc(prod_ready, 1)
                    for k in range(3):
                        a, b = (k + 1) % 3, (k + 2) % 3
                        dve.tensor_tensor(o3[:, :, k, 2 * V0:3 * V0], p(a, b), p(b, a), ALU.subtract)
                    dve.wait_ge(prod_ready, 2 * i + 2)
                    dve.tensor_tensor(out[:, :, S0:VD], out[:, :, S0:VD], p(2, 2), ALU.add).then_inc(dve_msgs, 1)
                else:
                    wv = w_ps[m][:, :, :, :].rearrange("p a b w -> p (a b) w")
                    pv = prod[:, 0, :, :].rearrange("p j (f k) -> p j f k", k=3)
                    dve.tensor_tensor(pv, v, e3.unsqueeze(2).broadcast_to([P, JB, V0, 3]), ALU.mult)\
                        .then_inc(prod_ready, 1)
                    dve.wait_ge(w_done, i + 1)
                    dve.tensor_tensor(w0f[:, :, :], wv[:, :, S0:2 * S0], r[:, :, 0:S0], ALU.mult)
                    dve.wait_ge(prod_ready, 3 * i + 1)
                    dve.tensor_reduce(dot[:, :, :], pv, AXX, ALU.add).then_inc(prod_ready, 1)
                    dve.wait_ge(act_msgs, i + 1)
                    sc = scaled[:, m, :, :]
                    dve.tensor_tensor(out[:, :, 0:S0], wv[:, :, 0:S0], sc[:, :, 0:S0], ALU.mult)
                    o3 = out[:, :, VD:4 * VD].rearrange("p j (k f) -> p j k f", k=3)
                    dve.tensor_tensor(o3[:, :, :, S0:VD], wv[:, :, 2 * S0:2 * S0 + V0].unsqueeze(2).broadcast_to([P, JB, 3, V0]),
                                      sc[:, :, S0:D].rearrange("p j (f k) -> p j k f", k=3), ALU.mult)
                    dve.wait_ge(prod_ready, 3 * i + 2)
                    dve.tensor_tensor(out[:, :, S0:VD], wv[:, :, 2 * S0 + V0:TW], dot[:, :, :], ALU.mult)\
                        .then_inc(prod_ready, 1)
                    dve.tensor_tensor(o3[:, :, :, 0:S0], w0f[:, :, :].unsqueeze(2).broadcast_to([P, JB, 3, S0]),
                                      e3.unsqueeze(3).broadcast_to([P, JB, 3, S0]), ALU.mult).then_inc(dve_msgs, 1)
                if has(j, u, 1):
                    relate(j + (u + 1) // SL, (u + 1) % SL)
                if has(j, u, -1):
                    add_up(j + (u - 1) // SL, (u - 1) % SL)
            steps(dve, body)
            add_up(NJ - 1, SL - 1)

        @block.tensor
        def _(pe):
            def attributes(j, u):
                i = SL * j + u
                pe.wait_ge(rec_loaded[u], 16 * j + 16)
                if has(j, u, -1):
                    pe.wait_ge(recT_ready, i)
                pe.transpose(recT_ps[:, :], recs[:, u, :, :].rearrange("p j w -> p (j w)"), net.ident[:, :])\
                    .then_inc(recT_done, 1)

            def hidden(j, u):
                i = SL * j + u
                pe.wait_ge(recT_ready, i + 1)
                if has(j, u, -1):
                    pe.wait_ge(hid_ready, i)
                for h in range(JB // 2):
                    last = pe.matmul(hid_ps[:, h, :], net.wfc1[:, h, :], recT[:, u % 2, :], start=True, stop=True)
                last.then_inc(hid_done, 1)

            def weights(j, u):
                i = SL * j + u
                pe.wait_ge(hid_ready, i + 1)
                if has(j, u, -2):
                    pe.wait_ge(dve_msgs, i - 1)
                for q in (0, 2, 1, 3):
                    half = slice(q // 2 * S0, (q // 2 + 1) * S0)
                    last = pe.matmul(w_ps[u % 2][:, q // 2, q % 2, 0:TW], hidT[half, u % 2, q % 2, :],
                                     net.wfc2[half, :], start=True, stop=True)
                last.then_inc(w_done, 1)

            if kind == "conv":
                for u in range(2):
                    attributes(0, u)
                    hidden(0, u)
                weights(0, 0)
                attributes(0, 2)

            def body(j, u):
                i, m = SL * j + u, u % 2
                if kind == "conv" and has(j, u, 1):
                    weights(j + (u + 1) // SL, (u + 1) % SL)
                if kind == "conv" and has(j, u, 2):
                    hidden(j + (u + 2) // SL, (u + 2) % SL)
                pe.wait_ge(hot_ready, i + 1)
                if has(j, u, -2):
                    pe.wait_ge(acc_added, i - 1)
                if kind == "plain":
                    pe.wait_ge(gathered[u], 64 * j + 64)
                    for q in range(JB):
                        pe.matmul(agg_ps[m][:, 0:D], hot[:, m, q, :], rows[:, u, q, 0:D], start=(q == 0),
                                  stop=False, skip_group_check=True)
                        if q == 0:
                            pe.wait_ge(act_msgs, i + 1)
                            pe.wait_ge(dve_msgs, i + 1)
                        last = pe.matmul(agg_ps[m][:, D:C], hot[:, m, q, :], msg[:, m, q, :], start=False,
                                         stop=(q == JB - 1), skip_group_check=True)
                else:
                    pe.wait_ge(act_msgs, i + 1)
                    pe.wait_ge(dve_msgs, i + 1)
                    for q in range(JB):
                        last = pe.matmul(agg_ps[m][:, 0:C], hot[:, m, q, :], msg[:, m, q, 0:C], start=(q == 0),
                                         stop=(q == JB - 1))
                last.then_inc(agg_done, 1)
                if kind == "conv" and has(j, u, 3):
                    attributes(j + (u + 3) // SL, (u + 3) % SL)
            steps(pe, body)



def outer_schedule(lay):
    w = {k: v[0] for k, v in lay["chunks"].items()}
    plan = []
    for b in range(NXB):
        if b < 4:
            first = [(2 * v + uu, w["ss"][:, 2 * b + uu, v, :], "ab"[uu]) for v in range(4) for uu in range(2)]
            second = [(4 * k + 2 * vi + uu, w["sv"][:, 2 * b + uu, vi, :], ("cd"[uu], k))
                      for vi in range(2) for uu in range(2) for k in range(3)]
        else:
            k, ub = (b - 4) // 2, 2 * ((b - 4) % 2)
            first = [(2 * v + uu, w["vs"][:, ub + uu, v, :], ("cd"[uu], k)) for v in range(4) for uu in range(2)]
            second = [(2 * vi + uu, w["vv"][:, ub + uu, vi, :], "ab"[uu]) for vi in range(2) for uu in range(2)]
        plan += [first, second]
    return plan


def outer_stage(net, tag, nxt, lay, prep, acc, C, table):
    nc = net.nc
    plan = outer_schedule(lay)
    NP_ = len(plan)
    with net.stage() as c:
        agg = net.sb(f"{tag}_agg", [P, GT, C], F32, c)
        xin = net.sb(f"{tag}_xin", [P, GT, D], F32, c)
        xnew = net.sb(f"{tag}_xnew", [P, 2, GT, D], F32, c)
        usum = net.sb(f"{tag}_usum", [P, 3, GN], F32, c)
        xa = net.sb(f"{tag}_xa", [P, 2, 3, GN], F32, c)
        arep = net.sb(f"{tag}_arep", [P, 2, NXB, GN], F32, c)
        even = net.sb(f"{tag}_even", [P, 2, 8, GN], F32, c)
        odd = net.sb(f"{tag}_odd", [P, 12, GN], F32, c)
        y = net.sb(f"{tag}_y", [P, GT, D], F32, c)
        stats = net.sb(f"{tag}_stats", [P, GT, 6], F32, c)
        mv = net.sb(f"{tag}_mv", [P, GT, 2], F32, c)
        sd = net.sb(f"{tag}_sd", [P, GT], F32, c)
        rstd = net.sb(f"{tag}_rstd", [P, GT], F32, c)
        nT = net.sb(f"{tag}_nT", [P, 4, GN], F32, c)
        trow = net.sb(f"{tag}_trow", [P, GT, TW], F32, c)
        aggT = nT[:, 0:2, :]
        vecT = net.sb(f"{tag}_vecT", [VD, 3, GN], F32, c)
        t_ps, x_ps = net.ps(f"{tag}_t_ps", [P, 512], c), net.ps(f"{tag}_x_ps", [P, 512], c)
        v_ps = [net.ps(f"{tag}_v_ps{s}", [P, 512], c) for s in range(2)]
        rep_ps = [net.ps(f"{tag}_rep_ps{s}", [P, 2, GN], c) for s in range(2)]
        us_ps, uv_ps = net.ps(f"{tag}_us_ps", [P, 512], c), net.ps(f"{tag}_uv_ps", [P, 2, GN], c)
        next_ps = [x_ps, t_ps]

        loaded = net.sem(f"{tag}_loaded", c)
        zeroed = net.sem(f"{tag}_zeroed", c)
        transposed = net.sem(f"{tag}_transposed", c)
        opsT_ready = net.sem(f"{tag}_opsT_ready", c)
        lin_done = net.sem(f"{tag}_lin_done", c)
        a_ready = net.sem(f"{tag}_a_ready", c)
        arep_done = net.sem(f"{tag}_arep_done", c)
        arep_ready = net.sem(f"{tag}_arep_ready", c)
        xrep_done = net.sem(f"{tag}_xrep_done", c)
        prod_ready = net.sem(f"{tag}_prod_ready", c)
        prod_used = net.sem(f"{tag}_prod_used", c)
        usum_ready = net.sem(f"{tag}_usum_ready", c)
        nat_done = net.sem(f"{tag}_nat_done", c)
        y_ready = net.sem(f"{tag}_y_ready", c)
        stats_ready = net.sem(f"{tag}_stats_ready", c)
        var_ready = net.sem(f"{tag}_var_ready", c)
        sd_ready = net.sem(f"{tag}_sd_ready", c)
        rstd_ready = net.sem(f"{tag}_rstd_ready", c)
        x_new = net.sem(f"{tag}_x_new", c)
        new_transposed = net.sem(f"{tag}_new_transposed", c)
        nT_ready = net.sem(f"{tag}_nT_ready", c)
        next_done = net.sem(f"{tag}_next_done", c)
        row_ready = net.sem(f"{tag}_row_ready", c)
        base_ready = net.sem(f"{tag}_base_ready", c)
        stored = net.sem(f"{tag}_stored", c)
        block = c.enter_context(nc.Block())
        NJG = NG // 2
        assert NG % 2 == 1

        def groups(eng, body):
            body(0, 0)
            body(0, 1)
            with eng.Fori(1, NJG) as j:
                body(j, 0)
                body(j, 1)
            body(NJG, 0)

        def has(j, u, d):
            return not isinstance(j, int) or 0 <= 2 * j + u + d < NG

        def at(j, u, d):
            return j + (u + d) // 2, (u + d) % 2

        def v_of(ap):
            return ap.rearrange("p (f k) -> p k f", k=3)

        @block.sync
        def _(sp):
            def load(j, u):
                g = 2 * j + u
                if has(j, u, -1):
                    sp.wait_ge(transposed, g)
                sp.dma_start(xin[:, :, :], net.xres[:, bass.ds(GT * g, GT), :]).then_inc(loaded, 16)
                sp.dma_start(agg[:, :, :], acc[:, bass.ds(GT * g, GT), 0:C]).then_inc(loaded, 16)

            def store(j, u):
                g = 2 * j + u
                sp.wait_ge(row_ready, g + 1)
                sp.dma_start(table[bass.ds(g * GN, GN), :].rearrange("(h p) w -> p h w", p=P),
                             trow[:, :, :]).then_inc(stored, 16)

            load(0, 0)

            def body(j, u):
                if has(j, u, 1):
                    load(*at(j, u, 1))
                if has(j, u, -1):
                    store(*at(j, u, -1))
            groups(sp, body)
            store(NJG, 0)
            sp.wait_ge(stored, 16 * NG)

        @block.tensor
        def _(pe):
            def mm(to, lhsT, rhs, start=True, stop=True, **kw):
                return pe.matmul(to, lhsT, rhs, start=start, stop=stop, **kw)

            def transposes(j, u):
                g = 2 * j + u
                pe.wait_ge(loaded, 32 * g + 32)
                if has(j, u, -1):
                    pe.wait_ge(arep_ready, NXB // 2 * g)
                if has(j, u, -3):
                    pe.wait_ge(row_ready, g - 2)
                    if nxt == "conv":
                        pe.wait_ge(base_ready, g - 2)
                ident = net.ident[:, :]
                for h in range(GT):
                    n = slice(h * P, (h + 1) * P)
                    ag = agg[:, h, :]
                    for b in range(2):
                        mm(t_ps[S0 * b:S0 * (b + 1), n], ag[:, D * b:D * b + S0], ident)
                    pe.transpose(t_ps[0:V0, GN + h * P:GN + (h + 1) * P], ag[:, 2 * D:2 * D + V0], ident)
                    vecs = [ag[:, S0:D], ag[:, D + S0:2 * D], ag[:, 2 * D + V0:2 * D + V0 + VD]]
                    for b, ap in enumerate(vecs):
                        for k in range(3):
                            o = (k % 2) * GN + h * P
                            mm(v_ps[k // 2][V0 * b:V0 * (b + 1), o:o + P], v_of(ap)[:, k, :], ident)
                    xu = xin[:, h, :]
                    xv = v_of(xu[:, S0:D])
                    mm(x_ps[0:S0, n], xu[:, 0:S0], ident)
                    mm(x_ps[S0:S0 + V0, n], xv[:, 0, :], ident)
                    mm(x_ps[S0 + V0:P, n], xv[:, 1, :], ident)
                    last = pe.transpose(x_ps[0:V0, GN + h * P:GN + (h + 1) * P], xv[:, 2, :], ident)
                last.then_inc(transposed, 1)

            def linear(j, u):
                g = 2 * j + u
                pe.wait_ge(opsT_ready, g + 1)
                mm(t_ps[0:S0, 0:GN], lay["m0"], aggT[:, 0, :], stop=False)
                mm(t_ps[0:S0, 0:GN], lay["mdot"], aggT[0:V0, 1, :], start=False)
                mm(t_ps[S0:S0 + V0, 0:GN], lay["m1"], vecT[:, 0, :])
                mm(t_ps[S0 + V0:P, 0:GN], lay["m1"], vecT[:, 1, :])
                mm(t_ps[V0:2 * V0, GN:2 * GN], lay["m1"], vecT[:, 2, :]).then_inc(lin_done, 1)

            def a_operands(j, u, banks):
                g = 2 * j + u
                for n in banks:
                    if n == 0:
                        pe.wait_ge(a_ready, g + 1)
                    if n >= 2:
                        pe.wait_ge(arep_ready, NXB // 2 * g + n - 1)
                    for i in range(2):
                        m = 2 * n + i
                        part, sel = (1, m) if m < 8 else (2, m - 6)
                        last = mm(v_ps[n % 2][:, i * GN:(i + 1) * GN], net.sel_v[:, sel, :], xa[:, u, part, :])
                    last.then_inc(arep_done, 1)

            def x_operands(j, u, b):
                g = 2 * j + u
                if b >= 2 or has(j, u, -1):
                    pe.wait_ge(prod_ready, NP_ * g + 2 * b - 2)
                for i in range(2):
                    m = 2 * b + i
                    part, sel = (0, m) if m < 16 else (2, m - 16)
                    last = mm(rep_ps[b % 2][:, i, :], net.sel_u[:, sel, :], xa[:, u, part, :])
                last.then_inc(xrep_done, 1)

            where = {"a": (us_ps[0:S0, 0:GN], ("s", 0)), "b": (us_ps[S0:P, 0:GN], ("s", 1))}
            for k in range(3):
                where["c", k] = (uv_ps[V0 * k:V0 * (k + 1), 0, :], ("v", k))
                where["d", k] = (uv_ps[V0 * (k + 1):V0 * (k + 2), 1, :], ("v", k + 1))
            opened = {where[x][1] for x in ("a", ("c", 0), ("c", 1), ("c", 2))}
            firsts, lasts = {}, {}
            for n, chunks in enumerate(plan):
                for m, (_, _, region) in enumerate(chunks):
                    quarter = where[region][1]
                    if quarter not in opened:
                        firsts.setdefault(quarter, (n, m))
                    lasts[quarter] = (n, m)

            def sum_up(j, u, b):
                g = 2 * j + u
                kw = {"skip_group_check": True}
                if b == 0:
                    if has(j, u, -1):
                        pe.wait_ge(usum_ready, g)
                    mm(where["a"][0], lay["l0"], xa[:, u, 0, :], stop=False, **kw)
                    for k in range(3):
                        mm(where["c", k][0], lay["l1"][:, k, :], xa[:, u, 2 if k == 2 else 0, :], stop=False, **kw)
                for part in range(2):
                    n = 2 * b + part
                    pe.wait_ge(prod_ready, NP_ * g + n + 1)
                    for m, (chunk, w, region) in enumerate(plan[n]):
                        to, quarter = where[region]
                        last = mm(to, w, (odd[:, chunk, :] if part else even[:, b % 2, chunk, :]),
                                  start=firsts.get(quarter) == (n, m), stop=lasts[quarter] == (n, m), **kw)
                    last.then_inc(prod_used, 1)

            def natural(j, u):
                g = 2 * j + u
                if has(j, u, -1):
                    pe.wait_ge(row_ready, g)
                    if nxt == "conv":
                        pe.wait_ge(base_ready, g)
                pe.wait_ge(usum_ready, g + 1)
                for h in range(GT):
                    n = slice(h * P, (h + 1) * P)
                    mm(x_ps[:, D * h:D * h + S0], usum[:, 0, n], net.merge[:, :])
                    mm(x_ps[:, D * h + S0:D * (h + 1)], usum[:, 1, n], net.ident[:, 0:VD], stop=False)
                    last = mm(x_ps[:, D * h + S0:D * (h + 1)], usum[:, 2, n], net.ident[:, V0:P], start=False)
                last.then_inc(nat_done, 1)

            def turn_new(j, u):
                g = 2 * j + u
                if has(j, u, 2):
                    pe.wait_ge(arep_ready, NXB // 2 * (g + 2) + 3)
                pe.wait_ge(x_new, g + 1)
                for h in range(GT):
                    xv = v_of(xnew[:, u, h, S0:D])
                    mm(v_ps[0][0:S0, h * P:(h + 1) * P], xnew[:, u, h, 0:S0], net.ident[:, :])
                    for k in range(3):
                        o = ((k + 1) % 2) * GN + h * P
                        last = pe.transpose(v_ps[(k + 1) // 2][0:V0, o:o + P], xv[:, k, :], net.ident[:, :])
                last.then_inc(new_transposed, 1)

            def next_rows(j, u):
                g = 2 * j + u
                pe.wait_ge(nT_ready, g + 1)
                for h in range(GT):
                    n = slice(h * P, (h + 1) * P)
                    if nxt == "conv":
                        mm(next_ps[h][:, 192:320], nT[0:S0, 0, n], prep["ws"])
                        for k in range(3):
                            last = mm(next_ps[h][:, 320 + 64 * k:384 + 64 * k], nT[0:V0, k + 1, n], prep["wv"])
                    else:
                        last = mm(next_ps[h][:, 192:224], nT[0:S0, 0, n], prep["ws"])
                last.then_inc(next_done, 1)

            pe.wait_ge(zeroed, 1)
            transposes(0, 0)
            linear(0, 0)
            a_operands(0, 0, range(NXB // 2))

            def body(j, u):
                past, coming = has(j, u, -1), has(j, u, 1)
                last, after = at(j, u, -1), at(j, u, 1)
                for b in range(NXB):
                    x_operands(j, u, b)
                    if b >= 1:
                        sum_up(j, u, b - 1)
                    elif past:
                        sum_up(*last, NXB - 1)
                    if b == 1 and coming:
                        transposes(*after)
                    if b == 2 and coming:
                        linear(*after)
                    if b == 3 and past:
                        natural(*last)
                    if b in (3, 4, 5) and coming:
                        a_operands(*after, [b - 3])
                    if b == 6 and past:
                        turn_new(*last)
                    if b == 7 and past:
                        next_rows(*last)
                    if b in (7, 8) and coming:
                        a_operands(*after, [b - 4])
            groups(pe, body)
            sum_up(NJG, 0, NXB - 1)
            natural(NJG, 0)
            turn_new(NJG, 0)
            next_rows(NJG, 0)

        @block.scalar
        def _(act):
            def copy(to, frm, **kw):
                return act.activation(to, frm, ACT.Copy, **kw)

            def front(j, u):
                g = 2 * j + u
                act.wait_ge(transposed, g + 1)
                copy(aggT[:, 0, :], t_ps[:, 0:GN])
                copy(aggT[0:V0, 1, :], t_ps[0:V0, GN:2 * GN])
                copy(vecT[:, 0:2, :], v_ps[0][0:VD, :].rearrange("p (k n) -> p k n", k=2))
                copy(vecT[:, 2, :], v_ps[1][0:VD, 0:GN])
                if has(j, u, -2):
                    act.wait_ge(prod_used, NP_ * (g - 1))
                copy(xa[:, u, 0, :], x_ps[:, 0:GN])
                copy(xa[0:V0, u, 2, :], x_ps[0:V0, GN:2 * GN]).then_inc(opsT_ready, 1)
                act.wait_ge(lin_done, g + 1)
                copy(xa[:, u, 1, :], t_ps[:, 0:GN])
                copy(xa[V0:2 * V0, u, 2, :], t_ps[V0:2 * V0, GN:2 * GN]).then_inc(a_ready, 1)

            def a_operands(j, u, banks):
                g = 2 * j + u
                if has(j, u, -2):
                    act.wait_ge(prod_ready, NP_ * (g - 1))
                for n in banks:
                    act.wait_ge(arep_done, NXB // 2 * g + n + 1)
                    copy(arep[:, u, 2 * n:2 * n + 2, :], v_ps[n % 2][:, :].rearrange("p (k n) -> p k n", k=2))\
                        .then_inc(arep_ready, 1)

            def finish(j, u):
                g = 2 * j + u
                act.wait_ge(prod_used, NP_ * (g + 1))
                if has(j, u, -1):
                    act.wait_ge(nat_done, g)
                copy(usum[:, 0, :], us_ps[:, 0:GN])
                copy(usum[0:VD, 1, :], uv_ps[0:VD, 0, :])
                copy(usum[V0:2 * V0, 2, :], uv_ps[V0:2 * V0, 1, :])
                copy(usum[2 * V0:P, 2, :], uv_ps[2 * V0:P, 1, :]).then_inc(usum_ready, 1)

            def deviation(j, u):
                g = 2 * j + u
                act.wait_ge(var_ready, g + 1)
                if has(j, u, -1):
                    act.wait_ge(rstd_ready, g)
                act.activation(sd[:, :], mv[:, :, 1], ACT.Sqrt, bias=net.eps[:, 0:1]).then_inc(sd_ready, 1)

            def prepare(j, u):
                g = 2 * j + u
                act.wait_ge(new_transposed, g + 1)
                copy(nT[0:S0, 0, :], v_ps[0][0:S0, 0:GN])
                copy(nT[0:V0, 1, :], v_ps[0][0:V0, GN:2 * GN])
                copy(nT[0:V0, 2:4, :], v_ps[1][0:V0, :].rearrange("p (k n) -> p k n", k=2)).then_inc(nT_ready, 1)
                if has(j, u, -1):
                    act.wait_ge(stored, 16 * g)
                act.wait_ge(next_done, g + 1)
                for h in range(GT):
                    row, q = trow[:, h, :], next_ps[h]
                    if nxt == "conv":
                        by = net.nodea[:, bass.ds(GT * g + h, 1)]
                        copy(row[:, 0:S0], q[:, 192:256], scale=by)
                        last = copy(v_of(row[:, S0:D]),
                                    q[:, 320:512].rearrange("p (k h f) -> p k h f", k=3, h=2)[:, :, 0, :], scale=by)
                    else:
                        copy(row[:, 0:D], xnew[:, u, h, :])
                        last = copy(row[:, D:TW], q[:, 192:224])
                last.then_inc(row_ready, 1)

            act.wait_ge(zeroed, 1)
            front(0, 0)
            a_operands(0, 0, range(NXB // 2))

            def body(j, u):
                past, coming = has(j, u, -1), has(j, u, 1)
                last, after = at(j, u, -1), at(j, u, 1)
                if past:
                    finish(*last)
                if coming:
                    front(*after)
                    a_operands(*after, [0, 1])
                if past:
                    deviation(*last)
                if coming:
                    a_operands(*after, [2])
                if past:
                    prepare(*last)
                if coming:
                    a_operands(*after, [3, 4])
            groups(act, body)
            finish(NJG, 0)
            deviation(NJG, 0)
            prepare(NJG, 0)

        @block.vector
        def _(dve):
            counts = Count(dve, f"{tag}_counts", 0)
            dve.memset(xa[2 * V0:P, :, 2, :], 0.0)
            dve.memset(usum[:, 1:3, :], 0.0)
            if nxt == "conv":
                dve.memset(trow[:, :, D:TW], 0.0)
            dve.memset(stats[:, :, :], 0.0).then_inc(zeroed, 1)

            def products(j, u, b):
                g = 2 * j + u
                if b == 0:
                    dve.wait_ge(arep_ready, NXB // 2 * (g + 1))
                dve.wait_ge(xrep_done, NXB * g + b + 1)
                x2 = rep_ps[b % 2][:, :, :]
                if b < 4:
                    sets = [(0, 4), (4, 6)]
                else:
                    sets = [(0, 4), (4 + 2 * ((b - 4) // 2), 2)]
                for part, (first, n) in enumerate(sets):
                    if part == 0 and (b >= 2 or has(j, u, -1)):
                        dve.wait_ge(prod_used, NP_ * g + 2 * b - 3)
                    if part == 1 and (b >= 1 or has(j, u, -1)):
                        dve.wait_ge(prod_used, NP_ * g + 2 * b)
                    to = (odd[:, 0:2 * n, :] if part else even[:, b % 2, 0:2 * n, :])\
                        .rearrange("p (v i) n -> p v i n", i=2)
                    dve.tensor_tensor(to, x2.unsqueeze(1).broadcast_to([P, n, 2, GN]),
                                      arep[:, u, first:first + n, :].unsqueeze(2).broadcast_to([P, n, 2, GN]),
                                      ALU.mult).then_inc(prod_ready, 1)

            def result(j, u):
                g = 2 * j + u
                dve.wait_ge(nat_done, g + 1)
                if has(j, u, -1):
                    dve.wait_ge(x_new, g)
                for h in range(GT):
                    x = net.xres[:, bass.ds(GT * g + h, 1), :].rearrange("p a f -> p (a f)")
                    ys = y[:, h, :]
                    dve.scalar_tensor_tensor(ys[:, 0:S0], x[:, 0:S0], 2.0, x_ps[:, D * h:D * h + S0], ALU.mult, ALU.add)
                    last = dve.scalar_tensor_tensor(
                        v_of(ys[:, S0:D]), v_of(x[:, S0:D]), 2.0,
                        x_ps[:, D * h + S0:D * (h + 1)].rearrange("p (k f) -> p k f", k=3), ALU.mult, ALU.add)
                last.then_inc(y_ready, 1)
                dve.wait_ge(y_ready, g + 1)
                for h in range(GT):
                    last = dve.bn_stats(stats[:, h, :], y[:, h, :])
                last.then_inc(stats_ready, 1)
                counts.up(1)
                dve.wait_ge(loaded, 16)
                dve.wait_ge(stats_ready, counts.reg)
                for h in range(GT):
                    last = dve.bn_aggr(mv[:, h, :], stats[:, h, :])
                last.then_inc(var_ready, 1)

            def norm(j, u):
                g = 2 * j + u
                dve.wait_ge(sd_ready, g + 1)
                dve.reciprocal(rstd[:, :], sd[:, :]).then_inc(rstd_ready, 1)
                dve.wait_ge(rstd_ready, g + 1)
                if has(j, u, -2):
                    dve.wait_ge(row_ready, g - 1)
                for h in range(GT):
                    to = net.xres[:, bass.ds(GT * g + h, 1), :].rearrange("p a f -> p (a f)")
                    dve.tensor_scalar(to, y[:, h, :], mv[:, h, 0:1], rstd[:, h:h + 1], ALU.subtract, ALU.mult)
                    last = dve.tensor_scalar(xnew[:, u, h, :], y[:, h, :], mv[:, h, 0:1], rstd[:, h:h + 1],
                                             ALU.subtract, ALU.mult)
                last.then_inc(x_new, 1)

            def base(j, u):
                g = 2 * j + u
                dve.wait_ge(row_ready, g + 1)
                for h in range(GT):
                    by, q, xn = net.nodea[:, bass.ds(GT * g + h, 1)], next_ps[h], xnew[:, u, h, :]
                    to = net.base[:, bass.ds(GT * g + h, 1), :].rearrange("p a f -> p (a f)")
                    dve.scalar_tensor_tensor(to[:, 0:S0], q[:, 256:320], by, xn[:, 0:S0], ALU.mult, ALU.add)
                    last = dve.scalar_tensor_tensor(
                        v_of(to[:, S0:D]), q[:, 320:512].rearrange("p (k h f) -> p k h f", k=3, h=2)[:, :, 1, :],
                        by, v_of(xn[:, S0:D]), ALU.mult, ALU.add)
                last.then_inc(base_ready, 1)

            def body(j, u):
                past = has(j, u, -1)
                for b in range(NXB):
                    products(j, u, b)
                    if b == 4 and past:
                        result(*at(j, u, -1))
                    if b == 5 and past:
                        norm(*at(j, u, -1))
                    if b == 8 and past and nxt == "conv":
                        base(*at(j, u, -1))
            groups(dve, body)
            result(NJG, 0)
            norm(NJG, 0)
            if nxt == "conv":
                base(NJG, 0)


def node_stage(net, tag, kind, nxt, lay, prep, acc, C, table, out):
    nc = net.nc
    with net.stage() as c:
        agg = net.sb(f"{tag}_agg", [P, 2, C], F32, c)
        xnew = net.sb(f"{tag}_xnew", [P, 2, D], F32, c)
        aggT = net.sb(f"{tag}_aggT", [P, 2 * P], F32, c)
        vecT = net.sb(f"{tag}_vecT", [VD, 3 * P], F32, c)
        if kind == "cross":
            wT = net.sb(f"{tag}_wT", [S0, 2 * P], F32, c)
            w_both = net.sb(f"{tag}_w_both", [VD, VD], F32, c)
            wT_ps = net.ps(f"{tag}_wT_ps", [P, 512], c)
            scal, vec, NS = w_both[:, 0:S0], w_both[:, S0:VD], S0
        else:
            scal, vec, NS = lay["scal"], lay["vec"], S0 + 1
        a_nat = net.sb(f"{tag}_a_nat", [P, 2, D], F32, c)
        y = net.sb(f"{tag}_y", [P, 2, D], F32, c)
        stats = net.sb(f"{tag}_stats", [P, 6], F32, c)
        mv = net.sb(f"{tag}_mv", [P, 2], F32, c)
        sd = net.sb(f"{tag}_sd", [P, 1], F32, c)
        rstd = net.sb(f"{tag}_rstd", [P, 1], F32, c)
        by_count = net.sb(f"{tag}_by_count", [P, NT], F32, c)
        alpha = net.sb(f"{tag}_alpha", [P, 1], F32, c)
        nT = net.sb(f"{tag}_nT", [S0, 4 * P], F32, c)
        trow = net.sb(f"{tag}_trow", [P, 2, TW], F32, c)
        aggT_ps = net.ps(f"{tag}_aggT_ps", [P, 512], c)
        vecT_ps = net.ps(f"{tag}_vecT_ps", [P, 512], c)
        lin_ps = [net.ps(f"{tag}_lin_ps{s}", [P, 512], c) for s in range(2)]
        next_ps = net.ps(f"{tag}_next_ps", [P, 512], c)
        nT_ps = net.ps(f"{tag}_nT_ps", [P, 512], c)
        loaded = [net.sem(f"{tag}_loaded{s}", c) for s in range(2)]
        agg_transposed = net.sem(f"{tag}_agg_transposed", c)
        aggT_ready = net.sem(f"{tag}_aggT_ready", c)
        w_transposed = net.sem(f"{tag}_w_transposed", c)
        wT_ready = net.sem(f"{tag}_wT_ready", c)
        w_done = net.sem(f"{tag}_w_done", c)
        w_ready = net.sem(f"{tag}_w_ready", c)
        lin_done = net.sem(f"{tag}_lin_done", c)
        a_ready = net.sem(f"{tag}_a_ready", c)
        rstd_ready = net.sem(f"{tag}_rstd_ready", c)
        relu_ready = net.sem(f"{tag}_relu_ready", c)
        dve_step = net.sem(f"{tag}_dve_step", c)
        var_ready = net.sem(f"{tag}_var_ready", c)
        sd_ready = net.sem(f"{tag}_sd_ready", c)
        x_new = net.sem(f"{tag}_x_new", c)
        new_transposed = net.sem(f"{tag}_new_transposed", c)
        nT_ready = net.sem(f"{tag}_nT_ready", c)
        next_done = net.sem(f"{tag}_next_done", c)
        row_ready = net.sem(f"{tag}_row_ready", c)
        stored = [net.sem(f"{tag}_stored{s}", c) for s in range(2)]
        block = c.enter_context(nc.Block())

        NJT = NT // 2
        assert NT % 2 == 1

        def tiles(eng, body):
            body(0, 0)
            body(0, 1)
            with eng.Fori(1, NJT - 1) as j:
                body(j, 0)
                body(j, 1)
            body(NJT - 1, 0)
            body(NJT - 1, 1)
            body(NJT, 0)

        def has(j, u, d):
            return not isinstance(j, int) or 0 <= 2 * j + u + d

        def prev(j, u):
            return j + (u - 1) // 2, (u - 1) % 2

        def ahead(part, j, u, by):
            if not isinstance(j, int) or 2 * j + u + by < NT:
                part(j + (u + by) // 2, (u + by) % 2)

        @block.sync
        def _(sp):
            def load(j, u):
                t = 2 * j + u
                if has(j, u, -2):
                    sp.wait_ge(agg_transposed, t - 1)
                sp.dma_start(agg[:, u, :], acc[:, bass.ds(t, 1), 0:C].rearrange("p a f -> p (a f)"))\
                    .then_inc(loaded[u], 16)

            load(0, 0)
            load(0, 1)

            def body(j, u):
                ahead(load, j, u, 2)
                if nxt is None and has(j, u, -1):
                    store(*prev(j, u))

            def store(j, u):
                t = 2 * j + u
                sp.wait_ge(x_new, t + 1)
                rows = TAIL if isinstance(j, int) and t == NT - 1 else P
                sp.dma_start(out[bass.ds(t * P, rows), :], xnew[0:rows, u, :]).then_inc(stored[u], 16)
            tiles(sp, body)
            if nxt is None:
                store(NJT, 0)
            sp.wait_ge(stored[0], 16 * (NJT + 1))
            sp.wait_ge(stored[1], 16 * NJT)

        def v_of(ap):
            return ap.rearrange("p (f k) -> p k f", k=3)

        def k_of(ap):
            return ap.rearrange("p (k f) -> p k f", k=3)

        @block.tensor
        def _(pe):
            mm = pe.matmul

            def transpose(to, frm):
                return pe.transpose(to, frm, net.ident[:, :])

            def prepare(j, u):
                t = 2 * j + u
                pe.wait_ge(x_new, t + 1)
                if has(j, u, -1):
                    pe.wait_ge(nT_ready, t)
                mm(nT_ps[0:S0, 0:P], xnew[:, u, 0:S0], net.ident[:, :], start=True, stop=True)
                xv = v_of(xnew[:, u, S0:D])
                for k in range(3):
                    last = transpose(nT_ps[0:V0, (k + 1) * P:(k + 2) * P], xv[:, k, :])
                last.then_inc(new_transposed, 1)
                pe.wait_ge(nT_ready, t + 1)
                if has(j, u, -1):
                    pe.wait_ge(row_ready, t)
                mm(next_ps[:, 0:V0], nT[:, 0:P], prep["ws"], start=True, stop=True).then_inc(next_done, 1)

            def turn(j, u):
                t = 2 * j + u
                pe.wait_ge(loaded[u], 16 * j + 16)
                if has(j, u, -1):
                    pe.wait_ge(aggT_ready, t)
                ag = agg[:, u, :]
                mm(aggT_ps[0:VD, 0:P], ag[:, 0:VD], net.ident[:, :], start=True, stop=True)
                for k in range(3):
                    last = transpose(vecT_ps[0:VD, k * P:(k + 1) * P], ag[:, VD * (k + 1):VD * (k + 2)])
                last.then_inc(agg_transposed, 1)

            def multiply(j, u):
                t = 2 * j + u
                pe.wait_ge(aggT_ready, t + 1)
                if has(j, u, -2):
                    pe.wait_ge(a_ready if kind == "conv" else relu_ready, t - 1)
                lin = lin_ps[u]
                mm(lin[:, 0:NS], aggT[0:VD, 0:P], scal, start=True, stop=True)
                for k in range(3):
                    last = mm(lin[:, NS + V0 * k:NS + V0 * (k + 1)], vecT[:, k * P:(k + 1) * P], vec,
                              start=True, stop=True)
                last.then_inc(lin_done, 1)

            if kind == "cross":
                pe.transpose(wT_ps[0:S0, 0:VD], lay["scal"], net.ident[0:VD, 0:VD])
                pe.transpose(wT_ps[0:V0, P:P + VD], lay["vec"], net.ident[0:VD, 0:VD]).then_inc(w_transposed, 1)
                pe.wait_ge(wT_ready, 1)
                mm(nT_ps[0:VD, 0:S0], wT[:, 0:VD], lay["hs"], start=True, stop=True)
                mm(nT_ps[0:VD, S0:VD], wT[0:V0, P:P + VD], lay["hv"], start=True, stop=True).then_inc(w_done, 1)
                pe.wait_ge(w_ready, 1)
            turn(0, 0)
            multiply(0, 0)
            turn(0, 1)

            def body(j, u):
                ahead(multiply, j, u, 1)
                ahead(turn, j, u, 2)
                if nxt is not None and has(j, u, -1):
                    prepare(*prev(j, u))
            tiles(pe, body)
            if nxt is not None:
                prepare(NJT, 0)

        @block.scalar
        def _(act):
            def copy(to, frm, **kw):
                return act.activation(to, frm, ACT.Copy, **kw)

            def prepare(j, u):
                t = 2 * j + u
                act.wait_ge(new_transposed, t + 1)
                if has(j, u, -1):
                    act.wait_ge(next_done, t)
                copy(nT[:, 0:P], nT_ps[0:S0, 0:P])
                copy(nT[0:V0, P:4 * P], nT_ps[0:V0, P:4 * P]).then_inc(nT_ready, 1)
                if has(j, u, -2):
                    act.wait_ge(stored[u], 16 * j)
                act.wait_ge(next_done, t + 1)
                copy(trow[:, u, 0:D], xnew[:, u, :])
                copy(trow[:, u, D:TW], next_ps[:, 0:V0]).then_inc(row_ready, 1)
                act.wait_ge(row_ready, t + 1)
                act.dma_start(table[bass.ds(t * P, P), :], trow[:, u, :]).then_inc(stored[u], 16)

            def turned(j, u):
                t = 2 * j + u
                act.wait_ge(agg_transposed, t + 1)
                if has(j, u, -1):
                    act.wait_ge(lin_done, t)
                copy(aggT[0:VD, 0:P], aggT_ps[0:VD, 0:P])
                copy(vecT[:, :], vecT_ps[0:VD, 0:3 * P]).then_inc(aggT_ready, 1)

            def relu(j, u):
                t = 2 * j + u
                act.wait_ge(lin_done, t + 1)
                if has(j, u, -2):
                    act.wait_ge(var_ready, t - 1)
                lin, to = lin_ps[u], a_nat[:, u, :]
                act.activation(to[:, 0:S0], lin[:, 0:S0], ACT.Relu)
                act.activation(v_of(to[:, S0:D]), k_of(lin[:, S0:D]), ACT.Relu).then_inc(relu_ready, 1)

            if kind == "cross":
                act.wait_ge(w_transposed, 1)
                copy(wT[:, 0:VD], wT_ps[0:S0, 0:VD])
                copy(wT[0:V0, P:P + VD], wT_ps[0:V0, P:P + VD]).then_inc(wT_ready, 1)
                act.wait_ge(w_done, 1)
                copy(w_both[:, :], nT_ps[0:VD, 0:VD]).then_inc(w_ready, 1)
            turned(0, 0)
            if kind == "cross":
                relu(0, 0)
            turned(0, 1)

            def body(j, u):
                t = 2 * j + u
                if kind == "cross":
                    ahead(relu, j, u, 1)
                ahead(turned, j, u, 2)
                act.wait_ge(var_ready, t + 1)
                act.activation(sd[:, :], mv[:, 1:2], ACT.Sqrt, bias=net.eps[:, 0:1]).then_inc(sd_ready, 1)
                if nxt is not None and has(j, u, -1):
                    prepare(*prev(j, u))
            tiles(act, body)
            if nxt is not None:
                prepare(NJT, 0)

        @block.vector
        def _(dve):
            stats_count = Count(dve, f"{tag}_stats_count", 0)
            CHAIN = 2
            START = 3 if kind == "conv" else 0

            def body(j, u):
                t = 2 * j + u
                n_own = [0]

                def step(ins):
                    n_own[0] += 1
                    ins.then_inc(dve_step, 1)
                    dve.wait_ge(dve_step, CHAIN * t + START + n_own[0])

                ys, lin = y[:, u, :], lin_ps[u]
                if kind == "conv":
                    b = net.base[:, bass.ds(t, 1), :].rearrange("p a f -> p (a f)")
                    by = by_count[:, bass.ds(t, 1)]
                    dve.wait_ge(lin_done, t + 1)
                    step(dve.tensor_scalar(alpha[:, :], lin[:, S0:S0 + 1], by, by, ALU.mult, ALU.mult))
                    dve.scalar_tensor_tensor(ys[:, 0:S0], lin[:, 0:S0], alpha[:, :], b[:, 0:S0], ALU.mult, ALU.add)
                    step(dve.scalar_tensor_tensor(v_of(ys[:, S0:D]), k_of(lin[:, S0 + 1:D + 1]), alpha[:, :],
                                                  v_of(b[:, S0:D]), ALU.mult, ALU.add))
                else:
                    x = net.xres[:, bass.ds(t, 1), :].rearrange("p a f -> p (a f)")
                    dve.wait_ge(relu_ready, t + 1)
                    step(dve.scalar_tensor_tensor(ys, x, 2.0, a_nat[:, u, :], ALU.mult, ALU.add))
                dve.bn_stats(stats[:, :], ys).then_inc(a_ready if kind == "conv" else dve_step, 1)
                stats_count.up(1 if kind == "conv" else CHAIN)
                dve.wait_ge(loaded[0], 16)
                dve.wait_ge(a_ready if kind == "conv" else dve_step, stats_count.reg)
                dve.bn_aggr(mv[:, :], stats[:, :]).then_inc(var_ready, 1)
                dve.wait_ge(sd_ready, t + 1)
                dve.reciprocal(rstd[:, :], sd[:, :]).then_inc(rstd_ready, 1)
                dve.wait_ge(rstd_ready, t + 1)
                if has(j, u, -2):
                    if nxt is not None:
                        dve.wait_ge(row_ready, t - 1)
                    else:
                        dve.wait_ge(stored[u], 16 * j)
                if nxt is not None:
                    dve.tensor_scalar(net.xres[:, bass.ds(t, 1), :].rearrange("p a f -> p (a f)"), ys,
                                      mv[:, 0:1], rstd[:, 0:1], ALU.subtract, ALU.mult)
                dve.tensor_scalar(xnew[:, u, :], ys, mv[:, 0:1], rstd[:, 0:1], ALU.subtract, ALU.mult)\
                    .then_inc(x_new, 1)
            if kind == "conv":
                counts = acc[:, 0:NT, 4 * VD:C].rearrange("p t o -> p (t o)")
                dve.tensor_scalar(by_count[:, :], counts, 1.0, None, ALU.max).then_inc(dve_step, 1)
                dve.wait_ge(dve_step, 1)
                dve.reciprocal(by_count[:, :], by_count[:, :]).then_inc(dve_step, 1)
                dve.wait_ge(dve_step, 2)
                dve.scalar_tensor_tensor(by_count[:, :], by_count[:, :], 1.0 / math.sqrt(VD), net.nodea[:, 0:NT],
                                         ALU.mult, ALU.mult).then_inc(dve_step, 1)
                dve.wait_ge(dve_step, 3)
            tiles(dve, body)


def gnn_kernel(nc, ins, out):
    with ExitStack() as ctx:
        net = Net(nc, ctx)
        ctx.enter_context(nc.allow_non_contiguous_dma(reason="small tables, one value a node"))
        g = lambda n: ins[n]
        rec_src = net.dram("rec_src", [E + GE, 6])
        rec_dst = net.dram("rec_dst", [E + GE, 22])
        net.pads = [(rec_src, 6), (rec_dst, 22)]
        table = net.dram("table", [NTP * P, TW])
        net.xres = net.sb("xres", [P, NTP, D])
        net.base = net.sb("base", [P, NTP, D])
        net.nodea = net.sb("nodea", [P, NTP])
        net.wfc1 = net.sb("wfc1", [JB * 22, JB // 2, 2 * S0])
        net.wfc2 = net.sb("wfc2", [2 * S0, TW])

        def full_layer(n, ss, vv, sv, vs, l0, l1, m0d, m1d, m0, m1, mdot, f, msv, fsv):
            t = {k: net.sb(f"w{n}_{k}", shape) for k, shape in (
                ("ss", [P, 8, 4, S0]), ("vv", [P, 4, 2, S0]), ("sv", [P, 8, 2, V0]), ("vs", [P, 4, 4, V0]),
                ("l0", [P, S0]), ("l1", [P, 3, V0]), ("m0", [2 * S0, S0]), ("m1", [VD, V0]), ("mdot", [V0, S0]),
                ("msv", [S0, V0]))}
            lay = {"chunks": {"ss": (t["ss"], ss), "vv": (t["vv"], vv), "sv": (t["sv"], sv), "vs": (t["vs"], vs)},
                   "plain": [(t["l0"][0:S0, :], l0), (t["l1"][S0:S0 + V0, 0, :], l1),
                             (t["l1"][S0 + V0:P, 1, :], l1), (t["l1"][0:V0, 2, :], l1),
                             (t["m0"][0:S0, :], m0), (t["m0"][S0:2 * S0, :], m0d),
                             (t["m1"][0:V0, :], m1), (t["m1"][V0:2 * V0, :], m1d), (t["mdot"][:, :], mdot),
                             (t["msv"][:, :], msv)],
                   "scales": [(t["ss"][:, :, :, :], f["ss"]), (t["vv"][:, :, :, :], f["vv"]),
                              (t["sv"][:, :, :, :], f["uv"]), (t["vs"][:, :, :, :], f["uv"]),
                              (t["l0"][:, :], f["l0"]), (t["l1"][:, :, :], f["l1"]), (t["m0"][0:S0, :], f["m0"]),
                              (t["m0"][S0:2 * S0, :], f["m0d"]), (t["m1"][0:V0, :], f["m1"]),
                              (t["m1"][V0:2 * V0, :], f["m1d"]), (t["mdot"][:, :], f["mdot"]), (t["msv"][:, :], fsv)]}
            for k in ("l0", "m0", "m1", "mdot"):
                lay[k] = t[k][:, :]
            lay["l1"] = t["l1"]
            lay["prep"] = {"ws": t["msv"][:, :]}
            return lay

        i64, i32, i96 = 1.0 / 8, 1.0 / math.sqrt(V0), 1.0 / math.sqrt(VD)
        fan0, fan1 = S0 * S0 + V0 * V0, 2 * S0 * V0
        lay0 = full_layer(0, g("L0_gnn_wu000"), g("L0_gnn_wu110"), g("L0_gnn_wu011"), g("L0_gnn_wu101"),
                          g("L0_gnn_lu0"), g("L0_gnn_lu1"),
                          g("L0_gnn_wm000").rearrange("u o w -> u (o w)"), g("L0_gnn_wm101").rearrange("u o w -> u (o w)"),
                          g("L0_gnn_lm0"), g("L0_gnn_lm1"), g("L0_gnn_wm110").rearrange("u o w -> u (o w)"),
                          dict(ss=1 / math.sqrt(fan0), vv=K3 / math.sqrt(fan0), uv=1 / math.sqrt(fan1), l0=i64, l1=i32,
                               m0=i64, m0d=i96, m1=i32, m1d=i96, mdot=K3 * i96),
                          g("L0_gnn_wm011").rearrange("u o w -> u (o w)"), i96)
        lay2 = full_layer(2, g("L2_gnn_Wu_ss"), g("L2_gnn_Wu_vv"), g("L2_gnn_Wu_sv"), g("L2_gnn_Wu_vs"),
                          g("L2_gnn_Lu_s"), g("L2_gnn_Lu_v"), g("L2_gnn_Wm_ss"), g("L2_gnn_Wm_vs"),
                          g("L2_gnn_Lm_s"), g("L2_gnn_Lm_v"), g("L2_gnn_Wm_vv"),
                          dict(ss=0.015625, vv=K3 * 0.03125, uv=1 / math.sqrt(2048), l0=i64, l1=i32,
                               m0=i64, m0d=i64, m1=i32, m1d=i32, mdot=K3 * i32),
                          g("L2_gnn_Wm_sv"), i64)
        w1 = {k: net.sb(f"w1_{k}", s) for k, s in (("ws", [S0, 2 * S0]), ("wv", [V0, 2 * V0]),
                                                  ("scal", [VD, S0 + 1]), ("vec", [VD, V0]))}
        lay1 = {"chunks": {}, "plain": [
                    (w1["ws"][:, 0:S0], g("L1_gnn_Wl1_0")), (w1["ws"][:, S0:2 * S0], g("L1_gnn_Wsc0")),
                    (w1["wv"][:, 0:V0], g("L1_gnn_Wl1_1")), (w1["wv"][:, V0:2 * V0], g("L1_gnn_Wsc1")),
                    (w1["scal"][:, 0:S0], g("L1_gnn_Wl2_s")), (w1["scal"][:, S0:S0 + 1], g("L1_gnn_Wa")),
                    (w1["vec"][:, :], g("L1_gnn_Wl2_v")),
                    *[(net.wfc1[22 * q + 6:22 * (q + 1), q % 2, q // 2 * S0:(q // 2 + 1) * S0], g("L1_gnn_Wfc1"))
                      for q in range(JB)],
                    (net.wfc2[0:S0, :], g("L1_gnn_Wfc2")), (net.wfc2[S0:2 * S0, :], g("L1_gnn_Wfc2")),
                    (net.xres[:, 0:NT - 1, :], g("x")[0:(NT - 1) * P, :].rearrange("(t p) f -> p t f", p=P)),
                    (net.xres[0:TAIL, NT - 1, :], g("x")[(NT - 1) * P:N, :]),
                    (net.nodea[:, 0:NT - 1].rearrange("p (t o) -> p t o", o=1),
                     g("node_vec1")[0:(NT - 1) * P, :].rearrange("(t p) o -> p t o", p=P)),
                    (net.nodea[0:TAIL, NT - 1:NT], g("node_vec1")[(NT - 1) * P:N, :])],
                "scales": [(w1["ws"][:, :], i64), (w1["wv"][:, :], i32), (net.wfc1[:, :, :], 0.25),
                           (net.wfc2[:, 0:TW - V0], i64), (net.wfc2[:, TW - V0:TW], i64 * K3)],
                "scal": w1["scal"][:, :], "vec": w1["vec"][:, :],
                "prep": {"ws": w1["ws"][:, :], "wv": w1["wv"][:, :]}}
        w3 = {k: net.sb(f"w3_{k}", s) for k, s in (("w3", [S0, V0]), ("scal", [VD, S0]), ("vec", [VD, V0]),
                                                  ("hs", [S0, S0]), ("hv", [V0, V0]))}
        C0, C1 = 1 / math.sqrt(S0 + V0), math.sqrt(3.0 / (S0 + 2 * V0))
        lay3 = {"chunks": {}, "plain": [
                    (w3["w3"][:, :], g("L3_gnn_W3")), (w3["scal"][0:S0, :], g("L3_gnn_W1")),
                    (w3["scal"][S0:VD, :], g("L3_gnn_W2")), (w3["vec"][0:V0, :], g("L3_gnn_W4")),
                    (w3["vec"][2 * V0:VD, :], g("L3_gnn_W5")), (w3["hs"][:, :], g("L3_gnn_Ws")),
                    (w3["hv"][:, :], g("L3_gnn_Wv"))],
                "scales": [(w3["w3"][:, :], C1 * K3), (w3["scal"][0:S0, :], C0), (w3["scal"][S0:VD, :], C0 * K3),
                           (w3["vec"][0:V0, :], C1 * K3), (w3["vec"][2 * V0:VD, :], C1 / math.sqrt(6.0)),
                           (w3["hs"][:, :], i64), (w3["hv"][:, :], i32)],
                "scal": w3["scal"][:, :], "vec": w3["vec"][:, :], "hs": w3["hs"][:, :], "hv": w3["hv"][:, :],
                "prep": {"ws": w3["w3"][:, :]}}

        with ExitStack() as c:
            block = c.enter_context(nc.Block())

            @block.vector
            def _(dve):
                dve.memset(net.xres[:, NT - 1:NTP, :], 0.0)
                dve.memset(net.nodea[:, NT - 1:NTP], 0.0)
                dve.memset(net.wfc1[:, :, :], 0.0)
                for lay in (lay0, lay2):
                    dve.memset(lay["l0"], 0.0)
                    dve.memset(lay["l1"][:, :, :], 0.0)

        constants(net)

        def schedule(tag):
            return (net.sb(f"{tag}_erow", [1, NIP], I32), net.sb(f"{tag}_trow", [1, NIP], I32),
                    net.sb(f"{tag}_tbase", [P, NIP], F32))

        by_src, by_dst = schedule("src"), schedule("dst")
        fills = [(w3["vec"][V0:2 * V0, :], net.ident[V0:2 * V0, V0:2 * V0])]
        fills += [(lay["m1"][2 * V0:VD, :], net.ident[2 * V0:VD, 2 * V0:VD]) for lay in (lay0, lay2)]
        prepare_edges(net, ins, rec_src, rec_dst, by_src, by_dst, [lay0, lay1, lay2, lay3], fills,
                      lay0["prep"]["ws"], table)
        CM = 2 * D + V0 + VD
        acc = net.sb("acc", [P, NT + 1, CM])

        edge_loop(net, "e0", "plain", rec_src, by_src, table, acc, CM)
        outer_stage(net, "n0", "conv", lay0, lay1["prep"], acc, CM, table)
        edge_loop(net, "e1", "conv", rec_dst, by_dst, table, acc, 4 * VD + 1)
        node_stage(net, "n1", "conv", "plain", lay1, lay2["prep"], acc, 4 * VD + 1, table, out)
        edge_loop(net, "e2", "plain", rec_src, by_src, table, acc, CM)
        outer_stage(net, "n2", "cross", lay2, lay3["prep"], acc, CM, table)
        edge_loop(net, "e3", "cross", rec_dst, by_dst, table, acc, 4 * VD)
        node_stage(net, "n3", "cross", None, lay3, None, acc, 4 * VD, table, out)


def kernel(**inputs):
    import numpy as _np
    import concourse.bacc as _bacc
    from concourse import mybir as _mybir
    from concourse.bass_utils import run_bass_kernel_spmd as _run

    nc = _bacc.Bacc("TRN2", target_bir_lowering=False, num_devices=1)
    arrays, args = {}, {}
    for name in inputs:
        a = _np.ascontiguousarray(inputs[name])
        arrays[f"in_{name}"] = a
        args[name] = nc.dram_tensor(f"in_{name}", a.shape, _mybir.dt.from_np(a.dtype), kind="ExternalInput").ap()
    out = nc.dram_tensor("out_x", (N, D), F32, kind="ExternalOutput").ap()
    gnn_kernel(nc, args, out)
    r = _run(nc, [arrays], core_ids=[0])
    return r.results[0]["out_x"]
```
